# Optimizing a Trainium2 kernel written in Bass

```python
import numpy as np
import jax
import jax.numpy as jnp

def _softmax(x, axis=-1):
    return jax.nn.softmax(x, axis=axis)

def _gelu(x):
    return jax.nn.gelu(x, approximate=True)

def _silu(x):
    return jax.nn.silu(x)

def _sigmoid(x):
    return jax.nn.sigmoid(x)

def _layernorm(x, axis=-1, eps=1e-05):
    m = jnp.mean(x, axis=axis, keepdims=True)
    v = jnp.var(x, axis=axis, keepdims=True)
    return (x - m) / jnp.sqrt(v + eps)

def _scatter_add(tgt, idx, src, axis=0):
    return tgt.at[idx].add(src)

def _segment_sum(src, seg, n):
    return jax.ops.segment_sum(src, seg, n)
kernel_name = 'mk_prb_d4_jaxref_r8_526b2f'

def setup_inputs(seed: int=0):
    np.random.seed(seed)
    _w = jnp.asarray

    def _L0_attn_setup():
        import jax, jax.numpy as jnp
        import numpy as np
        B, SQ, HIDDEN = (2, 256, 256)
        HEADS, GROUPS, KVC = (16, 4, 128)
        HPG = HEADS // GROUPS
        LAYER_INDEX = 1
        SCALE = KVC ** (-0.5)
        key = jax.random.key(seed)
        k1, k2, k3, k4 = jax.random.split(key, 4)
        return {'x': jax.random.normal(k1, (B, SQ, HIDDEN), jnp.float32), 'w_q': jax.random.normal(k2, (HIDDEN, HEADS * KVC), jnp.float32) * 0.02, 'w_kv': jax.random.normal(k3, (HIDDEN, 2 * GROUPS * KVC), jnp.float32) * 0.02, 'w_dense': jax.random.normal(k4, (HEADS * KVC, HIDDEN), jnp.float32) * 0.02}
    _L0_attn_in = _L0_attn_setup()

    def _L0_ffn_setup():
        import jax, jax.numpy as jnp
        import numpy as np
        HIDDEN = 256
        INTER = 1024
        SCALE = 64.0

        def fwht(x):
            orig_shape = x.shape
            n = orig_shape[-1]
            x = x.reshape(-1, n)
            h = 1
            while h < n:
                x = x.reshape(-1, n // (2 * h), 2, h)
                a, b = (x[:, :, 0, :], x[:, :, 1, :])
                x = jnp.stack([a + b, a - b], axis=2).reshape(-1, n)
                h *= 2
            return (x / jnp.sqrt(jnp.asarray(n, x.dtype))).reshape(orig_shape)
        key = jax.random.key(seed)
        ks = jax.random.split(key, 8)
        inp = jax.random.normal(ks[0], (4, 256, HIDDEN), dtype=jnp.float32)
        SU_ug = jnp.where(jax.random.bernoulli(ks[1], 0.5, (HIDDEN,)), 1.0, -1.0).astype(jnp.float32)
        SU_dp = jnp.where(jax.random.bernoulli(ks[2], 0.5, (INTER,)), 1.0, -1.0).astype(jnp.float32)
        Wscale_ug = jax.random.uniform(ks[3], (2 * INTER,), jnp.float32, 0.5, 1.5)
        Wscale_dp = jax.random.uniform(ks[4], (HIDDEN,), jnp.float32, 0.5, 1.5)
        W_up = jax.random.normal(ks[5], (INTER, HIDDEN), dtype=jnp.float32) * 0.02
        W_gate = jax.random.normal(ks[6], (INTER, HIDDEN), dtype=jnp.float32) * 0.02
        W_down = jax.random.normal(ks[7], (HIDDEN, INTER), dtype=jnp.float32) * 0.02
        return {'input': inp, 'SU_ug': SU_ug, 'SU_dp': SU_dp, 'Wscale_ug': Wscale_ug, 'Wscale_dp': Wscale_dp, 'W_up': W_up, 'W_gate': W_gate, 'W_down': W_down}
    _L0_ffn_in = _L0_ffn_setup()

    def _L1_attn_setup():
        import jax, jax.numpy as jnp
        import numpy as np
        D_MODEL = 256
        K_DIM = 128
        V_DIM = 128
        H = 16
        B = 1
        S = 256
        SCALE_BASE = 512.0
        THETA = 10000.0
        EPS = 1e-05

        def _rotate_half(x):
            xr = x.reshape(*x.shape[:-1], -1, 2)
            x1, x2 = (xr[..., 0], xr[..., 1])
            return jnp.stack((-x2, x1), axis=-1).reshape(x.shape)

        def _rope_xpos(q, k, seq_len, dim):
            pos = jnp.arange(seq_len, dtype=jnp.float32)
            inv_freq = 1.0 / THETA ** (jnp.arange(0, dim, 2, dtype=jnp.float32) / dim)
            freqs = jnp.repeat(pos[:, None] * inv_freq[None, :], 2, axis=-1)
            cos, sin = (jnp.cos(freqs), jnp.sin(freqs))
            sbase = (jnp.arange(0, dim, 2, dtype=jnp.float32) + 0.4 * dim) / (1.4 * dim)
            power = (pos - seq_len // 2) / SCALE_BASE
            scale = jnp.repeat(sbase[None, :] ** power[:, None], 2, axis=-1)
            q = (q * cos + _rotate_half(q) * sin) * scale
            k = (k * cos + _rotate_half(k) * sin) / scale
            return (q, k)
        key = jax.random.key(seed)
        ks = jax.random.split(key, 11)
        lin = lambda k, i, o: jax.random.normal(k, (i, o), jnp.float32) * 0.02
        return {'x': jax.random.normal(ks[0], (B, S, D_MODEL), jnp.float32), 'Wq': lin(ks[1], D_MODEL, K_DIM * H), 'bq': jnp.zeros((K_DIM * H,), jnp.float32), 'Wk': lin(ks[2], D_MODEL, K_DIM * H), 'bk': jnp.zeros((K_DIM * H,), jnp.float32), 'Wv': lin(ks[3], D_MODEL, V_DIM * H), 'bv': jnp.zeros((V_DIM * H,), jnp.float32), 'Wg': lin(ks[4], D_MODEL, V_DIM * H), 'bg': jnp.zeros((V_DIM * H,), jnp.float32), 'Wo': lin(ks[5], V_DIM * H, D_MODEL), 'bo': jnp.zeros((D_MODEL,), jnp.float32)}
    _L1_attn_in = _L1_attn_setup()

    def _L1_ffn_setup():
        import jax, jax.numpy as jnp
        import numpy as np
        D_IN = 256
        D_OUT = 256
        EPS = 1e-05
        key = jax.random.key(seed)
        k_x, k_w = jax.random.split(key)
        x = jax.random.normal(k_x, (8, 256, D_IN), dtype=jnp.float32)
        weight = jax.random.normal(k_w, (D_OUT, D_IN), dtype=jnp.float32)
        gamma = jnp.ones((D_OUT,), dtype=jnp.float32)
        beta = jnp.zeros((D_OUT,), dtype=jnp.float32)
        ln_weight = jnp.ones((D_IN,), dtype=jnp.float32)
        ln_bias = jnp.zeros((D_IN,), dtype=jnp.float32)
        return {'x': x, 'weight': weight, 'gamma': gamma, 'beta': beta, 'ln_weight': ln_weight, 'ln_bias': ln_bias}
    _L1_ffn_in = _L1_ffn_setup()

    def _L2_attn_setup():
        import jax, jax.numpy as jnp
        import numpy as np
        HIDDEN = 256
        N_HEADS = 16
        HEAD_DIM = HIDDEN // N_HEADS

        def rotate_half(x):
            x1, x2 = jnp.split(x, 2, axis=-1)
            return jnp.concatenate([-x2, x1], axis=-1)
        key = jax.random.key(seed)
        k0, k1, k2, k3, k4 = jax.random.split(key, 5)
        B, S = (1, 256)
        scale = 1.0 / np.sqrt(HIDDEN)
        return {'hidden_states': jax.random.normal(k0, (B, S, HIDDEN), dtype=jnp.float32), 'Wq': jax.random.normal(k1, (HIDDEN, HIDDEN), dtype=jnp.float32) * scale, 'Wk': jax.random.normal(k2, (HIDDEN, HIDDEN), dtype=jnp.float32) * scale, 'Wv': jax.random.normal(k3, (HIDDEN, HIDDEN), dtype=jnp.float32) * scale, 'Wo': jax.random.normal(k4, (HIDDEN, HIDDEN), dtype=jnp.float32) * scale, 'gate': jnp.zeros((1, N_HEADS, 1, 1), dtype=jnp.float32)}
    _L2_attn_in = _L2_attn_setup()

    def _L2_ffn_setup():
        import jax, jax.numpy as jnp
        import numpy as np

        def binarize_weight(w):
            alpha = jnp.mean(jnp.abs(w), axis=tuple(range(1, w.ndim)), keepdims=True)
            bw = jnp.where(w >= 0, 1.0, -1.0) * alpha
            return jax.lax.stop_gradient(bw - w) + w
        key = jax.random.key(seed)
        k1, k2, k3 = jax.random.split(key, 3)
        in_features, out_features = (256, 256)
        x = jax.random.normal(k1, (8, 256, in_features), dtype=jnp.float32)
        std = np.sqrt(2.0 / out_features).astype(np.float32)
        weight = jax.random.normal(k2, (out_features, in_features), dtype=jnp.float32) * std
        bias = jax.random.normal(k3, (out_features,), dtype=jnp.float32) * 0.01
        return {'x': x, 'weight': weight, 'bias': bias}
    _L2_ffn_in = _L2_ffn_setup()

    def _L3_attn_setup():
        import jax, jax.numpy as jnp
        import numpy as np
        B, L, DM = (2, 256, 256)
        H, P, N = (32, 64, 64)
        D_INNER = H * P
        PROJ = 2 * D_INNER + 2 * H * N + H
        EPS = 1e-05
        key = jax.random.key(seed)
        k0, k1, k2 = jax.random.split(key, 3)
        return {'x': jax.random.normal(k0, (B, L, DM), jnp.float32), 'W_in': jax.random.normal(k1, (PROJ, DM), jnp.float32) * DM ** (-0.5), 'W_out': jax.random.normal(k2, (DM, D_INNER), jnp.float32) * D_INNER ** (-0.5), 'gamma': jnp.ones((D_INNER,), jnp.float32), 'beta': jnp.zeros((D_INNER,), jnp.float32), 'D': jnp.ones((H, P), jnp.float32)}
    _L3_attn_in = _L3_attn_setup()

    def _L3_ffn_setup():
        import jax, jax.numpy as jnp
        import numpy as np
        B, S, H = (2, 128, 256)
        I = 128
        E = 32
        Z = 32
        K = 8
        SCALE = 1.5
        CAP = 128
        EPS = 1e-20

        def _moe_forward(x, w_cls, bias, w_gate_up, w_down):
            T = x.shape[0] * x.shape[1]
            xf = x.reshape(T, H)
            logits = xf.astype(jnp.float32) @ w_cls.T
            scores = jax.nn.softmax(logits, axis=-1)
            _, topk_idx = jax.lax.top_k(scores + bias[None, :], K)
            w = jnp.take_along_axis(scores, topk_idx, axis=-1)
            w = w / (w.sum(-1, keepdims=True) + EPS) * SCALE
            routed = topk_idx < E
            w_r = jnp.where(routed, w, 0.0)
            w_z = jnp.where(routed, 0.0, w)
            N = T * K
            flat_ids = jnp.where(routed, topk_idx, E).reshape(-1)
            x_exp = jnp.repeat(xf, K, axis=0)
            order = jnp.argsort(flat_ids)
            ids_s = flat_ids[order]
            counts = jax.ops.segment_sum(jnp.ones(N, jnp.int32), flat_ids, num_segments=E + 1)
            starts = jnp.cumsum(counts) - counts
            pos = jnp.arange(N) - starts[ids_s]
            buf = jnp.zeros((E, CAP, H), xf.dtype).at[ids_s, pos].set(x_exp[order], mode='drop')
            gu = jnp.einsum('ech,ehf->ecf', buf, w_gate_up)
            g, u = jnp.split(gu, 2, axis=-1)
            act = jax.nn.silu(g) * u
            y = jnp.einsum('eci,eih->ech', act, w_down)
            valid = (ids_s < E) & (pos < CAP)
            y_tok = jnp.where(valid[:, None], y[jnp.clip(ids_s, 0, E - 1), jnp.clip(pos, 0, CAP - 1)], 0.0)
            y_exp = jnp.zeros((N, H), xf.dtype).at[order].set(y_tok).reshape(T, K, H)
            routed_out = jnp.einsum('tk,tkh->th', w_r, y_exp)
            out = routed_out * (1.0 + w_z.sum(-1, keepdims=True))
            return out.reshape(x.shape)
        key = jax.random.key(seed)
        ks = jax.random.split(key, 5)
        x = jax.random.normal(ks[0], (B, S, H), jnp.float32)
        w_cls = jax.random.normal(ks[1], (E + Z, H), jnp.float32) / np.float32(np.sqrt(H))
        bias = jax.random.normal(ks[2], (E + Z,), jnp.float32) * 0.02
        w_gate_up = jax.random.normal(ks[3], (E, H, 2 * I), jnp.float32) * 0.02
        w_down = jax.random.normal(ks[4], (E, I, H), jnp.float32) * 0.02
        return {'x': x, 'w_cls': w_cls, 'bias': bias, 'w_gate_up': w_gate_up, 'w_down': w_down}
    _L3_ffn_in = _L3_ffn_setup()
    _d = {'L0_attn_x': _L0_attn_in['x'], 'L0_attn_w_q': _L0_attn_in['w_q'], 'L0_attn_w_kv': _L0_attn_in['w_kv'], 'L0_attn_w_dense': _L0_attn_in['w_dense'], 'L0_ffn_SU_ug': _L0_ffn_in['SU_ug'], 'L0_ffn_SU_dp': _L0_ffn_in['SU_dp'], 'L0_ffn_Wscale_ug': _L0_ffn_in['Wscale_ug'], 'L0_ffn_Wscale_dp': _L0_ffn_in['Wscale_dp'], 'L0_ffn_W_up': _L0_ffn_in['W_up'], 'L0_ffn_W_gate': _L0_ffn_in['W_gate'], 'L0_ffn_W_down': _L0_ffn_in['W_down'], 'L1_attn_Wq': _L1_attn_in['Wq'], 'L1_attn_bq': _L1_attn_in['bq'], 'L1_attn_Wk': _L1_attn_in['Wk'], 'L1_attn_bk': _L1_attn_in['bk'], 'L1_attn_Wv': _L1_attn_in['Wv'], 'L1_attn_bv': _L1_attn_in['bv'], 'L1_attn_Wg': _L1_attn_in['Wg'], 'L1_attn_bg': _L1_attn_in['bg'], 'L1_attn_Wo': _L1_attn_in['Wo'], 'L1_attn_bo': _L1_attn_in['bo'], 'L1_ffn_weight': _L1_ffn_in['weight'], 'L1_ffn_gamma': _L1_ffn_in['gamma'], 'L1_ffn_beta': _L1_ffn_in['beta'], 'L1_ffn_ln_weight': _L1_ffn_in['ln_weight'], 'L1_ffn_ln_bias': _L1_ffn_in['ln_bias'], 'L2_attn_Wq': _L2_attn_in['Wq'], 'L2_attn_Wk': _L2_attn_in['Wk'], 'L2_attn_Wv': _L2_attn_in['Wv'], 'L2_attn_Wo': _L2_attn_in['Wo'], 'L2_attn_gate': _L2_attn_in['gate'], 'L2_ffn_weight': _L2_ffn_in['weight'], 'L2_ffn_bias': _L2_ffn_in['bias'], 'L3_attn_W_in': _L3_attn_in['W_in'], 'L3_attn_W_out': _L3_attn_in['W_out'], 'L3_attn_gamma': _L3_attn_in['gamma'], 'L3_attn_beta': _L3_attn_in['beta'], 'L3_attn_D': _L3_attn_in['D'], 'L3_ffn_w_cls': _L3_ffn_in['w_cls'], 'L3_ffn_bias': _L3_ffn_in['bias'], 'L3_ffn_w_gate_up': _L3_ffn_in['w_gate_up'], 'L3_ffn_w_down': _L3_ffn_in['w_down']}
    _x0 = _d['L0_attn_x']
    _d['L0_attn_x'] = jax.random.normal(jax.random.fold_in(jax.random.key(seed), 1), (2, 1024, 256), dtype=_x0.dtype)
    del _x0
    return _d

def reference(L0_attn_x, L0_attn_w_q, L0_attn_w_kv, L0_attn_w_dense, L0_ffn_SU_ug, L0_ffn_SU_dp, L0_ffn_Wscale_ug, L0_ffn_Wscale_dp, L0_ffn_W_up, L0_ffn_W_gate, L0_ffn_W_down, L1_attn_Wq, L1_attn_bq, L1_attn_Wk, L1_attn_bk, L1_attn_Wv, L1_attn_bv, L1_attn_Wg, L1_attn_bg, L1_attn_Wo, L1_attn_bo, L1_ffn_weight, L1_ffn_gamma, L1_ffn_beta, L1_ffn_ln_weight, L1_ffn_ln_bias, L2_attn_Wq, L2_attn_Wk, L2_attn_Wv, L2_attn_Wo, L2_attn_gate, L2_ffn_weight, L2_ffn_bias, L3_attn_W_in, L3_attn_W_out, L3_attn_gamma, L3_attn_beta, L3_attn_D, L3_ffn_w_cls, L3_ffn_bias, L3_ffn_w_gate_up, L3_ffn_w_down):

    def _L0_attn_ref(x, w_q, w_kv, w_dense):
        import jax, jax.numpy as jnp
        import numpy as np
        B, SQ, HIDDEN = (2, 256, 256)
        HEADS, GROUPS, KVC = (16, 4, 128)
        HPG = HEADS // GROUPS
        LAYER_INDEX = 1
        SCALE = KVC ** (-0.5)
        b, sq, _ = x.shape
        sk = sq
        q = jnp.einsum('bsh,he->bse', x, w_q).reshape(b, sq, GROUPS, HPG, KVC)
        kv = jnp.einsum('bsh,he->bse', x, w_kv)
        k, v = jnp.split(kv, 2, axis=-1)
        k = k.reshape(b, sk, GROUPS, KVC)
        v = v.reshape(b, sk, GROUPS, KVC)
        scores = jnp.einsum('bqgpd,bkgd->bgqpk', q, k) * (SCALE / LAYER_INDEX)
        scores = scores.astype(jnp.float32) * LAYER_INDEX
        causal = jnp.arange(sq)[:, None] >= jnp.arange(sk)[None, :]
        scores = jnp.where(causal[None, None, :, None, :], scores, -jnp.inf)
        probs = jax.nn.softmax(scores, axis=-1).astype(x.dtype)
        ctx = jnp.einsum('bgqpk,bkgd->bqgpd', probs, v).reshape(b, sq, HEADS * KVC)
        return jnp.einsum('bse,eh->bsh', ctx, w_dense)

    def _L0_ffn_ref(input, SU_ug, SU_dp, Wscale_ug, Wscale_dp, W_up, W_gate, W_down):
        import jax, jax.numpy as jnp
        import numpy as np
        HIDDEN = 256
        INTER = 1024
        SCALE = 64.0

        def fwht(x):
            orig_shape = x.shape
            n = orig_shape[-1]
            x = x.reshape(-1, n)
            h = 1
            while h < n:
                x = x.reshape(-1, n // (2 * h), 2, h)
                a, b = (x[:, :, 0, :], x[:, :, 1, :])
                x = jnp.stack([a + b, a - b], axis=2).reshape(-1, n)
                h *= 2
            return (x / jnp.sqrt(jnp.asarray(n, x.dtype))).reshape(orig_shape)
        n = SU_ug.shape[0]
        x = input.reshape(-1, n)
        x = fwht(x * SU_ug) / SCALE
        x_up = x @ W_up.T * (Wscale_ug[:INTER] * SCALE)
        x_gate = x @ W_gate.T * (Wscale_ug[INTER:] * SCALE)
        x = jax.nn.silu(x_gate) * x_up
        x = fwht(x * SU_dp) / SCALE
        x = x @ W_down.T * (Wscale_dp * SCALE)
        return x.reshape(input.shape)

    def _L1_attn_ref(x, Wq, bq, Wk, bk, Wv, bv, Wg, bg, Wo, bo):
        import jax, jax.numpy as jnp
        import numpy as np
        D_MODEL = 256
        K_DIM = 128
        V_DIM = 128
        H = 16
        B = 1
        S = 256
        SCALE_BASE = 512.0
        THETA = 10000.0
        EPS = 1e-05

        def _rotate_half(x):
            xr = x.reshape(*x.shape[:-1], -1, 2)
            x1, x2 = (xr[..., 0], xr[..., 1])
            return jnp.stack((-x2, x1), axis=-1).reshape(x.shape)

        def _rope_xpos(q, k, seq_len, dim):
            pos = jnp.arange(seq_len, dtype=jnp.float32)
            inv_freq = 1.0 / THETA ** (jnp.arange(0, dim, 2, dtype=jnp.float32) / dim)
            freqs = jnp.repeat(pos[:, None] * inv_freq[None, :], 2, axis=-1)
            cos, sin = (jnp.cos(freqs), jnp.sin(freqs))
            sbase = (jnp.arange(0, dim, 2, dtype=jnp.float32) + 0.4 * dim) / (1.4 * dim)
            power = (pos - seq_len // 2) / SCALE_BASE
            scale = jnp.repeat(sbase[None, :] ** power[:, None], 2, axis=-1)
            q = (q * cos + _rotate_half(q) * sin) * scale
            k = (k * cos + _rotate_half(k) * sin) / scale
            return (q, k)
        Bb, Ss, Dd = x.shape
        heads = lambda t: t.reshape(Bb, Ss, H, -1).transpose(0, 2, 1, 3)
        q = heads(x @ Wq + bq)
        k = heads(x @ Wk + bk)
        v = heads(x @ Wv + bv)
        q, k = _rope_xpos(q, k, Ss, K_DIM)
        gamma = 1.0 - 2.0 ** (-5.0 - jnp.arange(H, dtype=jnp.float32))
        pos = jnp.arange(Ss, dtype=jnp.float32)
        pm = pos[:, None] - pos[None, :]
        decay_mask = jnp.where(pm >= 0, gamma[:, None, None] ** jnp.maximum(pm, 0.0), 0.0)
        scores = jnp.einsum('bhid,bhjd->bhij', q, k) * decay_mask
        ret = jnp.einsum('bhij,bhjd->bhid', scores, v)
        concat = ret.transpose(0, 2, 1, 3).reshape(Bb * Ss, H, V_DIM)
        mu = concat.mean(-1, keepdims=True)
        var = ((concat - mu) ** 2).mean(-1, keepdims=True)
        gn = ((concat - mu) / jnp.sqrt(var + EPS)).reshape(Bb, Ss, H * V_DIM)
        out = jax.nn.silu(x @ Wg + bg) * gn @ Wo + bo
        return out

    def _L1_ffn_ref(x, weight, gamma, beta, ln_weight, ln_bias):
        import jax, jax.numpy as jnp
        import numpy as np
        D_IN = 256
        D_OUT = 256
        EPS = 1e-05
        mean = jnp.mean(x, axis=-1, keepdims=True)
        var = jnp.mean(jnp.square(x - mean), axis=-1, keepdims=True)
        xn = (x - mean) * jax.lax.rsqrt(var + EPS) * ln_weight + ln_bias
        quant_w = jnp.sign(weight)
        scale = jnp.max(jnp.abs(weight))
        out = jnp.einsum('bsk,ok->bso', xn, quant_w)
        return out * scale * gamma + beta

    def _L2_attn_ref(hidden_states, Wq, Wk, Wv, Wo, gate):
        import jax, jax.numpy as jnp
        import numpy as np
        HIDDEN = 256
        N_HEADS = 16
        HEAD_DIM = HIDDEN // N_HEADS

        def rotate_half(x):
            x1, x2 = jnp.split(x, 2, axis=-1)
            return jnp.concatenate([-x2, x1], axis=-1)
        B, S, H = hidden_states.shape
        q = hidden_states @ Wq.T
        k = hidden_states @ Wk.T
        v = hidden_states @ Wv.T
        inv_freq = 1.0 / 10000.0 ** (jnp.arange(0, H, 2, dtype=jnp.float32) / H)
        t = jnp.arange(S, dtype=jnp.float32)
        freqs = t[:, None] * inv_freq[None, :]
        emb = jnp.concatenate([freqs, freqs], axis=-1)[None]
        cos, sin = (jnp.cos(emb), jnp.sin(emb))
        q = q * cos + rotate_half(q) * sin
        k = k * cos + rotate_half(k) * sin

        def split_heads(x):
            return x.reshape(B, S, N_HEADS, HEAD_DIM).transpose(0, 2, 1, 3)
        q, k, v = (split_heads(q), split_heads(k), split_heads(v))
        k_feat = jax.nn.elu(k) + 1.0
        memory = jnp.einsum('bhsd,bhse->bhde', k_feat, v)
        norm_term = k_feat.sum(axis=2)
        q_feat = jax.nn.elu(q) + 1.0
        mem_out = jnp.einsum('bhsd,bhde->bhse', q_feat, memory)
        denom = jnp.einsum('bhsd,bhd->bhs', q_feat, norm_term)[..., None]
        mem_out = mem_out / denom
        scale = 1.0 / jnp.sqrt(jnp.float32(HEAD_DIM))
        scores = jnp.einsum('bhqd,bhkd->bhqk', q, k) * scale
        attn = jnp.einsum('bhqk,bhkd->bhqd', jax.nn.softmax(scores, axis=-1), v)
        g = jax.nn.sigmoid(gate)
        combined = g * mem_out + (1.0 - g) * attn
        combined = combined.transpose(0, 2, 1, 3).reshape(B, S, H)
        return combined @ Wo.T

    def _L2_ffn_ref(x, weight, bias):
        import jax, jax.numpy as jnp
        import numpy as np

        def binarize_weight(w):
            alpha = jnp.mean(jnp.abs(w), axis=tuple(range(1, w.ndim)), keepdims=True)
            bw = jnp.where(w >= 0, 1.0, -1.0) * alpha
            return jax.lax.stop_gradient(bw - w) + w
        bw = binarize_weight(weight)
        return jnp.einsum('bsi,oi->bso', x, bw) + bias

    def _L3_attn_ref(x, W_in, W_out, gamma, beta, D):
        import jax, jax.numpy as jnp
        import numpy as np
        B, L, DM = (2, 256, 256)
        H, P, N = (32, 64, 64)
        D_INNER = H * P
        PROJ = 2 * D_INNER + 2 * H * N + H
        EPS = 1e-05
        Bz, Lz, _ = x.shape
        zxbca = x @ W_in.T
        x_t, z_t, b_t, c_t, a_log = jnp.split(zxbca, [D_INNER, 2 * D_INNER, 2 * D_INNER + H * N, 2 * D_INNER + 2 * H * N], axis=-1)
        x_t = x_t.reshape(Bz, Lz, H, P)
        b_t = b_t.reshape(Bz, Lz, H, N)
        c_t = c_t.reshape(Bz, Lz, H, N)
        decay = jnp.exp(-jnp.exp(a_log))

        def step(states, inp):
            xt, bt, ct, dec = inp
            states = states * dec[:, :, None, None] + xt[..., None] * bt[:, :, None, :]
            yt = jnp.einsum('bhpn,bhn->bhp', states, ct) + xt * D
            return (states, yt)
        init = jnp.zeros((Bz, H, P, N), x.dtype)
        xs = (jnp.moveaxis(x_t, 1, 0), jnp.moveaxis(b_t, 1, 0), jnp.moveaxis(c_t, 1, 0), jnp.moveaxis(decay, 1, 0))
        _, ys = jax.lax.scan(step, init, xs)
        y = jnp.moveaxis(ys, 0, 1).reshape(Bz, Lz, D_INNER)
        y = y * jax.nn.silu(z_t)
        mu = y.mean(-1, keepdims=True)
        var = y.var(-1, keepdims=True)
        y = (y - mu) * jax.lax.rsqrt(var + EPS) * gamma + beta
        return y @ W_out.T

    def _L3_ffn_ref(x, w_cls, bias, w_gate_up, w_down):
        import jax, jax.numpy as jnp
        import numpy as np
        B, S, H = (2, 128, 256)
        I = 128
        E = 32
        Z = 32
        K = 8
        SCALE = 1.5
        CAP = 128
        EPS = 1e-20

        def _moe_forward(x, w_cls, bias, w_gate_up, w_down):
            T = x.shape[0] * x.shape[1]
            xf = x.reshape(T, H)
            logits = xf.astype(jnp.float32) @ w_cls.T
            scores = jax.nn.softmax(logits, axis=-1)
            _, topk_idx = jax.lax.top_k(scores + bias[None, :], K)
            w = jnp.take_along_axis(scores, topk_idx, axis=-1)
            w = w / (w.sum(-1, keepdims=True) + EPS) * SCALE
            routed = topk_idx < E
            w_r = jnp.where(routed, w, 0.0)
            w_z = jnp.where(routed, 0.0, w)
            N = T * K
            flat_ids = jnp.where(routed, topk_idx, E).reshape(-1)
            x_exp = jnp.repeat(xf, K, axis=0)
            order = jnp.argsort(flat_ids)
            ids_s = flat_ids[order]
            counts = jax.ops.segment_sum(jnp.ones(N, jnp.int32), flat_ids, num_segments=E + 1)
            starts = jnp.cumsum(counts) - counts
            pos = jnp.arange(N) - starts[ids_s]
            buf = jnp.zeros((E, CAP, H), xf.dtype).at[ids_s, pos].set(x_exp[order], mode='drop')
            gu = jnp.einsum('ech,ehf->ecf', buf, w_gate_up)
            g, u = jnp.split(gu, 2, axis=-1)
            act = jax.nn.silu(g) * u
            y = jnp.einsum('eci,eih->ech', act, w_down)
            valid = (ids_s < E) & (pos < CAP)
            y_tok = jnp.where(valid[:, None], y[jnp.clip(ids_s, 0, E - 1), jnp.clip(pos, 0, CAP - 1)], 0.0)
            y_exp = jnp.zeros((N, H), xf.dtype).at[order].set(y_tok).reshape(T, K, H)
            routed_out = jnp.einsum('tk,tkh->th', w_r, y_exp)
            out = routed_out * (1.0 + w_z.sum(-1, keepdims=True))
            return out.reshape(x.shape)
        return _moe_forward(x, w_cls, bias, w_gate_up, w_down)
    x = L0_attn_x
    xn = _layernorm(x, axis=-1)
    x = x + _L0_attn_ref(xn, L0_attn_w_q, L0_attn_w_kv, L0_attn_w_dense) + _L0_ffn_ref(xn, L0_ffn_SU_ug, L0_ffn_SU_dp, L0_ffn_Wscale_ug, L0_ffn_Wscale_dp, L0_ffn_W_up, L0_ffn_W_gate, L0_ffn_W_down)
    xn = _layernorm(x, axis=-1)
    x = x + _L1_attn_ref(xn, L1_attn_Wq, L1_attn_bq, L1_attn_Wk, L1_attn_bk, L1_attn_Wv, L1_attn_bv, L1_attn_Wg, L1_attn_bg, L1_attn_Wo, L1_attn_bo) + _L1_ffn_ref(xn, L1_ffn_weight, L1_ffn_gamma, L1_ffn_beta, L1_ffn_ln_weight, L1_ffn_ln_bias)
    xn = _layernorm(x, axis=-1)
    x = x + _L2_attn_ref(xn, L2_attn_Wq, L2_attn_Wk, L2_attn_Wv, L2_attn_Wo, L2_attn_gate) + _L2_ffn_ref(xn, L2_ffn_weight, L2_ffn_bias)
    xn = _layernorm(x, axis=-1)
    x = x + _L3_attn_ref(xn, L3_attn_W_in, L3_attn_W_out, L3_attn_gamma, L3_attn_beta, L3_attn_D) + _L3_ffn_ref(xn, L3_ffn_w_cls, L3_ffn_bias, L3_ffn_w_gate_up, L3_ffn_w_down)
    return x

_drawn_inputs = setup_inputs


def setup_inputs(seed=0):
    import zlib

    import numpy as np

    out = dict(_drawn_inputs(seed))
    spreads = {'L1_attn_bq': (0.0, 0.8),
     'L1_attn_bk': (0.0, 0.8),
     'L1_attn_bv': (0.0, 0.8),
     'L1_attn_bg': (0.0, 0.8),
     'L1_attn_bo': (0.0, 0.8),
     'L1_ffn_gamma': (1.0, 0.2),
     'L1_ffn_beta': (0.0, 0.8),
     'L1_ffn_ln_weight': (1.0, 0.2),
     'L1_ffn_ln_bias': (0.0, 0.1),
     'L2_attn_gate': (0.0, 0.8),
     'L3_attn_gamma': (1.0, 0.6),
     'L3_attn_beta': (0.0, 0.8),
     'L3_attn_D': (1.0, 0.6)}
    factors = {'L0_attn_w_q': 8.0,
     'L0_ffn_Wscale_ug': 4.178,
     'L0_ffn_Wscale_dp': 5.8,
     'L1_attn_Wq': 8.0,
     'L1_attn_Wk': 8.0,
     'L1_attn_Wv': 8.0,
     'L1_attn_Wg': 8.0,
     'L1_attn_Wo': 8.0,
     'L2_attn_Wq': 8.0,
     'L2_attn_Wk': 8.0,
     'L2_attn_Wv': 8.0,
     'L2_attn_Wo': 8.0,
     'L2_ffn_weight': 3.975,
     'L2_ffn_bias': 200.0,
     'L3_attn_W_in': 4.281,
     'L3_attn_W_out': 4.259,
     'L3_ffn_w_cls': 8.0,
     'L3_ffn_bias': 8.0,
     'L3_ffn_w_gate_up': 8.0,
     'L3_ffn_w_down': 8.0}
    for name, (base, spread) in spreads.items():
        noise = np.random.default_rng([zlib.crc32(name.encode()), seed]).standard_normal(out[name].shape)
        drawn = base * np.exp(spread * noise) if base else spread * noise
        out[name] = jnp.asarray(drawn.astype(out[name].dtype))
    for name, factor in factors.items():
        out[name] = (out[name] * factor).astype(out[name].dtype)
    return out
```

```python
from contextlib import ExitStack

import numpy as np

import concourse.bass as bass
from concourse import mybir

F32 = mybir.dt.float32
I32 = mybir.dt.int32
U32 = mybir.dt.uint32
BF16 = mybir.dt.bfloat16
ALU = mybir.AluOpType
ACT = mybir.ActivationFunctionType
AX_X = mybir.AxisListType.X
ds = bass.ds

P = 128
BANK = 512
B, S, D = 2, 1024, 256
T = B * S
DC = D // P
NQ = S // P
TT = T // P
NJ = T // BANK
EPS = 1e-5


class Stage:

    counts = []

    def __init__(self, nc, name):
        self.nc, self.name, self.ctx = nc, name, ExitStack()

    def __enter__(self):
        return self

    def __exit__(self, *e):
        return self.ctx.__exit__(*e)

    def sb(self, name, shape, dt=F32):
        return self.ctx.enter_context(self.nc.sbuf_tensor(f"{self.name}_{name}", shape, dt))

    def ps(self, name, cols=BANK):
        return self.ctx.enter_context(self.nc.psum_tensor(f"{self.name}_{name}", [P, cols], F32))

    def sem(self, name):
        s = self.ctx.enter_context(self.nc.semaphore(f"{self.name}_{name}"))
        Stage.counts.append(s.num)
        return s


def clear_semaphores(nc):
    numbers = sorted(set(Stage.counts))
    Stage.counts.clear()
    with nc.Block() as block:

        @block.gpsimd
        def _(pool):
            while numbers:
                first = last = numbers.pop(0)
                while numbers and numbers[0] == last + 1:
                    last = numbers.pop(0)
                pool.sem_clear(range(first, last + 1))


def rows(w):
    return w.rearrange("(c p) n -> p c n", p=P)


def wait(engine, sem, value):
    if not isinstance(value, int) or value > 0:
        engine.wait_ge(sem, value)


def norm_stage(nc, k, name, src, dst):
    with Stage(nc, name) as st:
        mean = [st.ps(f"mean{i}") for i in range(2)]
        var = [st.ps(f"var{i}") for i in range(2)]
        sq = st.sb("sq", [P, 2, DC, BANK])
        std = st.sb("std", [P, 2, BANK])
        rstd = st.sb("rstd", [P, 2, BANK])
        mean_ready, centred, squared = st.sem("mean_ready"), st.sem("centred"), st.sem("squared")
        var_ready, std_ready, rstd_ready = st.sem("var_ready"), st.sem("std_ready"), st.sem("rstd_ready")
        scaled = st.sem("scaled")

        def tok(j):
            return slice(j * BANK, (j + 1) * BANK)

        with nc.Block() as block:

            @block.tensor
            def _(pe):
                def mean_of(j):
                    if j >= 2:
                        pe.wait_ge(centred, j - 1)
                    for c in range(DC):
                        mm = pe.matmul(mean[j % 2][:, :], k.avg[:, :], src[:, c, tok(j)], start=(c == 0), stop=(c == DC - 1))
                    mm.then_inc(mean_ready, 1)

                def var_of(j):
                    pe.wait_ge(squared, j + 1)
                    if j >= 2:
                        pe.wait_ge(std_ready, j - 1)
                    for c in range(DC):
                        mm = pe.matmul(var[j % 2][:, :], k.avg[:, :], sq[:, j % 2, c, :], start=(c == 0), stop=(c == DC - 1))
                    mm.then_inc(var_ready, 1)

                mean_of(0)
                for j in range(NJ):
                    if j + 1 < NJ:
                        mean_of(j + 1)
                    var_of(j)

            @block.vector
            def _(dve):
                def centre(j):
                    dve.wait_ge(mean_ready, j + 1)
                    for c in range(DC):
                        op = dve.tensor_tensor(dst[:, c, tok(j)], src[:, c, tok(j)], mean[j % 2][:, :], ALU.subtract)
                    op.then_inc(centred, 1)

                centre(0)
                for j in range(NJ):
                    if j + 1 < NJ:
                        centre(j + 1)
                    dve.wait_ge(std_ready, j + 1)
                    if j >= 2:
                        dve.wait_ge(scaled, j - 1)
                    dve.reciprocal(rstd[:, j % 2, :], std[:, j % 2, :]).then_inc(rstd_ready, 1)

            @block.scalar
            def _(act):
                for j in range(NJ):
                    act.wait_ge(centred, j + 1)
                    if j >= 2:
                        act.wait_ge(var_ready, j - 1)
                    act.activation(sq[:, j % 2, :, :], dst[:, :, tok(j)], ACT.Square).then_inc(squared, 1)
                    act.wait_ge(var_ready, j + 1)
                    if j >= 2:
                        act.wait_ge(rstd_ready, j - 1)
                    act.activation(std[:, j % 2, :], var[j % 2][:, :], ACT.Sqrt, bias=k.eps[:, 0:1]).then_inc(std_ready, 1)

            @block.gpsimd
            def _(pool):
                for j in range(NJ):
                    pool.wait_ge(rstd_ready, j + 1)
                    for c in range(DC):
                        op = pool.tensor_tensor(dst[:, c, tok(j)], dst[:, c, tok(j)], rstd[:, j % 2, :], ALU.mult)
                    op.then_inc(scaled, 1)


L0_HEADS, L0_GROUPS, L0_HD = 16, 4, 128
L0_HPG = L0_HEADS // L0_GROUPS
L0_SCALE = L0_HD ** -0.5


def l0_attn(nc, k, a):
    with Stage(nc, "l0a") as st:
        KT = st.sb("KT", [P, L0_GROUPS, T])
        V = st.sb("V", [P, TT, L0_GROUPS * L0_HD])
        wkv = st.sb("wkv", [P, DC, 2 * L0_GROUPS * L0_HD])
        l0_kv(nc, k, a, KT, V, wkv)
        l0_heads(nc, k, a, KT, V)


def l0_kv(nc, k, a, KT, V, wkv):
    with Stage(nc, "l0kv") as st:
        acc = [st.ps(f"acc{i}") for i in range(8)]
        w_loaded, made, kept_act, kept_dve = st.sem("w_loaded"), st.sem("made"), st.sem("kept_act"), st.sem("kept_dve")
        GD = L0_GROUPS * L0_HD
        jobs = [("k", g, j) for g in range(L0_GROUPS) for j in range(NJ)] + [("v", t, 0) for t in range(TT)]

        def target(n):
            kind, i, j = jobs[n]
            return KT[:, i, j * BANK:(j + 1) * BANK] if kind == "k" else V[:, i, :]

        with nc.Block() as block:

            @block.sync
            def _(sp):
                sp.dma_start(wkv[:, :, :], rows(a["L0_attn_w_kv"])).then_inc(w_loaded, 16)

            @block.tensor
            def _(pe):
                pe.wait_ge(w_loaded, 16)
                for n, (kind, i, j) in enumerate(jobs):
                    if n >= 8:
                        pe.wait_ge(kept_act if n % 2 == 0 else kept_dve, (n - 8) // 2 + 1)
                    for c in range(DC):
                        if kind == "k":
                            mm = pe.matmul(acc[n % 8][:, :], wkv[:, c, i * P:(i + 1) * P], k.XN[:, c, j * BANK:(j + 1) * BANK],
                                           start=(c == 0), stop=(c == DC - 1))
                        else:
                            mm = pe.matmul(acc[n % 8][:, :], k.XN[:, c, i * P:(i + 1) * P], wkv[:, c, GD:2 * GD],
                                           start=(c == 0), stop=(c == DC - 1))
                    mm.then_inc(made, 1)

            @block.scalar
            def _(act):
                for n in range(0, len(jobs), 2):
                    act.wait_ge(made, n + 1)
                    act.activation(target(n), acc[n % 8][:, :], ACT.Copy).then_inc(kept_act, 1)

            @block.vector
            def _(dve):
                for n in range(1, len(jobs), 2):
                    dve.wait_ge(made, n + 1)
                    dve.tensor_copy(target(n), acc[n % 8][:, :]).then_inc(kept_dve, 1)


def l0_heads(nc, k, a, KT, V):
    U = B * NQ
    GPB = sum(-(-(t + 1) // 4) for t in range(NQ))
    G = B * GPB
    group_of = [(u, g) for u in range(U) for g in range(-(-(u % NQ + 1) // 4))]
    first_group = [group_of.index((u, 0)) for u in range(U)]

    with Stage(nc, "l0h") as st:
        wq = st.sb("wq", [P, DC, P])
        wd = st.sb("wd", [P, D])
        QT = st.sb("QT", [P, T])
        probs = st.sb("probs", [P, 2, S])
        PT = st.sb("PT", [P, 2, NQ, P])
        ctx = st.sb("ctx", [P, 2, P])
        ctxT = st.sb("ctxT", [P, 2, P])
        top = st.sb("top", [P, 2])
        negtop = st.sb("negtop", [P, 2])
        total = st.sb("total", [P, 2])
        inv = st.sb("inv", [P, 2])
        sc = [st.ps(f"sc{i}", 2 * BANK) for i in range(2)]
        tp = [st.ps(f"tp{i}") for i in range(2)]
        cx = st.ps("cx")
        outp = st.ps("outp")
        wq_loaded, wd_loaded = st.sem("wq_loaded"), st.sem("wd_loaded")
        q_made, q_kept = st.sem("q_made"), st.sem("q_kept")
        scores_ready, masked, top_ready, negtop_ready = st.sem("scores_ready"), st.sem("masked"), st.sem("top_ready"), st.sem("negtop_ready")
        probs_ready, inv_ready = st.sem("probs_ready"), st.sem("inv_ready")
        turned, pt_act, pt_dve, pv_done = st.sem("turned"), st.sem("pt_act"), st.sem("pt_dve"), st.sem("pv_done")
        ctx_ready, ctx_turned, ctxT_ready = st.sem("ctx_ready"), st.sem("ctx_turned"), st.sem("ctxT_ready")
        dense_done, added = st.sem("dense_done"), st.sem("added")

        def keys(u):
            return (u % NQ + 1) * P

        with nc.Block() as block:

            @block.sync
            def _(sp):
                sp.dma_start(wq[:, :, :], rows(a["L0_attn_w_q"])[:, :, 0:P]).then_inc(wq_loaded, 16)
                sp.dma_start(wd[:, :], a["L0_attn_w_dense"][0:P, :]).then_inc(wd_loaded, 16)
                with sp.Fori(1, L0_HEADS) as h:
                    sp.wait_ge(q_made, h * NJ)
                    sp.dma_start(wq[:, :, :], rows(a["L0_attn_w_q"])[:, :, ds(h * P, P)]).then_inc(wq_loaded, 16)
                    sp.wait_ge(dense_done, h * U)
                    sp.dma_start(wd[:, :], a["L0_attn_w_dense"][ds(h * P, P), :]).then_inc(wd_loaded, 16)

            @block.tensor
            def _(pe):
                with pe.Fori(0, L0_GROUPS) as g:
                    with pe.Fori(0, L0_HPG) as hg:
                        h = g * L0_HPG + hg

                        def scores(u):
                            b, t = divmod(u, NQ)
                            if u >= 2:
                                pe.wait_ge(probs_ready, h * U + u - 1)
                            elif u == 0:
                                pe.wait_ge(q_kept, h * NJ + 2)
                            else:
                                pe.wait_ge(q_kept, h * NJ + 4)
                            for lo in range(0, keys(u), BANK):
                                n = min(BANK, keys(u) - lo)
                                mm = pe.matmul(sc[u % 2][:, lo:lo + n], QT[:, u * P:(u + 1) * P],
                                               KT[:, ds(g, 1), b * S + lo:b * S + lo + n], start=True, stop=True)
                            mm.then_inc(scores_ready, 1)

                        def turn_probs(u):
                            t = u % NQ
                            pe.wait_ge(probs_ready, h * U + u + 1)
                            for n in range(first_group[u], first_group[u] + -(-(t + 1) // 4)):
                                if n % 2 == 0:
                                    pe.wait_ge(pt_act, h * (G // 2) + n // 2 + 1)
                                else:
                                    pe.wait_ge(pt_dve, h * (G // 2) + n // 2 + 1)
                                q = 4 * (n - first_group[u])
                                for kb in range(q, min(q + 4, t + 1)):
                                    mm = pe.transpose(tp[n % 2][:, (kb - q) * P:(kb - q + 1) * P],
                                                      probs[:, u % 2, kb * P:(kb + 1) * P], k.ident[:, :])
                                mm.then_inc(turned, 1)

                        def weigh_values(u):
                            b, t = divmod(u, NQ)
                            last = first_group[u] + -(-(t + 1) // 4) - 1
                            pe.wait_ge(pt_act, h * (G // 2) + last // 2 + 2)
                            pe.wait_ge(pt_dve, h * (G // 2) + (last + 1) // 2 + 1)
                            for kb in range(t + 1):
                                mm = pe.matmul(cx[:, 0:P], PT[:, u % 2, kb, :],
                                               V[:, b * NQ + kb, ds(g * P, P)], start=(kb == 0), stop=(kb == t))
                            mm.then_inc(pv_done, 1)

                        def turn_ctx(u):
                            pe.wait_ge(ctx_ready, h * U + u + 1)
                            pe.transpose(cx[:, P:2 * P], ctx[:, u % 2, :], k.ident[:, :]).then_inc(ctx_turned, 1)

                        def dense(u):
                            if u == 0:
                                pe.wait_ge(wd_loaded, h * 16 + 16)
                            pe.wait_ge(ctxT_ready, h * U + u + 1)
                            pe.wait_ge(added, h * U + u + 1)
                            for c in range(DC):
                                mm = pe.matmul(outp[:, c * P:(c + 1) * P], wd[:, c * P:(c + 1) * P], ctxT[:, u % 2, :],
                                               start=True, stop=True)
                            mm.then_inc(dense_done, 1)

                        pe.wait_ge(wq_loaded, h * 16 + 16)
                        for j in range(NJ):
                            for c in range(DC):
                                mm = pe.matmul(sc[j // 2][:, (j % 2) * BANK:(j % 2 + 1) * BANK], wq[:, c, :],
                                               k.XN[:, c, j * BANK:(j + 1) * BANK], start=(c == 0), stop=(c == DC - 1))
                            mm.then_inc(q_made, 1)
                        for s in range(U + 2):
                            if s < U:
                                scores(s)
                            if s >= 2:
                                turn_ctx(s - 2)
                            if 1 <= s <= U:
                                turn_probs(s - 1)
                            if s >= 2:
                                dense(s - 2)
                            if 1 <= s <= U:
                                weigh_values(s - 1)

            @block.vector
            def _(dve):
                dve.sem_inc(pt_dve, 1)
                dve.sem_inc(added, 1)
                with dve.Fori(0, L0_HEADS) as h:

                    def row_max(u):
                        t = u % NQ
                        diag = sc[u % 2][:, t * P:(t + 1) * P]
                        dve.wait_ge(scores_ready, h * U + u + 1)
                        dve.tensor_tensor(diag, diag, k.causal[:, :], ALU.add).then_inc(masked, 1)
                        dve.wait_ge(masked, h * U + u + 1)
                        dve.reduce_max(top[:, u % 2:u % 2 + 1], sc[u % 2][:, 0:keys(u)], AX_X).then_inc(top_ready, 1)
                        dve.wait_ge(top_ready, h * U + u + 1)
                        dve.tensor_scalar(negtop[:, u % 2:u % 2 + 1], top[:, u % 2:u % 2 + 1], -L0_SCALE, None,
                                          ALU.mult).then_inc(negtop_ready, 1)

                    def invert(u):
                        dve.wait_ge(probs_ready, h * U + u + 1)
                        dve.reciprocal(inv[:, u % 2:u % 2 + 1], total[:, u % 2:u % 2 + 1]).then_inc(inv_ready, 1)

                    def keep_turned(u):
                        t = u % NQ
                        for n in range(first_group[u], first_group[u] + -(-(t + 1) // 4)):
                            if n % 2 == 1:
                                q = 4 * (n - first_group[u])
                                m = min(4, t + 1 - q)
                                dve.wait_ge(turned, h * G + n + 1)
                                if u >= 2:
                                    dve.wait_ge(pv_done, h * U + u - 1)
                                dve.tensor_copy(PT[:, u % 2, q:q + m, :], tp[1][:, 0:m * P]).then_inc(pt_dve, 1)

                    def add_dense(u):
                        dve.wait_ge(dense_done, h * U + u + 1)
                        x = k.XT[:, :, u * P:(u + 1) * P]
                        dve.tensor_tensor(x, x, outp[:, 0:DC * P].rearrange("p (c n) -> p c n", c=DC), ALU.add).then_inc(added, 1)

                    def scale_ctx(u):
                        dve.wait_ge(pv_done, h * U + u + 1)
                        dve.wait_ge(inv_ready, h * U + u + 1)
                        dve.tensor_scalar(ctx[:, u % 2, :], cx[:, 0:P], inv[:, u % 2:u % 2 + 1], None,
                                          ALU.mult).then_inc(ctx_ready, 1)

                    for s in range(U + 2):
                        if 1 <= s <= U:
                            invert(s - 1)
                        if s < U:
                            row_max(s)
                        if 1 <= s <= U:
                            keep_turned(s - 1)
                        if s >= 2:
                            add_dense(s - 2)
                        if 1 <= s <= U:
                            scale_ctx(s - 1)

            @block.scalar
            def _(act):
                act.sem_inc(pt_act, 1)
                with act.Fori(0, L0_HEADS) as h:

                    def keep_turned(u):
                        t = u % NQ
                        for n in range(first_group[u], first_group[u] + -(-(t + 1) // 4)):
                            if n % 2 == 0:
                                q = 4 * (n - first_group[u])
                                m = min(4, t + 1 - q)
                                act.wait_ge(turned, h * G + n + 1)
                                if u >= 2:
                                    act.wait_ge(pv_done, h * U + u - 1)
                                act.activation(PT[:, u % 2, q:q + m, :], tp[0][:, 0:m * P].rearrange("p (m n) -> p m n", m=m),
                                               ACT.Copy).then_inc(pt_act, 1)

                    def keep_ctxT(u):
                        act.wait_ge(ctx_turned, h * U + u + 1)
                        if u >= 2:
                            act.wait_ge(dense_done, h * U + u - 1)
                        act.activation(ctxT[:, u % 2, :], cx[:, P:2 * P], ACT.Copy).then_inc(ctxT_ready, 1)

                    def exp(u):
                        act.wait_ge(negtop_ready, h * U + u + 1)
                        if u >= 2:
                            act.wait_ge(turned, h * G + first_group[u - 1])
                        act.activation(probs[:, u % 2, 0:keys(u)], sc[u % 2][:, 0:keys(u)], ACT.Exp,
                                       bias=negtop[:, u % 2:u % 2 + 1], scale=L0_SCALE,
                                       accum_out=total[:, u % 2:u % 2 + 1]).then_inc(probs_ready, 1)

                    for j in range(NJ):
                        act.wait_ge(q_made, h * NJ + j + 1)
                        act.activation(QT[:, j * BANK:(j + 1) * BANK], sc[j // 2][:, (j % 2) * BANK:(j % 2 + 1) * BANK],
                                       ACT.Copy).then_inc(q_kept, 1)
                    for s in range(U + 2):
                        if s >= 2:
                            keep_ctxT(s - 2)
                        if 1 <= s <= U:
                            keep_turned(s - 1)
                        if s < U:
                            exp(s)


L0_INTER = 1024
L0_FC = L0_INTER // P


def l0_ffn(nc, k, a):
    with Stage(nc, "l0f") as st:
        wu = st.sb("wu", [P, DC, L0_INTER])
        wg = st.sb("wg", [P, DC, L0_INTER])
        wdn = st.sb("wdn", [P, L0_FC, D])
        su = st.sb("su", [P, DC])
        sd = st.sb("sd", [P, L0_FC])
        su_n = st.sb("su_n", [P, DC])
        sd_n = st.sb("sd_n", [P, L0_FC])
        s_up = st.sb("s_up", [P, L0_FC])
        s_gate = st.sb("s_gate", [P, L0_FC])
        s_down = st.sb("s_down", [P, DC])
        with Stage(nc, "l0w") as s2:
            had = s2.sb("had", [P, 2, P])
            raw = s2.sb("raw", [P, 2, DC, L0_INTER])
            rawd = s2.sb("rawd", [P, L0_FC, D])
            bf0 = s2.sb("bf0", [P, L0_FC, D])
            bf1 = s2.sb("bf1", [P, L0_FC, D])
            acc = [s2.ps(f"acc{i}") for i in range(8)]
            loaded, made, kept, had_ready, flown = s2.sem("loaded"), s2.sem("made"), s2.sem("kept"), s2.sem("had_ready"), s2.sem("flown")
            NL = 9

            with nc.Block() as block:

                @block.sync
                def _(sp):
                    sp.dma_start(had[:, 0, :], a["c_had"]).then_inc(loaded, 16)
                    sp.dma_start(su[:, :], a["L0_ffn_SU_ug_cols"]).then_inc(loaded, 16)
                    sp.dma_start(raw[:, 0, :, :], rows(a["L0_ffn_W_upT"])).then_inc(loaded, 16)
                    sp.dma_start(raw[:, 1, :, :], rows(a["L0_ffn_W_gateT"])).then_inc(loaded, 16)
                    sp.dma_start(rawd[:, :, :], rows(a["L0_ffn_W_downT"])).then_inc(loaded, 16)
                    sp.dma_start(sd[:, :], a["L0_ffn_SU_dp_cols"]).then_inc(loaded, 16)
                    sp.dma_start(s_up[:, :], a["L0_ffn_Wscale_ug_cols"][:, 0:L0_FC]).then_inc(loaded, 16)
                    sp.dma_start(s_gate[:, :], a["L0_ffn_Wscale_ug_cols"][:, L0_FC:2 * L0_FC]).then_inc(loaded, 16)
                    sp.dma_start(s_down[:, :], a["L0_ffn_Wscale_dp_cols"]).then_inc(loaded, 16)

                @block.tensor
                def _(pe):
                    pe.wait_ge(had_ready, 1)
                    n = 0
                    for m in range(2):
                        for half in range(2):
                            for lo in range(0, L0_INTER, BANK):
                                for c in range(DC):
                                    neg = 1 if half == 1 and c == 1 else 0
                                    mm = pe.matmul(acc[n % 8][:, :], had[:, neg, :], raw[:, m, c, lo:lo + BANK],
                                                   start=(c == 0), stop=(c == DC - 1))
                                mm.then_inc(made, 1)
                                n += 1
                    for i in range(L0_FC // 2):
                        pe.wait_ge(kept, i + 1)
                        pe.matmul(acc[i][:, :], had[:, 0, :], rawd[:, 2 * i:2 * i + 2, :], start=True, stop=True).then_inc(made, 1)

                @block.scalar
                def _(act):
                    act.wait_ge(had_ready, 3)
                    for n in range(8):
                        m, half, q = n // 4, n // 2 % 2, n % 2
                        act.wait_ge(made, n + 1)
                        act.activation((wu, wg)[m][:, half, q * BANK:(q + 1) * BANK], acc[n][:, :], ACT.Copy,
                                       scale=su_n[:, half:half + 1]).then_inc(kept, 1)
                    for i in range(L0_FC // 2):
                        act.wait_ge(made, 9 + i)
                        act.activation(bf0[:, 2 * i:2 * i + 2, :], acc[i][:, :].rearrange("p (i n) -> p i n", i=2),
                                       ACT.Copy).then_inc(kept, 1)

                @block.vector
                def _(dve):
                    dve.wait_ge(loaded, 16 * NL)
                    dve.tensor_scalar(had[:, 1, :], had[:, 0, :], -1.0, None, ALU.mult).then_inc(had_ready, 1)
                    dve.tensor_scalar(su_n[:, :], su[:, :], D ** -0.5, None, ALU.mult).then_inc(had_ready, 1)
                    dve.tensor_scalar(sd_n[:, :], sd[:, :], L0_INTER ** -0.5, None, ALU.mult).then_inc(had_ready, 1)
                    dve.wait_ge(kept, 12)
                    src, dst = bf0, bf1
                    for i, h in enumerate((1, 2, 4)):
                        if i:
                            dve.wait_ge(flown, 2 * i)
                        sv = src[:, :, :].rearrange("p (g t h) n -> p g t (h n)", t=2, h=h)
                        dv = dst[:, :, :].rearrange("p (g t h) n -> p g t (h n)", t=2, h=h)
                        dve.tensor_tensor(dv[:, :, 0, :], sv[:, :, 0, :], sv[:, :, 1, :], ALU.add).then_inc(flown, 1)
                        dve.tensor_tensor(dv[:, :, 1, :], sv[:, :, 0, :], sv[:, :, 1, :], ALU.subtract).then_inc(flown, 1)
                        src, dst = dst, src
                    dve.wait_ge(flown, 6)
                    dve.wait_ge(had_ready, 3)
                    for i in range(L0_FC):
                        dve.tensor_scalar(wdn[:, i, :], src[:, i, :], sd_n[:, i:i + 1], None, ALU.mult)

        hid = st.sb("hid", [P, L0_FC, BANK])
        sg = st.sb("sg", [P, 2, BANK])
        up = [st.ps(f"up{i}") for i in range(2)]
        gate = [st.ps(f"gate{i}") for i in range(2)]
        down = [st.ps(f"down{i}") for i in range(2)]
        gate_ready, up_ready, silu_ready, hid_ready = st.sem("gate_ready"), st.sem("up_ready"), st.sem("silu_ready"), st.sem("hid_ready")
        down_ready, added = st.sem("down_ready"), st.sem("added")

        with nc.Block() as block:

            @block.tensor
            def _(pe):
                with pe.Fori(0, NJ) as j:
                    for f in range(L0_FC):
                        for w, psum, ready, used in ((wg, gate, gate_ready, silu_ready), (wu, up, up_ready, hid_ready)):
                            pe.wait_ge(used, j * L0_FC + f + 1)
                            for c in range(DC):
                                mm = pe.matmul(psum[f % 2][:, :], w[:, c, f * P:(f + 1) * P], k.XN[:, c, ds(j * BANK, BANK)],
                                               start=(c == 0), stop=(c == DC - 1))
                            mm.then_inc(ready, 1)
                    for c in range(DC):
                        pe.wait_ge(added, j * DC + c + 1)
                        for f in range(L0_FC):
                            if c == 0:
                                pe.wait_ge(hid_ready, j * L0_FC + f + 1 + 2)
                            mm = pe.matmul(down[c][:, :], wdn[:, f, c * P:(c + 1) * P], hid[:, f, :],
                                           start=(f == 0), stop=(f == L0_FC - 1))
                        mm.then_inc(down_ready, 1)

            @block.scalar
            def _(act):
                act.sem_inc(silu_ready, 2)
                with act.Fori(0, NJ) as j:
                    for f in range(L0_FC):
                        act.wait_ge(gate_ready, j * L0_FC + f + 1)
                        act.wait_ge(hid_ready, j * L0_FC + f + 1)
                        act.activation(sg[:, f % 2, :], gate[f % 2][:, :], ACT.Silu, scale=s_gate[:, f:f + 1]).then_inc(silu_ready, 1)

            @block.vector
            def _(dve):
                dve.sem_inc(hid_ready, 2)
                dve.sem_inc(added, 1)
                with dve.Fori(0, NJ) as j:
                    for f in range(L0_FC):
                        dve.wait_ge(up_ready, j * L0_FC + f + 1)
                        dve.wait_ge(silu_ready, j * L0_FC + f + 1 + 2)
                        dve.scalar_tensor_tensor(out=hid[:, f, :], in0=up[f % 2][:, :], scalar=s_up[:, f:f + 1],
                                                 in1=sg[:, f % 2, :], op0=ALU.mult, op1=ALU.mult).then_inc(hid_ready, 1)
                    for c in range(DC):
                        dve.wait_ge(down_ready, j * DC + c + 1)
                        x = k.XT[:, c, ds(j * BANK, BANK)]
                        dve.scalar_tensor_tensor(out=x, in0=down[c][:, :], scalar=s_down[:, c:c + 1], in1=x,
                                                 op0=ALU.mult, op1=ALU.add).then_inc(added, 1)



L1_HEADS, L1_HD = 16, 128
QUAD = 4
NZ = S // BANK
NQD = B * NZ


def l1_attn(nc, k, a):
    with Stage(nc, "l1a") as st:
        w4 = st.sb("w4", [P, 4, DC, P])
        wo = st.sb("wo", [P, D])
        bias = st.sb("bias", [P, 3])
        bv = st.sb("bv", [P, P])
        mask = st.sb("mask", [P, P])
        grow = st.sb("grow", [P, P])
        gcol = st.sb("gcol", [P, 2])
        cosq, sinq = st.sb("cosq", [P, S]), st.sb("sinq", [P, S])
        cosk, sink = st.sb("cosk", [P, S]), st.sb("sink", [P, S])
        neghalf = st.sb("neghalf", [P, QUAD])
        qraw, kraw = st.sb("qraw", [P, 2, BANK]), st.sb("kraw", [P, 2, BANK])
        qc, kc = st.sb("qc", [P, 2, BANK]), st.sb("kc", [P, 2, BANK])
        qs, ks = st.sb("qs", [P, 2, BANK]), st.sb("ks", [P, 2, BANK])
        qT, kT, qdT = st.sb("qT", [P, 2, BANK]), st.sb("kT", [P, 2, BANK]), st.sb("qdT", [P, 2, BANK])
        v = st.sb("v", [P, 2, QUAD, P])
        ktok = st.sb("ktok", [P, 2, QUAD, P])
        smT = st.sb("smT", [P, 2, QUAD, P])
        state = st.sb("state", [P, 2, QUAD, P])
        sg = st.sb("sg", [P, 2, BANK])
        stats = st.sb("stats", [P, QUAD, 6])
        mv = st.sb("mv", [P, QUAD, 2])
        veps = st.sb("veps", [P, QUAD])
        rstd = st.sb("rstd", [P, QUAD])
        gn = st.sb("gn", [P, QUAD, P])
        gated = st.sb("gated", [P, 2, BANK])
        pq, pk, pg, pv = st.ps("pq"), st.ps("pk"), st.ps("pg"), st.ps("pv")
        psc, pkt, pds, pret = st.ps("psc"), st.ps("pkt"), st.ps("pds"), st.ps("pret")
        pgt, pout = pq, (pk, pg)

        loaded_w4, loaded_wo, loaded_hc, loaded_t = st.sem("loaded_w4"), st.sem("loaded_wo"), st.sem("loaded_hc"), st.sem("loaded_t")
        q_made, k_made, g_made, v_made = st.sem("q_made"), st.sem("k_made"), st.sem("g_made"), st.sem("v_made")
        sc_made, kt_made, ds_made, ret_made = st.sem("sc_made"), st.sem("kt_made"), st.sem("ds_made"), st.sem("ret_made")
        gt_made, out_made = st.sem("gt_made"), st.sem("out_made")
        q_kept, k_kept, silu_kept, kt_kept = st.sem("q_kept"), st.sem("k_kept"), st.sem("silu_kept"), st.sem("kt_kept")
        v_kept, q_rot, k_rot, sc_masked = st.sem("v_kept"), st.sem("q_rot"), st.sem("k_rot"), st.sem("sc_masked")
        states, linked, stat1, stat2, veps_ready = st.sem("states"), st.sem("linked"), st.sem("stat1"), st.sem("stat2"), st.sem("veps_ready")
        normed, gated_ready, added = st.sem("normed"), st.sem("gated_ready"), st.sem("added")
        q_cos, k_cos, q_roped, k_roped = st.sem("q_cos"), st.sem("k_cos"), st.sem("q_roped"), st.sem("k_roped")
        q_decayed, rstd_ready, half_set = st.sem("q_decayed"), st.sem("rstd_ready"), st.sem("half_set")
        NHC = 5

        def place(n):
            b, z = divmod(n, NZ)
            return b, z, b * S + z * BANK

        def steps(engine, step):
            for q in range(NQD):
                step(0, q)
            with engine.Fori(1, L1_HEADS) as h:
                for q in range(NQD):
                    step(h, q)

        with nc.Block() as block:

            @block.sync
            def _(sp):
                def load_head(h, q):
                    hh = ds(h, 1)
                    if q == 0:
                        wait(sp, v_made, NQD * h)
                        sp.dma_start(w4[:, :, :, :], a["L1_w4"][hh].rearrange("a p t c n -> (a p) t c n")).then_inc(loaded_w4, 16)
                    if q == 1:
                        wait(sp, silu_kept, NQD * h)
                        wait(sp, kt_kept, NQD * h)
                        wait(sp, q_decayed, NQD * h)
                        wait(sp, states, NQD * h)
                        sp.dma_start(bias[:, :], a["L1_bias"][hh].rearrange("a p n -> (a p) n")).then_inc(loaded_hc, 16)
                        sp.dma_start(bv[:, :], a["L1_attn_bv"][hh, :].to_broadcast([P, P])).then_inc(loaded_hc, 16)
                        sp.dma_start(mask[:, :], a["c_l1_mask"][hh].rearrange("a p n -> (a p) n")).then_inc(loaded_hc, 16)
                        sp.dma_start(grow[:, :], a["c_l1_grow"][hh, :].to_broadcast([P, P])).then_inc(loaded_hc, 16)
                        sp.dma_start(gcol[:, :], a["c_l1_gcol"][hh].rearrange("a p n -> (a p) n")).then_inc(loaded_hc, 16)
                    if q == 2:
                        wait(sp, out_made, 2 * NQD * h)
                        sp.dma_start(wo[:, :], a["L1_attn_Wo"][ds(h * P, P), :]).then_inc(loaded_wo, 16)

                load_head(0, 0)
                load_head(0, 1)
                sp.dma_start(cosq[:, :], a["c_l1_rope"][0]).then_inc(loaded_t, 16)
                sp.dma_start(sinq[:, :], a["c_l1_rope"][1]).then_inc(loaded_t, 16)
                sp.dma_start(cosk[:, :], a["c_l1_rope"][2]).then_inc(loaded_t, 16)
                sp.dma_start(sink[:, :], a["c_l1_rope"][3]).then_inc(loaded_t, 16)
                load_head(0, 2)
                with sp.Fori(1, L1_HEADS) as h:
                    for q in range(3):
                        load_head(h, q)

            @block.tensor
            def _(pe):
                def project(h, q):
                    n, o = h * NQD + q, q % 2
                    b, z, c0 = place(q)
                    if q == 0:
                        pe.wait_ge(loaded_w4, 16 * h + 16)
                    for i, (bank, made, used, count) in enumerate(((pq, q_made, gated_ready, n - 1), (pk, k_made, added, 2 * (n - 2) + 1),
                                                                   (pg, g_made, added, 2 * (n - 2) + 2))):
                        wait(pe, used, count)
                        for c in range(DC):
                            mm = pe.matmul(bank[:, :], w4[:, i, c, :], k.XN[:, c, c0:c0 + BANK], start=(c == 0), stop=(c == DC - 1))
                        mm.then_inc(made, 1)
                    wait(pe, v_kept, n)
                    for t in range(QUAD):
                        for c in range(DC):
                            mm = pe.matmul(pv[:, t * P:(t + 1) * P], k.XN[:, c, c0 + t * P:c0 + (t + 1) * P], w4[:, 3, c, :],
                                           start=(c == 0), stop=(c == DC - 1))
                    mm.then_inc(v_made, 1)

                def retain(h, q):
                    n, o = h * NQD + q, q % 2
                    b, z, c0 = place(q)
                    wait(pe, normed, n)
                    pe.wait_ge(sc_masked, n + 1)
                    pe.wait_ge(q_decayed, n + 1)
                    pe.wait_ge(states, n + 1)
                    for t in range(QUAD):
                        inter = t > 0 or z > 0
                        mm = pe.matmul(pret[:, t * P:(t + 1) * P], smT[:, o, t, :], v[:, o, t, :], start=True, stop=not inter)
                        if inter:
                            mm = pe.matmul(pret[:, t * P:(t + 1) * P], qdT[:, o, t * P:(t + 1) * P], state[:, o, t, :],
                                           start=False, stop=True)
                    mm.then_inc(ret_made, 1)

                def scores_states(h, q):
                    n, o = h * NQD + q, q % 2
                    pe.wait_ge(k_roped, n + 1)
                    wait(pe, kt_kept, n)
                    for t in range(QUAD):
                        mm = pe.transpose(pkt[:, t * P:(t + 1) * P], kT[:, o, t * P:(t + 1) * P], k.ident[:, :])
                    mm.then_inc(kt_made, 1)
                    pe.wait_ge(q_roped, n + 1)
                    wait(pe, sc_masked, n)
                    for t in range(QUAD):
                        mm = pe.matmul(psc[:, t * P:(t + 1) * P], kT[:, o, t * P:(t + 1) * P], qT[:, o, t * P:(t + 1) * P],
                                       start=True, stop=True)
                    mm.then_inc(sc_made, 1)
                    pe.wait_ge(kt_kept, n + 1)
                    pe.wait_ge(v_kept, n + 1)
                    wait(pe, states, n)
                    for t in range(QUAD):
                        mm = pe.matmul(pds[:, t * P:(t + 1) * P], ktok[:, o, t, :], v[:, o, t, :], start=True, stop=True)
                    mm.then_inc(ds_made, 1)

                def output(h, q):
                    n, o = h * NQD + q, q % 2
                    pe.wait_ge(normed, n + 1)
                    for t in range(QUAD):
                        mm = pe.transpose(pgt[:, t * P:(t + 1) * P], gn[:, t, :], k.ident[:, :])
                    mm.then_inc(gt_made, 1)
                    if q == 0:
                        pe.wait_ge(loaded_wo, 16 * h + 16)
                    pe.wait_ge(gated_ready, n + 1)
                    for c in range(DC):
                        pe.matmul(pout[c][:, :], wo[:, c * P:(c + 1) * P], gated[:, o, :], start=True, stop=True).then_inc(out_made, 1)

                def before(h, q):
                    return (h, q - 1) if q else (h - 1, NQD - 1)

                def step(h, q):
                    n = h * NQD + q
                    project(h, q)
                    first = isinstance(h, int) and n == 0
                    if not first:
                        retain(*before(h, q))
                    scores_states(h, q)
                    if not first:
                        pe.wait_ge(q_kept, n + 1)
                        pe.wait_ge(k_kept, n + 1)
                        pe.wait_ge(silu_kept, n + 1)
                        output(*before(h, q))

                steps(pe, step)
                retain(L1_HEADS - 1, NQD - 1)
                output(L1_HEADS - 1, NQD - 1)

            @block.scalar
            def _(act):
                def step(h, q):
                    n, o = h * NQD + q, q % 2
                    if q == 0:
                        act.wait_ge(loaded_hc, 16 * NHC * (h + 1))
                    act.wait_ge(q_made, n + 1)
                    wait(act, q_rot, n - 1)
                    wait(act, q_cos, n - 1)
                    act.activation(qraw[:, o, :], pq[:, :], ACT.Identity, bias=bias[:, 0:1]).then_inc(q_kept, 1)
                    act.wait_ge(k_made, n + 1)
                    wait(act, k_rot, n - 1)
                    wait(act, k_cos, n - 1)
                    act.activation(kraw[:, o, :], pk[:, :], ACT.Identity, bias=bias[:, 1:2]).then_inc(k_kept, 1)
                    act.wait_ge(g_made, n + 1)
                    wait(act, gated_ready, n - 1)
                    act.activation(sg[:, o, :], pg[:, :], ACT.Silu, bias=bias[:, 2:3]).then_inc(silu_kept, 1)
                    act.wait_ge(kt_made, n + 1)
                    wait(act, ds_made, n - 1)
                    act.activation(ktok[:, o, :, :], pkt[:, :].rearrange("p (t n) -> p t n", t=QUAD), ACT.Copy,
                                   scale=gcol[:, 0:1]).then_inc(kt_kept, 1)

                steps(act, step)

            @block.gpsimd
            def _(pool):
                pool.memset(neghalf[:, :], -0.5).then_inc(half_set, 1)
                pool.wait_ge(loaded_t, 64)
                pool.wait_ge(half_set, 1)

                def invert_std(n):
                    pool.wait_ge(veps_ready, n + 1)
                    wait(pool, normed, n)
                    pool.tensor_tensor(rstd[:, :], veps[:, :], neghalf[:, :], ALU.pow).then_inc(rstd_ready, 1)

                def step(h, q):
                    n, o = h * NQD + q, q % 2
                    b, z, c0 = place(q)
                    tok = slice(z * BANK, (z + 1) * BANK)
                    pool.wait_ge(k_kept, n + 1)
                    pool.tensor_tensor(qc[:, o, :], qraw[:, o, :], cosq[:, tok], ALU.mult).then_inc(q_cos, 1)
                    pool.tensor_tensor(kc[:, o, :], kraw[:, o, :], cosk[:, tok], ALU.mult).then_inc(k_cos, 1)
                    pool.wait_ge(k_rot, n + 1)
                    pool.wait_ge(k_cos, n + 1)
                    wait(pool, sc_made, n - 1)
                    pool.tensor_tensor(kT[:, o, :], kc[:, o, :], ks[:, o, :], ALU.add).then_inc(k_roped, 1)
                    pool.wait_ge(q_rot, n + 1)
                    pool.tensor_tensor(qT[:, o, :], qc[:, o, :], qs[:, o, :], ALU.add).then_inc(q_roped, 1)
                    pool.wait_ge(q_roped, n + 1)
                    wait(pool, ret_made, n - 1)
                    if q == 0:
                        pool.wait_ge(loaded_hc, 16 * NHC * (h + 1))
                    pool.tensor_tensor(qdT[:, o, :].rearrange("p (t n) -> p t n", t=QUAD), qT[:, o, :].rearrange("p (t n) -> p t n", t=QUAD),
                                       grow[:, :].unsqueeze(1).to_broadcast([P, QUAD, P]), ALU.mult).then_inc(q_decayed, 1)
                    if not (isinstance(h, int) and n == 0):
                        invert_std(n - 1)

                steps(pool, step)
                invert_std(L1_HEADS * NQD - 1)

            @block.vector
            def _(dve):
                HALF = P // 2

                def rotate(n, o, z, raw, sin, out, kept, roped, done):
                    tok = slice(z * BANK, (z + 1) * BANK)
                    dve.wait_ge(kept, n + 1)
                    wait(dve, roped, n - 1)
                    dve.tensor_tensor(out[0:HALF, o, :], raw[HALF:P, o, :], sin[HALF:P, tok], ALU.mult)
                    dve.tensor_tensor(out[HALF:P, o, :], raw[0:HALF, o, :], sin[0:HALF, tok], ALU.mult).then_inc(done, 1)

                def measure(n):
                    dve.wait_ge(ret_made, n + 1)
                    for t in range(QUAD):
                        dve.bn_stats(stats[:, t, :], pret[:, t * P:(t + 1) * P]).then_inc(stat1, 1)

                def aggregate(n):
                    for t in range(QUAD):
                        dve.bn_aggr(mv[:, t, :], stats[:, t, :]).then_inc(stat2, 1)
                    dve.wait_ge(stat2, QUAD * n + QUAD)
                    dve.tensor_scalar(veps[:, :], mv[:, :, 1], EPS, None, ALU.add).then_inc(veps_ready, 1)

                def normalise(n):
                    dve.wait_ge(rstd_ready, n + 1)
                    wait(dve, gt_made, n)
                    for t in range(QUAD):
                        op = dve.tensor_scalar(gn[:, t, :], pret[:, t * P:(t + 1) * P], mv[:, t, 0:1], rstd[:, t:t + 1],
                                               ALU.subtract, ALU.mult)
                    op.then_inc(normed, 1)

                def gate_and_add(n, o, c0):
                    dve.wait_ge(gt_made, n + 1)
                    dve.wait_ge(silu_kept, n + 1)
                    wait(dve, out_made, 2 * (n - 1))
                    dve.tensor_tensor(gated[:, o, :], pgt[:, :], sg[:, o, :], ALU.mult).then_inc(gated_ready, 1)
                    for c in range(DC):
                        dve.wait_ge(out_made, 2 * n + c + 1)
                        x = k.XT[:, c, c0:c0 + BANK]
                        dve.tensor_tensor(x, x, pout[c][:, :], ALU.add).then_inc(added, 1)

                def chain(h, q):
                    n, o = h * NQD + q, q % 2
                    b, z, _ = place(q)
                    base = (h * B + b) * (2 * QUAD - 3) + z * (QUAD - 1)
                    dve.wait_ge(ds_made, n + 1)
                    for t in range(QUAD if z + 1 < NZ else QUAD - 1):
                        out = state[:, o, t + 1, :] if t + 1 < QUAD else state[:, 1 - o, 0, :]
                        if t == 0 and z == 0:
                            op = dve.tensor_copy(out, pds[:, 0:P])
                        else:
                            if t:
                                dve.wait_ge(linked, base + t)
                            else:
                                dve.wait_ge(states, n)
                            op = dve.scalar_tensor_tensor(out=out, in0=state[:, o, t, :], scalar=gcol[:, 1:2], in1=pds[:, t * P:(t + 1) * P],
                                                          op0=ALU.mult, op1=ALU.add)
                        last = t == (QUAD - 1 if z + 1 < NZ else QUAD - 2)
                        op.then_inc(states if last else linked, 1)

                def step(h, q):
                    n, o = h * NQD + q, q % 2
                    b, z, c0 = place(q)
                    first = isinstance(h, int) and n == 0
                    rotate(n, o, z, qraw, sinq, qs, q_kept, q_roped, q_rot)
                    rotate(n, o, z, kraw, sink, ks, k_kept, k_roped, k_rot)
                    dve.wait_ge(v_made, n + 1)
                    wait(dve, ret_made, n - 1)
                    if q == 0:
                        dve.wait_ge(loaded_hc, 16 * NHC * (h + 1))
                    dve.tensor_tensor(v[:, o, :, :], pv[:, :].rearrange("p (t n) -> p t n", t=QUAD),
                                      bv[:, :].unsqueeze(1).to_broadcast([P, QUAD, P]), ALU.add).then_inc(v_kept, 1)
                    if not first:
                        measure(n - 1)
                        dve.wait_ge(stat1, QUAD * (n - 1) + QUAD)
                    dve.wait_ge(sc_made, n + 1)
                    dve.tensor_tensor(smT[:, o, :, :], psc[:, :].rearrange("p (t n) -> p t n", t=QUAD),
                                      mask[:, :].unsqueeze(1).to_broadcast([P, QUAD, P]), ALU.mult).then_inc(sc_masked, 1)
                    if not first:
                        aggregate(n - 1)
                    chain(h, q)
                    if not first:
                        normalise(n - 1)
                        gate_and_add(n - 1, 1 - o, place((q - 1) % NQD)[2])

                dve.wait_ge(loaded_t, 64)
                steps(dve, step)
                n = L1_HEADS * NQD - 1
                measure(n)
                dve.wait_ge(stat1, QUAD * n + QUAD)
                aggregate(n)
                normalise(n)
                gate_and_add(n, n % 2, place(NQD - 1)[2])


def l1_constants():
    f = np.float32
    pos = np.arange(S, dtype=f)
    inv_freq = (1.0 / f(10000.0) ** (np.arange(0, L1_HD, 2, dtype=f) / f(L1_HD))).astype(f)
    ang = (inv_freq[:, None] * pos[None, :]).astype(f)
    sbase = ((np.arange(0, L1_HD, 2, dtype=f) + f(0.4 * L1_HD)) / f(1.4 * L1_HD)).astype(f)
    power = ((pos - S // 2) / f(512.0)).astype(f)
    scale = (sbase[:, None] ** power[None, :]).astype(f)
    both = lambda m: np.concatenate([m, m]).astype(f)
    cross = lambda m: np.concatenate([m, -m]).astype(f)
    cos, sin = np.cos(ang), np.sin(ang)
    rope = np.stack([both(cos * scale), cross(sin * scale), both(cos / scale), cross(sin / scale)])
    gamma = 1.0 - 2.0 ** (-5.0 - np.arange(L1_HEADS, dtype=np.float64))
    i = np.arange(P)
    d = i[None, :] - i[:, None]
    mask = np.where(d >= 0, gamma[:, None, None] ** np.maximum(d, 0), 0.0)
    grow = gamma[:, None] ** (i + 1)[None, :]
    gcol = np.stack([gamma[:, None] ** (P - 1 - i)[None, :], np.repeat(gamma[:, None] ** P, P, 1)], axis=2)
    return {"c_l1_rope": rope, "c_l1_mask": mask.astype(f), "c_l1_grow": grow.astype(f), "c_l1_gcol": gcol.astype(f)}


def l1_layout(x):
    order = np.concatenate([np.arange(0, L1_HD, 2), np.arange(1, L1_HD, 2)])
    w = lambda m: m.reshape(DC, P, L1_HEADS, L1_HD).transpose(2, 1, 0, 3)
    w4 = np.stack([w(x["L1_attn_Wq"])[..., order], w(x["L1_attn_Wk"])[..., order], w(x["L1_attn_Wg"]), w(x["L1_attn_Wv"])], axis=2)
    b = lambda v: v.reshape(L1_HEADS, L1_HD)
    bias = np.stack([b(x["L1_attn_bq"])[:, order], b(x["L1_attn_bk"])[:, order], b(x["L1_attn_bg"])], axis=2)
    return {"L1_w4": w4, "L1_bias": bias, "L1_attn_bv": b(x["L1_attn_bv"]), "L1_attn_Wo": x["L1_attn_Wo"]}


def linear(nc, k, name, x, w, scale, bias):
    with Stage(nc, name) as st:
        acc = [st.ps(f"acc{i}") for i in range(4)]
        out = st.sb("out", [P, 2, BANK])
        made, scaled, added = st.sem("made"), st.sem("scaled"), st.sem("added")
        jobs = [(j, c) for j in range(NJ) for c in range(DC)]
        with nc.Block() as block:

            @block.tensor
            def _(pe):
                for n, (j, c) in enumerate(jobs):
                    wait(pe, scaled, n - 3)
                    for i in range(DC):
                        mm = pe.matmul(acc[n % 4][:, :], w[:, i, c * P:(c + 1) * P], x[:, i, j * BANK:(j + 1) * BANK],
                                       start=(i == 0), stop=(i == DC - 1))
                    mm.then_inc(made, 1)

            @block.scalar
            def _(act):
                for n, (j, c) in enumerate(jobs):
                    act.wait_ge(made, n + 1)
                    wait(act, added, n - 1)
                    act.activation(out[:, n % 2, :], acc[n % 4][:, :], ACT.Identity, bias=bias[:, c:c + 1],
                                   scale=scale[:, c:c + 1]).then_inc(scaled, 1)

            @block.vector
            def _(dve):
                for n, (j, c) in enumerate(jobs):
                    dve.wait_ge(scaled, n + 1)
                    t = k.XT[:, c, j * BANK:(j + 1) * BANK]
                    dve.tensor_tensor(t, t, out[:, n % 2, :], ALU.add).then_inc(added, 1)


def l1_ffn(nc, k, a):
    with Stage(nc, "l1f") as st:
        X2 = st.sb("X2", [P, DC, T])
        w = st.sb("w", [P, DC, D])
        sgn = st.sb("sgn", [P, 2, DC, D])
        v = st.sb("v", [P, 6, DC])
        top = st.sb("top", [P, 4])
        norm_stage(nc, k, "l1n", k.XN, X2)
        with Stage(nc, "l1p") as s2:
            loaded, tops, alltop, signs, done = s2.sem("loaded"), s2.sem("tops"), s2.sem("alltop"), s2.sem("signs"), s2.sem("done")
            with nc.Block() as block:

                @block.sync
                def _(sp):
                    sp.dma_start(w[:, :, :], rows(a["L1_ffn_weightT"])).then_inc(loaded, 16)
                    sp.dma_start(v[:, 0:5, :], a["L1_ffn_cols"]).then_inc(loaded, 16)

                @block.vector
                def _(dve):
                    dve.wait_ge(loaded, 32)
                    dve.tensor_reduce(top[:, 0:1], w[:, :, :], mybir.AxisListType.XY, ALU.max).then_inc(tops, 1)
                    dve.tensor_reduce(top[:, 1:2], w[:, :, :], mybir.AxisListType.XY, ALU.min).then_inc(tops, 1)
                    dve.tensor_scalar(sgn[:, 0, :, :], w[:, :, :], 0.0, None, ALU.is_gt).then_inc(signs, 1)
                    dve.tensor_scalar(sgn[:, 1, :, :], w[:, :, :], 0.0, None, ALU.is_lt).then_inc(signs, 1)
                    dve.tensor_tensor(v[:, 1, :], v[:, 1, :], v[:, 4, :], ALU.add)
                    dve.wait_ge(tops, 2)
                    dve.scalar_tensor_tensor(out=top[:, 2:3], in0=top[:, 1:2], scalar=-1.0, in1=top[:, 0:1],
                                             op0=ALU.mult, op1=ALU.max).then_inc(tops, 1)
                    dve.wait_ge(signs, 2)
                    dve.tensor_tensor(sgn[:, 0, :, :], sgn[:, 0, :, :], sgn[:, 1, :, :], ALU.subtract)
                    for c in range(DC):
                        dve.tensor_scalar(X2[:, c, :], X2[:, c, :], v[:, 2, c:c + 1], v[:, 3, c:c + 1], ALU.mult, ALU.add)
                    dve.wait_ge(alltop, 1)
                    dve.tensor_scalar(v[:, 0, :], v[:, 0, :], top[:, 3:4], None, ALU.mult)

                @block.gpsimd
                def _(pool):
                    pool.wait_ge(tops, 3)
                    pool.partition_all_reduce(top[:, 3:4], top[:, 2:3], P, bass.bass_isa.ReduceOp.max).then_inc(alltop, 1)

        linear(nc, k, "l1l", X2, sgn[:, 0, :, :], v[:, 0, :], v[:, 1, :])


def l2_ffn(nc, k, a):
    with Stage(nc, "l2f") as st:
        w = st.sb("w", [P, DC, D])
        t = st.sb("t", [P, 2, DC, D])
        sc = st.sb("sc", [P, DC])
        bias = st.sb("bias", [P, DC])
        with Stage(nc, "l2p") as s2:
            pa = s2.ps("pa")
            loaded, absd, mean_made, steps = s2.sem("loaded"), s2.sem("absd"), s2.sem("mean_made"), s2.sem("steps")
            with nc.Block() as block:

                @block.sync
                def _(sp):
                    sp.dma_start(w[:, :, :], rows(a["L2_ffn_weightT"])).then_inc(loaded, 16)
                    sp.dma_start(bias[:, :], a["L2_ffn_bias_cols"]).then_inc(loaded, 16)

                @block.tensor
                def _(pe):
                    pe.wait_ge(absd, 1)
                    for c in range(DC):
                        mm = pe.matmul(pa[:, 0:D], k.avg[:, :], t[:, 0, c, :], start=(c == 0), stop=(c == DC - 1))
                    mm.then_inc(mean_made, 1)

                @block.vector
                def _(dve):
                    dve.memset(sc[:, :], 1.0)
                    dve.wait_ge(loaded, 32)
                    dve.scalar_tensor_tensor(out=t[:, 0, :, :], in0=w[:, :, :], scalar=-1.0, in1=w[:, :, :],
                                             op0=ALU.mult, op1=ALU.max).then_inc(absd, 1)
                    dve.tensor_scalar(t[:, 1, :, :], w[:, :, :], 0.0, None, ALU.is_ge).then_inc(steps, 1)
                    dve.wait_ge(steps, 1)
                    dve.tensor_scalar(t[:, 1, :, :], t[:, 1, :, :], 2.0, -1.0, ALU.mult, ALU.add).then_inc(steps, 1)
                    dve.wait_ge(steps, 2)
                    dve.wait_ge(mean_made, 1)
                    for c in range(DC):
                        dve.tensor_tensor(t[:, 1, c, :], t[:, 1, c, :], pa[:, 0:D], ALU.mult).then_inc(steps, 1)
                    dve.wait_ge(steps, 4)
                    dve.tensor_tensor(t[:, 1, :, :], t[:, 1, :, :], w[:, :, :], ALU.subtract).then_inc(steps, 1)
                    dve.wait_ge(steps, 5)
                    dve.tensor_tensor(t[:, 1, :, :], t[:, 1, :, :], w[:, :, :], ALU.add)

        linear(nc, k, "l2l", k.XN, t[:, 1, :, :], sc, bias)


F32R = mybir.dt.float32r
L2_HEADS, L2_HD = 16, 16
L2_W = L2_HD + 1
L2_HPC = P // L2_HD
L2_SCALE = L2_HD ** -0.5
SPLIT = 4 * L2_HD
L2_N = L2_HEADS * B


def l2_attn(nc, k, a):
    split = nc.dram_tensor("l2_split", [2, 2, D, T], F32, kind="Internal").ap()
    with Stage(nc, "l2a") as st:
        VA = st.sb("VA", [P, TT, L2_HEADS, L2_W])
        mem = st.sb("mem", [P, DC, T])
        gate = st.sb("gate", [P, 2, DC])
        with Stage(nc, "l2q") as s2:
            QF = s2.sb("QF", [P, DC, T])
            KF = s2.sb("KF", [P, DC, T])
            l2_project(nc, k, a, split, VA, QF, KF)
            l2_memory(nc, k, a, VA, QF, KF, mem, gate)
        CT = st.sb("CT", [P, TT, D])
        l2_heads(nc, k, split, VA, CT)
        l2_output(nc, k, a, CT, mem, gate)


def l2_project(nc, k, a, split, VA, QF, KF):
    with Stage(nc, "l2p") as st:
        w = st.sb("w", [P, 3, DC, D])
        cos, sin = st.sb("cos", [P, S]), st.sb("sin", [P, S])
        xc, xs = st.sb("xc", [P, DC, BANK]), st.sb("xs", [P, DC, BANK])
        rot = st.sb("rot", [P, DC, BANK])
        hi, lo = st.sb("hi", [P, 2, DC, BANK], F32R), st.sb("lo", [P, 2, DC, BANK], F32R)
        low, ex = st.sb("low", [P, DC, BANK]), st.sb("ex", [P, DC, BANK])
        acc = [st.ps(f"acc{i}") for i in range(4)]
        vacc = [st.ps(f"vacc{i}") for i in range(2)]
        loaded, made, turned, roped = st.sem("loaded"), st.sem("made"), st.sem("turned"), st.sem("roped")
        hi_ready, lo_ready = st.sem("hi_ready"), st.sem("lo_ready")
        hi_stored, lo_stored = [st.sem(f"hi_stored{i}") for i in range(2)], [st.sem(f"lo_stored{i}") for i in range(2)]
        low_ready, ex_ready, feat = st.sem("low_ready"), st.sem("ex_ready"), st.sem("feat")
        v_made, v_kept, ones_set = st.sem("v_made"), st.sem("v_kept"), st.sem("ones_set")
        jobs = [(m, j) for j in range(NJ) for m in range(2)]

        with nc.Block() as block:

            @block.sync
            def _(sp):
                sp.dma_start(w[:, :, :, :], a["L2_w3"]).then_inc(loaded, 16)
                sp.dma_start(cos[:, :], a["c_l2_rope"][0]).then_inc(loaded, 16)
                sp.dma_start(sin[:, :], a["c_l2_rope"][1]).then_inc(loaded, 16)
                for n, (m, j) in enumerate(jobs):
                    tok = slice(j * BANK, (j + 1) * BANK)
                    sp.wait_ge(hi_ready, n + 1)
                    sp.dma_start(rows(split[m, 0])[:, :, tok], hi[:, n % 2, :, :].bitcast(F32)).then_inc(hi_stored[n % 2], 16)
                    sp.wait_ge(lo_ready, n + 1)
                    sp.dma_start(rows(split[m, 1])[:, :, tok], lo[:, n % 2, :, :].bitcast(F32)).then_inc(lo_stored[n % 2], 16)
                for sem in hi_stored + lo_stored:
                    sp.wait_ge(sem, 16 * (len(jobs) // 2))

            @block.tensor
            def _(pe):
                pe.wait_ge(loaded, 48)
                for n, (m, j) in enumerate(jobs):
                    wait(pe, turned, n - 1)
                    for o in range(DC):
                        for c in range(DC):
                            mm = pe.matmul(acc[n % 2 * 2 + o][:, :], w[:, m, c, o * P:(o + 1) * P], k.XN[:, c, j * BANK:(j + 1) * BANK],
                                           start=(c == 0), stop=(c == DC - 1))
                    mm.then_inc(made, 1)
                    for t in (2 * n, 2 * n + 1):
                        wait(pe, v_kept, t - 1)
                        for c in range(DC):
                            mm = pe.matmul(vacc[t % 2][:, 0:D], k.XN[:, c, t * P:(t + 1) * P], w[:, 2, c, :],
                                           start=(c == 0), stop=(c == DC - 1))
                        mm.then_inc(v_made, 1)

            @block.vector
            def _(dve):
                dve.wait_ge(loaded, 48)
                for n, (m, j) in enumerate(jobs):
                    A, Bk = acc[n % 2 * 2], acc[n % 2 * 2 + 1]
                    f = (QF, KF)[m]
                    tok, pos = slice(j * BANK, (j + 1) * BANK), slice(j * BANK % S, j * BANK % S + BANK)
                    dve.wait_ge(made, n + 1)
                    wait(dve, roped, n)
                    dve.tensor_tensor(xc[:, 0, :], A[:, :], cos[:, pos], ALU.mult)
                    dve.tensor_tensor(xc[:, 1, :], Bk[:, :], cos[:, pos], ALU.mult)
                    dve.tensor_tensor(xs[:, 0, :], Bk[:, :], sin[:, pos], ALU.mult)
                    dve.tensor_tensor(xs[:, 1, :], A[:, :], sin[:, pos], ALU.mult).then_inc(turned, 1)
                    dve.wait_ge(hi_ready, n + 1)
                    wait(dve, lo_stored[n % 2], 16 * (n // 2))
                    dve.tensor_tensor(lo[:, n % 2, :, :], rot[:, :, :], hi[:, n % 2, :, :].bitcast(F32), ALU.subtract).then_inc(lo_ready, 1)
                    wait(dve, ex_ready, n)
                    dve.tensor_scalar(low[:, :, :], rot[:, :, :], 0.0, None, ALU.min).then_inc(low_ready, 1)
                    dve.wait_ge(ex_ready, n + 1)
                    dve.scalar_tensor_tensor(out=f[:, :, tok], in0=rot[:, :, :], scalar=0.0, in1=ex[:, :, :],
                                             op0=ALU.max, op1=ALU.add).then_inc(feat, 1)

            @block.gpsimd
            def _(pool):
                pool.memset(VA[:, :, :, L2_HD:L2_W], 1.0)
                for n, (m, j) in enumerate(jobs):
                    pool.wait_ge(turned, n + 1)
                    wait(pool, feat, n)
                    wait(pool, hi_ready, n)
                    pool.tensor_tensor(rot[:, 0, :], xc[:, 0, :], xs[:, 0, :], ALU.subtract)
                    pool.tensor_tensor(rot[:, 1, :], xc[:, 1, :], xs[:, 1, :], ALU.add).then_inc(roped, 1)

            @block.scalar
            def _(act):
                for n, (m, j) in enumerate(jobs):
                    for t in (2 * n, 2 * n + 1):
                        act.wait_ge(v_made, t + 1)
                        act.activation(VA[:, t, :, 0:L2_HD], vacc[t % 2][:, 0:D].rearrange("p (h e) -> p h e", h=L2_HEADS),
                                       ACT.Copy).then_inc(v_kept, 1)
                    act.wait_ge(roped, n + 1)
                    wait(act, hi_stored[n % 2], 16 * (n // 2))
                    act.activation(hi[:, n % 2, :, :], rot[:, :, :], ACT.Copy).then_inc(hi_ready, 1)
                    act.wait_ge(low_ready, n + 1)
                    wait(act, feat, n)
                    act.activation(ex[:, :, :], low[:, :, :], ACT.Exp).then_inc(ex_ready, 1)


def l2_memory(nc, k, a, VA, QF, KF, mem, gate):
    with Stage(nc, "l2m") as st:
        blk = st.sb("blk", [P, P])
        ones = st.sb("ones", [P, P])
        ktok = st.sb("ktok", [P, 2, BANK])
        M, N = st.sb("M", [P, 2, P]), st.sb("N", [P, 2, P])
        raw = st.sb("raw", [P, DC])
        inv = st.sb("inv", [P, 2, BANK])
        ptr = [st.ps(f"ptr{i}") for i in range(2)]
        pm, pn = st.ps("pm"), st.ps("pn")
        num, den = [st.ps(f"num{i}") for i in range(2)], [st.ps(f"den{i}") for i in range(2)]
        loaded, set_up, turned, kept = st.sem("loaded"), st.sem("set_up"), st.sem("turned"), st.sem("kept")
        summed, masked, out_made, inv_ready, used, gates = st.sem("summed"), st.sem("masked"), st.sem("out_made"), st.sem("inv_ready"), st.sem("used"), st.sem("gates")
        jobs = [(b, c) for b in range(B) for c in range(DC)]
        QT_ = NQ // 4

        with nc.Block() as block:

            @block.sync
            def _(sp):
                sp.dma_start(blk[:, :], a["c_l2_block"]).then_inc(loaded, 16)
                sp.dma_start(raw[:, :], a["L2_gate_cols"]).then_inc(loaded, 16)

            @block.scalar
            def _(act):
                act.wait_ge(loaded, 32)
                act.activation(gate[:, 0, :], raw[:, :], ACT.Sigmoid).then_inc(gates, 1)
                for n in range(len(jobs) * QT_):
                    act.wait_ge(turned, n + 1)
                    wait(act, summed, n - 1)
                    act.activation(ktok[:, n % 2, :], ptr[n % 2][:, :], ACT.Copy).then_inc(kept, 1)

            @block.tensor
            def _(pe):
                def outputs(n):
                    b, c = jobs[n]
                    pe.wait_ge(masked, n + 1)
                    for z in range(NZ):
                        i = n * NZ + z
                        wait(pe, used, i - 1)
                        f = QF[:, c, b * S + z * BANK:b * S + (z + 1) * BANK]
                        pe.matmul(num[i % 2][:, :], M[:, n % 2, :], f, start=True, stop=True)
                        pe.matmul(den[i % 2][:, :], N[:, n % 2, :], f, start=True, stop=True).then_inc(out_made, 1)

                pe.wait_ge(set_up, 1)
                for n, (b, c) in enumerate(jobs):
                    for g in range(QT_):
                        i = n * QT_ + g
                        wait(pe, kept, i - 1)
                        for t in range(4):
                            lo = b * S + (g * 4 + t) * P
                            mm = pe.transpose(ptr[i % 2][:, t * P:(t + 1) * P], KF[:, c, lo:lo + P], k.ident[:, :])
                        mm.then_inc(turned, 1)
                    if n:
                        outputs(n - 1)
                    wait(pe, masked, n)
                    for g in range(QT_):
                        i = n * QT_ + g
                        pe.wait_ge(kept, i + 1)
                        for t in range(4):
                            kt = ktok[:, i % 2, t * P:(t + 1) * P]
                            first, last = g == 0 and t == 0, g == QT_ - 1 and t == 3
                            pe.matmul(pm[:, 0:P], kt, VA[:, b * NQ + g * 4 + t, c * L2_HPC:(c + 1) * L2_HPC, 0:L2_HD], start=first, stop=last)
                            mm = pe.matmul(pn[:, 0:P], kt, ones[:, :], start=first, stop=last)
                        mm.then_inc(summed, 1)
                outputs(len(jobs) - 1)

            @block.vector
            def _(dve):
                dve.memset(ones[:, :], 1.0).then_inc(set_up, 1)
                dve.wait_ge(gates, 1)
                dve.tensor_scalar(gate[:, 1, :], gate[:, 0, :], -1.0, 1.0, ALU.mult, ALU.add)

                def divide(n):
                    b, c = jobs[n]
                    for z in range(NZ):
                        i = n * NZ + z
                        dve.wait_ge(out_made, i + 1)
                        dve.reciprocal(inv[:, i % 2, :], den[i % 2][:, :]).then_inc(inv_ready, 1)
                        dve.wait_ge(inv_ready, i + 1)
                        dve.scalar_tensor_tensor(out=mem[:, c, b * S + z * BANK:b * S + (z + 1) * BANK], in0=num[i % 2][:, :],
                                                 scalar=gate[:, 0, c:c + 1], in1=inv[:, i % 2, :], op0=ALU.mult, op1=ALU.mult).then_inc(used, 1)

                for n in range(len(jobs)):
                    dve.wait_ge(summed, (n + 1) * QT_)
                    wait(dve, out_made, (n - 1) * NZ)
                    dve.tensor_tensor(M[:, n % 2, :], pm[:, 0:P], blk[:, :], ALU.mult)
                    dve.tensor_tensor(N[:, n % 2, :], pn[:, 0:P], blk[:, :], ALU.mult).then_inc(masked, 1)
                    if n:
                        divide(n - 1)
                divide(len(jobs) - 1)


def l2_heads(nc, k, split, VA, CT):
    with Stage(nc, "l2h") as st:
        Q1, K1 = st.sb("Q1", [P, S], F32R), st.sb("K1", [P, S], F32R)
        Q2, K2 = st.sb("Q2", [P, 2, S], F32R), st.sb("K2", [P, 2, S], F32R)
        PT = st.sb("PT", [P, 2, NQ, S])
        half = st.sb("half", [P, 2, NQ, 2])
        top = st.sb("top", [P, 2, NQ])
        mhi, mlo = st.sb("mhi", [NQ, 2, P], F32R), st.sb("mlo", [NQ, 2, P], F32R)
        inv = st.sb("inv", [P, NQ])
        s1 = [st.ps(f"s1_{i}") for i in range(2)]
        s2 = [st.ps(f"s2_{i}", 2 * BANK) for i in range(2)]
        pmt, pv = st.ps("pmt"), st.ps("pv")
        filled, q1_loaded = st.sem("filled"), st.sem("q1_loaded")
        q2_loaded, m_loaded = [st.sem(f"q2_loaded{i}") for i in range(B)], [st.sem(f"m_loaded{i}") for i in range(B)]
        s1_made, maxed, top_ready, top_turned = st.sem("s1_made"), st.sem("maxed"), st.sem("top_ready"), st.sem("top_turned")
        mhi_ready, m_ready, s2_made, exped = st.sem("mhi_ready"), st.sem("m_ready"), st.sem("s2_made"), st.sem("exped")
        pv_made, inv_ready, ctx_kept = st.sem("pv_made"), st.sem("inv_ready"), st.sem("ctx_kept")
        NP = 2 * NQ
        MROW = SPLIT

        def steps(engine, step):
            for b in range(B):
                step(0, b)
            with engine.Fori(1, L2_HEADS - 1) as h:
                for b in range(B):
                    step(h, b)
            for b in range(B):
                step(L2_HEADS - 1, b)

        def after(h, b):
            return (h, b + 1) if b + 1 < B else (h + 1, 0)

        def before(h, b):
            return (h, b - 1) if b else (h - 1, B - 1)

        def is_first(h, b):
            return isinstance(h, int) and h == 0 and b == 0

        def is_last(h, b):
            return isinstance(h, int) and h == L2_HEADS - 1 and b == B - 1

        with nc.Block() as block:

            @block.sync
            def _(sp):
                def q_rows(h, b):
                    return split[0][:, ds(h * L2_HD, L2_HD), b * S:(b + 1) * S]

                def k_rows(h, b):
                    return split[1][:, ds(h * L2_HD, L2_HD), b * S:(b + 1) * S]

                def load(Q, K, h, b, sem):
                    for part in range(2):
                        for rep in range(2):
                            sp.dma_start(Q[(2 * part + rep) * L2_HD:(2 * part + rep + 1) * L2_HD, :].bitcast(F32), q_rows(h, b)[part]).then_inc(sem, 16)
                            sp.dma_start(K[(2 * rep + part) * L2_HD:(2 * rep + part + 1) * L2_HD, :].bitcast(F32), k_rows(h, b)[part]).then_inc(sem, 16)

                def load_max(h, b):
                    n = B * h + b
                    sp.wait_ge(m_ready, n + 1)
                    wait(sp, s2_made, NQ * (n - 1))
                    for i, m in enumerate((mhi, mlo)):
                        sp.dma_start(Q2[MROW + i:MROW + i + 1, b, :].bitcast(F32).rearrange("a (t n) -> a t n", t=NQ), m[:, b, :].bitcast(F32)).then_inc(m_loaded[b], 16)

                sp.wait_ge(filled, 5)
                load(Q1, K1, 0, 0, q1_loaded)
                load(Q2[:, 0, :], K2[:, 0, :], 0, 0, q2_loaded[0])
                load_max(0, 0)

                def step(h, b):
                    n = B * h + b
                    if not is_last(h, b):
                        h1, b1 = after(h, b)
                        sp.wait_ge(s1_made, NP * (n + 1))
                        load(Q1, K1, h1, b1, q1_loaded)
                        wait(sp, s2_made, NQ * n)
                        load(Q2[:, b1, :], K2[:, b1, :], h1, b1, q2_loaded[b1])
                        load_max(h1, b1)

                steps(sp, step)

            @block.gpsimd
            def _(pool):
                for m in (Q1[SPLIT:P, :], K1[SPLIT:P, :], Q2[SPLIT:P, :, :], K2[SPLIT:P, :, :]):
                    pool.memset(m.bitcast(F32), 0.0).then_inc(filled, 1)
                pool.wait_ge(filled, 4)
                pool.memset(K2[MROW:MROW + 2, :, :].bitcast(F32), -1.0).then_inc(filled, 1)

            @block.tensor
            def _(pe):
                def first_pass(h, b, pieces):
                    n = B * h + b
                    for i in pieces:
                        t, z = divmod(i, 2)
                        if i == 0:
                            pe.wait_ge(q1_loaded, 128 * (n + 1))
                        wait(pe, maxed, NP * n + i - 1)
                        pe.matmul(s1[i % 2][:, :], Q1[:, t * P:(t + 1) * P], K1[:, z * BANK:(z + 1) * BANK],
                                  start=True, stop=True).then_inc(s1_made, 1)

                def turn_max(h, b):
                    n = B * h + b
                    pe.wait_ge(top_ready, n + 1)
                    wait(pe, m_ready, n)
                    pe.transpose(pmt[0:NQ, 0:P], top[:, b, :], k.ident[:, :]).then_inc(top_turned, 1)

                def second_pass(h, b, kb):
                    n = B * h + b
                    if kb == 0:
                        pe.wait_ge(q2_loaded[b], 128 * h + 128)
                        pe.wait_ge(m_loaded[b], 32 * h + 32)
                    wait(pe, exped, NQ * n + kb - 1)
                    for z in range(NZ):
                        mm = pe.matmul(s2[kb % 2][:, z * BANK:(z + 1) * BANK], K2[:, b, kb * P:(kb + 1) * P],
                                       Q2[:, b, z * BANK:(z + 1) * BANK], start=True, stop=True)
                    mm.then_inc(s2_made, 1)

                def values(h, b, t):
                    n = B * h + b
                    if t == 0:
                        pe.wait_ge(exped, NQ * (n + 1))
                        wait(pe, ctx_kept, n)
                    for kb in range(NQ):
                        mm = pe.matmul(pv[:, t * 32:t * 32 + L2_W], PT[:, b, kb, t * P:(t + 1) * P], VA[:, b * NQ + kb, ds(h, 1), :],
                                       start=(kb == 0), stop=(kb == NQ - 1))
                    if t == NQ - 1:
                        mm.then_inc(pv_made, 1)

                first_pass(0, 0, range(NP))
                turn_max(0, 0)

                def step(h, b):
                    for kb in range(NQ):
                        second_pass(h, b, kb)
                        if not is_last(h, b):
                            first_pass(*after(h, b), range(min(3 * kb, NP), min(3 * kb + 3, NP)))
                            if kb == 6:
                                turn_max(*after(h, b))
                        if not is_first(h, b):
                            values(*before(h, b), kb)

                steps(pe, step)
                for t in range(NQ):
                    values(L2_HEADS - 1, B - 1, t)

            @block.scalar
            def _(act):
                def step(h, b):
                    n = B * h + b
                    for kb in range(NQ):
                        act.wait_ge(s2_made, NQ * n + kb + 1)
                        act.activation(PT[:, b, kb, :], s2[kb % 2][:, :], ACT.Exp, scale=L2_SCALE).then_inc(exped, 1)

                steps(act, step)

            @block.vector
            def _(dve):
                def maxima(h, b):
                    n = B * h + b
                    for i in range(NP):
                        t, z = divmod(i, 2)
                        dve.wait_ge(s1_made, NP * n + i + 1)
                        dve.reduce_max(half[:, b, t, z:z + 1], s1[i % 2][:, :], AX_X).then_inc(maxed, 1)
                    dve.wait_ge(maxed, NP * (n + 1))
                    dve.reduce_max(top[:, b, :], half[:, b, :, :], AX_X).then_inc(top_ready, 1)
                    dve.wait_ge(top_turned, n + 1)
                    wait(dve, m_loaded[b], 32 * h)
                    dve.tensor_copy(mhi[:, b, :], pmt[0:NQ, 0:P]).then_inc(mhi_ready, 1)
                    dve.wait_ge(mhi_ready, n + 1)
                    dve.tensor_tensor(mlo[:, b, :], pmt[0:NQ, 0:P], mhi[:, b, :].bitcast(F32), ALU.subtract).then_inc(m_ready, 1)

                def normalise(h, b):
                    n = B * h + b
                    out = pv[:, 0:NQ * 32].rearrange("p (t e) -> p t e", e=32)
                    dve.wait_ge(pv_made, n + 1)
                    dve.reciprocal(inv[:, :], out[:, :, L2_HD]).then_inc(inv_ready, 1)
                    dve.wait_ge(inv_ready, n + 1)
                    dve.tensor_tensor(CT[:, b * NQ:(b + 1) * NQ, ds(h * L2_HD, L2_HD)], out[:, :, 0:L2_HD],
                                      inv[:, :].unsqueeze(2).to_broadcast([P, NQ, L2_HD]), ALU.mult).then_inc(ctx_kept, 1)

                maxima(0, 0)

                def step(h, b):
                    if not is_last(h, b):
                        maxima(*after(h, b))
                    if not is_first(h, b):
                        normalise(*before(h, b))

                steps(dve, step)
                normalise(L2_HEADS - 1, B - 1)


def l2_output(nc, k, a, CT, mem, gate):
    with Stage(nc, "l2o") as st:
        wo = st.sb("wo", [P, DC, D])
        comb = st.sb("comb", [P, 2, DC, BANK])
        ptr = [st.ps(f"ptr{i}") for i in range(4)]
        out = [st.ps(f"out{i}") for i in range(4)]
        loaded, turned, combined, made, added = st.sem("loaded"), st.sem("turned"), st.sem("combined"), st.sem("made"), st.sem("added")

        with nc.Block() as block:

            @block.sync
            def _(sp):
                sp.dma_start(wo[:, :, :], rows(a["L2_attn_WoT"])).then_inc(loaded, 16)

            @block.tensor
            def _(pe):
                def turn(j):
                    wait(pe, combined, DC * (j - 1))
                    for c in range(DC):
                        for t in range(4):
                            mm = pe.transpose(ptr[j % 2 * 2 + c][:, t * P:(t + 1) * P], CT[:, 4 * j + t, c * P:(c + 1) * P], k.ident[:, :])
                        mm.then_inc(turned, 1)

                turn(0)
                pe.wait_ge(loaded, 16)
                for j in range(NJ):
                    if j + 1 < NJ:
                        turn(j + 1)
                    pe.wait_ge(combined, DC * (j + 1))
                    wait(pe, added, DC * (j - 1))
                    for o in range(DC):
                        for c in range(DC):
                            mm = pe.matmul(out[j % 2 * 2 + o][:, :], wo[:, c, o * P:(o + 1) * P], comb[:, j % 2, c, :], start=(c == 0), stop=(c == DC - 1))
                        mm.then_inc(made, 1)

            @block.vector
            def _(dve):
                def combine(j):
                    wait(dve, made, DC * (j - 1))
                    for c in range(DC):
                        dve.wait_ge(turned, DC * j + c + 1)
                        dve.scalar_tensor_tensor(out=comb[:, j % 2, c, :], in0=ptr[j % 2 * 2 + c][:, :], scalar=gate[:, 1, c:c + 1],
                                                 in1=mem[:, c, j * BANK:(j + 1) * BANK], op0=ALU.mult, op1=ALU.add).then_inc(combined, 1)

                combine(0)
                for j in range(NJ):
                    if j + 1 < NJ:
                        combine(j + 1)
                    for o in range(DC):
                        dve.wait_ge(made, DC * j + o + 1)
                        x = k.XT[:, o, j * BANK:(j + 1) * BANK]
                        dve.tensor_tensor(x, x, out[j % 2 * 2 + o][:, :], ALU.add).then_inc(added, 1)


def l2_constants():
    f = np.float32
    inv_freq = (1.0 / f(10000.0) ** (np.arange(0, D, 2, dtype=f) / f(D))).astype(f)
    ang = (inv_freq[:, None] * np.arange(S, dtype=f)[None, :]).astype(f)
    i = np.arange(P) // L2_HD
    return {"c_l2_rope": np.stack([np.cos(ang), np.sin(ang)]).astype(f), "c_l2_block": (i[:, None] == i[None, :]).astype(f)}


def l2_layout(x):
    w = lambda m: m.T.reshape(DC, P, D).transpose(1, 0, 2)
    return {"L2_w3": np.stack([w(x["L2_attn_Wq"]), w(x["L2_attn_Wk"]), w(x["L2_attn_Wv"])], axis=1), "L2_attn_WoT": x["L2_attn_Wo"].T,
            "L2_gate_cols": np.repeat(x["L2_attn_gate"].reshape(-1), L2_HD).reshape(DC, P).T}


L3_HEADS, L3_HD = 32, 64
L3_INNER = L3_HEADS * L3_HD
L3_PAIRS = L3_HEADS // 2
NCH = T // P


def l3_attn(nc, k, a):
    decays = nc.dram_tensor("l3_decays", [2, L3_HEADS, T], F32, kind="Internal").ap()
    l3_decays(nc, k, a, decays)
    for b in range(B):
        with Stage(nc, f"l3a{b}") as st:
            Y = st.sb("Y", [P, L3_PAIRS, S])
            l3_pairs(nc, k, a, decays, b, Y)
            l3_output(nc, k, a, b, Y)
        if b + 1 < B:
            clear_semaphores(nc)


def l3_decays(nc, k, a, decays):
    with Stage(nc, "l3d") as st:
        H = L3_HEADS
        w = st.sb("w", [P, DC, H])
        ex = st.sb("ex", [H, 2, BANK])
        dec = st.sb("dec", [H, T])
        run = st.sb("run", [H, T])
        zero = st.sb("zero", [H, P])
        acc = [st.ps(f"acc{i}") for i in range(2)]
        loaded, made, exped, decayed, prods, stored = st.sem("loaded"), st.sem("made"), st.sem("exped"), st.sem("decayed"), st.sem("prods"), st.sem("stored")
        zeroed = st.sem("zeroed")
        with nc.Block() as block:

            @block.sync
            def _(sp):
                sp.dma_start(w[:, :, :], rows(a["L3_wa"])).then_inc(loaded, 16)
                sp.wait_ge(prods, NCH)
                sp.dma_start(decays[1], run[:, :]).then_inc(stored, 16)
                sp.wait_ge(zeroed, 2)
                sp.dma_start(decays[0], dec[:, :]).then_inc(stored, 16)
                sp.wait_ge(stored, 32)

            @block.tensor
            def _(pe):
                pe.wait_ge(loaded, 16)
                for j in range(NJ):
                    wait(pe, exped, j - 1)
                    for c in range(DC):
                        mm = pe.matmul(acc[j % 2][0:H, :], w[:, c, :], k.XN[:, c, j * BANK:(j + 1) * BANK], start=(c == 0), stop=(c == DC - 1))
                    mm.then_inc(made, 1)

            @block.scalar
            def _(act):
                for j in range(NJ):
                    act.wait_ge(made, j + 1)
                    act.activation(ex[:, j % 2, :], acc[j % 2][0:H, :], ACT.Exp).then_inc(exped, 1)
                    act.wait_ge(exped, j + 1)
                    act.activation(dec[:, j * BANK:(j + 1) * BANK], ex[:, j % 2, :], ACT.Exp, scale=-1.0).then_inc(decayed, 1)

            @block.vector
            def _(dve):
                dve.memset(zero[:, :], 0.0).then_inc(zeroed, 1)
                dve.wait_ge(zeroed, 1)
                for i in range(NCH):
                    if i % 4 == 0:
                        dve.wait_ge(decayed, i // 4 + 1)
                    t = slice(i * P, (i + 1) * P)
                    dve.tensor_tensor_scan(run[:, t], dec[:, t], zero[:, :], 1.0, ALU.mult, ALU.add).then_inc(prods, 1)
                dve.wait_ge(prods, NCH)
                dve.memset(dec[:, :].rearrange("h (i n) -> h i n", n=P)[:, :, 0:1], 0.0).then_inc(zeroed, 1)


def l3_pairs(nc, k, a, decays, b, Y):
    with Stage(nc, f"l3p{b}") as st:
        w4 = st.sb("w4", [P, 4, DC, P])
        dcol = st.sb("dcol", [P, 1])
        eye4 = st.sb("eye4", [P, BANK])
        blk = st.sb("blk", [P, P])
        decb = st.sb("decb", [P, 2, 2, BANK])
        prow = st.sb("prow", [P, 2, BANK])
        xT, bT = st.sb("xT", [P, 2, BANK]), st.sb("bT", [P, BANK])
        cT2 = st.sb("cT2", [P, 2, BANK])
        cdT = st.sb("cdT", [P, 2, BANK])
        sz = st.sb("sz", [P, 2, BANK])
        xtok = st.sb("xtok", [P, 2, QUAD, P])
        btok = st.sb("btok", [P, QUAD, P])
        table = st.sb("table", [P, 2, BANK])
        mixT = st.sb("mixT", [P, 2, 2, BANK])
        dsm = st.sb("dsm", [P, QUAD, P])
        state = st.sb("state", [P, 2, QUAD, P])
        skip = st.sb("skip", [P, BANK])
        px, pb, pc, pz, pds, py = (st.ps(n) for n in ("px", "pb", "pc", "pz", "pds", "py"))
        psc = st.ps("psc", 2 * BANK)
        loaded_w4, loaded_c, loaded_d, consts, zeroed = st.sem("loaded_w4"), st.sem("loaded_c"), [st.sem(f"loaded_d{i}") for i in range(2)], st.sem("consts"), st.sem("zeroed")
        x_made, b_made, c_made, z_made = st.sem("x_made"), st.sem("b_made"), st.sem("c_made"), st.sem("z_made")
        x_kept, b_kept, c_kept, z_kept = st.sem("x_kept"), st.sem("b_kept"), st.sem("c_kept"), st.sem("z_kept")
        xt_made, bt_made, xt_kept, bt_kept = st.sem("xt_made"), st.sem("bt_made"), st.sem("xt_kept"), st.sem("bt_kept")
        tables, sc_made, mixed, ds_made, ds_masked, states, linked = (st.sem(n) for n in ("tables", "sc_made", "mixed", "ds_made", "ds_masked", "states", "linked"))
        c_decayed, y_made, skipped, y_ready = st.sem("c_decayed"), st.sem("y_made"), st.sem("skipped"), st.sem("y_ready")

        def steps(engine, step):
            for z in range(NZ):
                step(0, z)
            with engine.Fori(1, L3_PAIRS) as h:
                for z in range(NZ):
                    step(h, z)

        def before(h, z):
            return (h, z - 1) if z else (h - 1, NZ - 1)

        def is_first(h, z):
            return isinstance(h, int) and h == 0 and z == 0

        with nc.Block() as block:

            @block.sync
            def _(sp):
                def load(h, z):
                    n, o = NZ * h + z, z
                    if z == 0:
                        wait(sp, z_made, NZ * h)
                        sp.dma_start(w4[:, :, :, :], a["L3_w4"][ds(h, 1)].rearrange("a p t c n -> (a p) t c n")).then_inc(loaded_w4, 16)
                    wait(sp, tables, 2 * n - 2)
                    tok = slice(b * S + z * BANK, b * S + (z + 1) * BANK)
                    for i in range(2):
                        sp.dma_start(decb[:, o, i, :], decays[0][ds(2 * h + i, 1), tok].to_broadcast([P, BANK])).then_inc(loaded_d[o], 16)
                    wait(sp, states, n - 1)
                    for i in range(2):
                        sp.dma_start(prow[i * L3_HD:(i + 1) * L3_HD, o, :],
                                     decays[1][ds(2 * h + i, 1), tok].to_broadcast([L3_HD, BANK])).then_inc(loaded_d[o], 16)

                sp.dma_start(eye4[:, :], a["c_eye4"]).then_inc(consts, 16)
                sp.dma_start(blk[:, :], a["c_l3_block"]).then_inc(consts, 16)
                load(0, 0)
                sp.dma_start(dcol[:, :], a["L3_dcol"][0]).then_inc(loaded_c, 16)
                load(0, 1)
                with sp.Fori(1, L3_PAIRS) as h:
                    load(h, 0)
                    sp.wait_ge(skipped, NZ * h)
                    sp.dma_start(dcol[:, :], a["L3_dcol"][ds(h, 1)].rearrange("a p n -> (a p) n")).then_inc(loaded_c, 16)
                    load(h, 1)

            @block.tensor
            def _(pe):
                def project(h, z):
                    n = NZ * h + z
                    if z == 0:
                        pe.wait_ge(loaded_w4, 16 * h + 16)
                    c0 = b * S + z * BANK
                    for i, (bank, made, used) in enumerate(((px, x_made, xt_kept), (pb, b_made, bt_kept), (pc, c_made, c_decayed), (pz, z_made, z_kept))):
                        wait(pe, used, n)
                        for c in range(DC):
                            mm = pe.matmul(bank[:, :], w4[:, i, c, :], k.XN[:, c, c0:c0 + BANK], start=(c == 0), stop=(c == DC - 1))
                        mm.then_inc(made, 1)

                def outputs(h, z):
                    n, o = NZ * h + z, z
                    pe.wait_ge(states, n + 1)
                    pe.wait_ge(c_decayed, n + 1)
                    pe.wait_ge(mixed, n + 1)
                    wait(pe, skipped, n)
                    for t in range(QUAD):
                        col = slice(t * P, (t + 1) * P)
                        inter = t > 0 or z > 0
                        if inter:
                            pe.matmul(py[:, col], state[:, o, t, :], cdT[:, o, col], start=True, stop=False, skip_group_check=True)
                        for i in range(2):
                            half = slice(i * L3_HD, (i + 1) * L3_HD)
                            mm = pe.matmul(py[half, col], xtok[:, o, t, half], mixT[:, o, i, col], start=not inter, stop=True,
                                           skip_group_check=True)
                    mm.then_inc(y_made, 1)

                def tables_and_states(h, z):
                    n, o = NZ * h + z, z
                    pe.wait_ge(x_kept, n + 1)
                    for t in range(QUAD):
                        mm = pe.transpose(px[:, t * P:(t + 1) * P], xT[:, o, t * P:(t + 1) * P], k.ident[:, :])
                    mm.then_inc(xt_made, 1)
                    pe.wait_ge(b_kept, n + 1)
                    for t in range(QUAD):
                        mm = pe.transpose(pb[:, t * P:(t + 1) * P], bT[:, t * P:(t + 1) * P], k.ident[:, :])
                    mm.then_inc(bt_made, 1)
                    pe.wait_ge(c_kept, n + 1)
                    wait(pe, mixed, n)
                    for t in range(QUAD):
                        mm = pe.matmul(psc[:, 2 * t * P:2 * (t + 1) * P], bT[:, t * P:(t + 1) * P], cT2[:, :, t * P:(t + 1) * P], start=True, stop=True)
                    mm.then_inc(sc_made, 1)
                    pe.wait_ge(bt_kept, n + 1)
                    pe.wait_ge(xt_kept, n + 1)
                    wait(pe, ds_masked, n)
                    for t in range(QUAD):
                        mm = pe.matmul(pds[:, t * P:(t + 1) * P], btok[:, t, :], xtok[:, o, t, :], start=True, stop=True)
                    mm.then_inc(ds_made, 1)

                pe.wait_ge(zeroed, 1)
                def step(h, z):
                    project(h, z)
                    if not is_first(h, z):
                        outputs(*before(h, z))
                    tables_and_states(h, z)

                steps(pe, step)
                outputs(L3_PAIRS - 1, NZ - 1)

            @block.scalar
            def _(act):
                def step(h, z):
                    n, o = NZ * h + z, z
                    act.wait_ge(x_made, n + 1)
                    wait(act, skipped, n - 1)
                    act.activation(xT[:, o, :], px[:, :], ACT.Copy).then_inc(x_kept, 1)
                    act.wait_ge(b_made, n + 1)
                    wait(act, sc_made, n)
                    act.activation(bT[:, :], pb[:, :], ACT.Copy).then_inc(b_kept, 1)
                    act.wait_ge(c_made, n + 1)
                    wait(act, sc_made, n)
                    act.activation(cT2[0:L3_HD, 0, :], pc[0:L3_HD, :], ACT.Copy)
                    act.activation(cT2[L3_HD:P, 1, :], pc[L3_HD:P, :], ACT.Copy).then_inc(c_kept, 1)
                    act.wait_ge(z_made, n + 1)
                    wait(act, y_ready, n - 1)
                    act.activation(sz[:, o, :], pz[:, :], ACT.Silu).then_inc(z_kept, 1)
                    act.wait_ge(xt_made, n + 1)
                    wait(act, y_made, n - 1)
                    act.activation(xtok[:, o, :, :], px[:, :].rearrange("p (t n) -> p t n", t=QUAD), ACT.Copy).then_inc(xt_kept, 1)

                steps(act, step)

            @block.gpsimd
            def _(pool):
                pool.memset(cT2[:, :, :], 0.0).then_inc(zeroed, 1)

                def gate(h, z):
                    n, o = NZ * h + z, z
                    pool.wait_ge(skipped, n + 1)
                    pool.wait_ge(z_kept, n + 1)
                    pool.tensor_tensor(Y[:, ds(h, 1), z * BANK:(z + 1) * BANK].rearrange("p a n -> p (a n)"), skip[:, :], sz[:, o, :],
                                       ALU.mult).then_inc(y_ready, 1)

                def step(h, z):
                    if not is_first(h, z):
                        gate(*before(h, z))

                steps(pool, step)
                gate(L3_PAIRS - 1, NZ - 1)

            @block.vector
            def _(dve):
                dve.wait_ge(consts, 32)

                def add_skip(h, z):
                    n, o = NZ * h + z, z
                    dve.wait_ge(y_made, n + 1)
                    wait(dve, y_ready, n)
                    if z == 0:
                        dve.wait_ge(loaded_c, 16 * h + 16)
                    dve.scalar_tensor_tensor(out=skip[:, :], in0=xT[:, o, :], scalar=dcol[:, 0:1], in1=py[:, :],
                                             op0=ALU.mult, op1=ALU.add).then_inc(skipped, 1)

                def step(h, z):
                    n, o = NZ * h + z, z
                    dve.wait_ge(loaded_d[o], 64 * h + 64)
                    wait(dve, mixed, n)
                    wait(dve, bt_kept, n)
                    for i in range(2):
                        dve.tensor_tensor_scan(table[:, i, :], decb[:, o, i, :], eye4[:, :], 0.0, ALU.mult, ALU.add).then_inc(tables, 1)
                    if not is_first(h, z):
                        add_skip(*before(h, z))
                    dve.wait_ge(c_kept, n + 1)
                    wait(dve, y_made, n - 1)
                    dve.tensor_tensor(cdT[:, o, :], pc[:, :], prow[:, o, :], ALU.mult).then_inc(c_decayed, 1)
                    dve.wait_ge(tables, 2 * n + 2)
                    dve.wait_ge(bt_made, n + 1)
                    wait(dve, ds_made, n)
                    last = table[:, :, :].rearrange("p i (t n) -> p t i n", t=QUAD)[:, :, :, P - 1:P]
                    dve.tensor_tensor(btok[:, :, :].rearrange("p t (i n) -> p t i n", i=2), pb[:, :].rearrange("p (t i n) -> p t i n", t=QUAD, i=2),
                                      last.to_broadcast([P, QUAD, 2, L3_HD]), ALU.mult).then_inc(bt_kept, 1)
                    dve.wait_ge(sc_made, n + 1)
                    dve.tensor_tensor(mixT[:, o, :, :].rearrange("p i (t n) -> p t i n", t=QUAD), psc[:, :].rearrange("p (t i n) -> p t i n", t=QUAD, i=2),
                                      table[:, :, :].rearrange("p i (t n) -> p t i n", t=QUAD), ALU.mult).then_inc(mixed, 1)
                    dve.wait_ge(ds_made, n + 1)
                    wait(dve, states, n)
                    dve.tensor_tensor(dsm[:, :, :], pds[:, :].rearrange("p (t n) -> p t n", t=QUAD), blk[:, :].unsqueeze(1).to_broadcast([P, QUAD, P]),
                                      ALU.mult).then_inc(ds_masked, 1)
                    base = (2 * QUAD - 3) * h + z * (QUAD - 1)
                    dve.wait_ge(ds_masked, n + 1)
                    for t in range(QUAD if z + 1 < NZ else QUAD - 1):
                        out = state[:, o, t + 1, :] if t + 1 < QUAD else state[:, 1 - o, 0, :]
                        if t == 0 and z == 0:
                            op = dve.tensor_copy(out, dsm[:, 0, :])
                        else:
                            if t:
                                dve.wait_ge(linked, base + t)
                            op = dve.scalar_tensor_tensor(out=out, in0=state[:, o, t, :], scalar=prow[:, o, (t + 1) * P - 1:(t + 1) * P], in1=dsm[:, t, :],
                                                          op0=ALU.mult, op1=ALU.add)
                        op.then_inc(states if t == (QUAD - 1 if z + 1 < NZ else QUAD - 2) else linked, 1)

                steps(dve, step)
                add_skip(L3_PAIRS - 1, NZ - 1)


def l3_output(nc, k, a, b, Y):
    with Stage(nc, f"l3o{b}") as st:
        NP_ = L3_PAIRS
        wout = st.sb("wout", [P, NP_, D])
        gb = st.sb("gb", [P, 2, NP_])
        sq = st.sb("sq", [P, 4, BANK])
        bcol = st.sb("bcol", [P, DC])
        avg = st.sb("avg", [P, P])
        std, rstd = st.sb("std", [P, BANK]), st.sb("rstd", [P, BANK])
        tmp = st.sb("tmp", [P, 2, BANK])
        mu = [st.ps(f"mu{i}") for i in range(2)]
        var, pbeta = st.ps("var"), st.ps("pbeta")
        out = [st.ps(f"out{i}") for i in range(2)]
        loaded, set_up, beta_made, beta_kept, gammad = (st.sem(n) for n in ("loaded", "set_up", "beta_made", "beta_kept", "gammad"))
        mu_made, centred, squared, var_made, std_ready, rstd_ready, out_made, scaled, added = (
            st.sem(n) for n in ("mu_made", "centred", "squared", "var_made", "std_ready", "rstd_ready", "out_made", "scaled", "added"))

        with nc.Block() as block:

            @block.sync
            def _(sp):
                sp.dma_start(wout[:, :, :], rows(a["L3_W_outT"])).then_inc(loaded, 16)
                sp.dma_start(gb[:, :, :], a["L3_gb"]).then_inc(loaded, 16)

            @block.tensor
            def _(pe):
                pe.wait_ge(set_up, 1)
                for z in range(NZ):
                    for i in range(NP_):
                        mm = pe.matmul(mu[z][:, :], avg[:, :], Y[:, i, z * BANK:(z + 1) * BANK], start=(i == 0), stop=(i == NP_ - 1))
                    mm.then_inc(mu_made, 1)
                pe.wait_ge(loaded, 32)
                for c in range(DC):
                    for i in range(NP_):
                        mm = pe.matmul(pbeta[:, c:c + 1], wout[:, i, c * P:(c + 1) * P], gb[:, 1, i:i + 1], start=(i == 0), stop=(i == NP_ - 1))
                mm.then_inc(beta_made, 1)
                for z in range(NZ):
                    wait(pe, std_ready, z)
                    for i in range(NP_):
                        n = z * NP_ + i
                        pe.wait_ge(squared, n + 1)
                        pe.matmul(var[:, :], avg[:, :], sq[:, n % 4, :], start=(i == 0), stop=(i == NP_ - 1)).then_inc(var_made, 1)
                    pe.wait_ge(gammad, NP_)
                    for c in range(DC):
                        wait(pe, scaled, z * DC + c - 1)
                        for i in range(NP_):
                            mm = pe.matmul(out[c][:, :], wout[:, i, c * P:(c + 1) * P], Y[:, i, z * BANK:(z + 1) * BANK],
                                           start=(i == 0), stop=(i == NP_ - 1))
                        mm.then_inc(out_made, 1)

            @block.scalar
            def _(act):
                for z in range(NZ):
                    for i in range(NP_):
                        n = z * NP_ + i
                        act.wait_ge(centred, n + 1)
                        wait(act, var_made, n - 3)
                        act.activation(sq[:, n % 4, :], Y[:, i, z * BANK:(z + 1) * BANK], ACT.Square).then_inc(squared, 1)
                    act.wait_ge(var_made, (z + 1) * NP_)
                    wait(act, rstd_ready, z)
                    act.activation(std[:, :], var[:, :], ACT.Sqrt, bias=k.eps[:, 0:1]).then_inc(std_ready, 1)

            @block.vector
            def _(dve):
                dve.memset(avg[:, :], 1.0 / L3_INNER).then_inc(set_up, 1)
                dve.wait_ge(loaded, 32)
                for z in range(NZ):
                    dve.wait_ge(mu_made, z + 1)
                    for i in range(NP_):
                        y = Y[:, i, z * BANK:(z + 1) * BANK]
                        dve.tensor_tensor(y, y, mu[z][:, :], ALU.subtract).then_inc(centred, 1)
                    if z == 0:
                        dve.wait_ge(beta_made, 1)
                        dve.tensor_copy(bcol[:, :], pbeta[:, 0:DC]).then_inc(beta_kept, 1)
                        for i in range(NP_):
                            dve.tensor_scalar(wout[:, i, :], wout[:, i, :], gb[:, 0, i:i + 1], None, ALU.mult).then_inc(gammad, 1)
                        dve.wait_ge(beta_kept, 1)
                    dve.wait_ge(std_ready, z + 1)
                    wait(dve, scaled, z * DC)
                    dve.reciprocal(rstd[:, :], std[:, :]).then_inc(rstd_ready, 1)
                    dve.wait_ge(rstd_ready, z + 1)
                    for c in range(DC):
                        n = z * DC + c
                        dve.wait_ge(out_made, n + 1)
                        wait(dve, added, n - 1)
                        dve.tensor_tensor(tmp[:, n % 2, :], out[c][:, :], rstd[:, :], ALU.mult).then_inc(scaled, 1)
                        dve.wait_ge(scaled, n + 1)
                        x = k.XT[:, c, b * S + z * BANK:b * S + (z + 1) * BANK]
                        dve.scalar_tensor_tensor(out=x, in0=tmp[:, n % 2, :], scalar=bcol[:, c:c + 1], in1=x, op0=ALU.add, op1=ALU.add).then_inc(added, 1)


def l3_constants():
    f = np.float32
    i = np.arange(P) // L3_HD
    return {"c_eye4": np.tile(np.eye(P, dtype=f), (1, QUAD)), "c_l3_block": (i[:, None] == i[None, :]).astype(f)}


def l3_layout(x):
    wT = x["L3_attn_W_in"].T
    part = lambda i: wT[:, i * L3_INNER:(i + 1) * L3_INNER].reshape(DC, P, L3_PAIRS, P).transpose(2, 1, 0, 3)
    gb = np.stack([x["L3_attn_gamma"].reshape(L3_PAIRS, P).T, x["L3_attn_beta"].reshape(L3_PAIRS, P).T], axis=1)
    return {"L3_w4": np.stack([part(0), part(2), part(3), part(1)], axis=2), "L3_wa": wT[:, 4 * L3_INNER:],
            "L3_dcol": x["L3_attn_D"].reshape(L3_PAIRS, P, 1), "L3_W_outT": x["L3_attn_W_out"].T, "L3_gb": gb}


MOE_E, MOE_Z, MOE_K = 32, 32, 8
MOE_I, MOE_CAP = 128, 128
MOE_N = MOE_E + MOE_Z
MOE_SCALE, MOE_TINY = 1.5, 1e-20
MOE_TURN = 4
MOE_OFF = 1e4
MOE_INFO = 7


def l3_ffn(nc, k, a):
    xtok = nc.dram_tensor("moe_xtok", [T + P, D], F32, kind="Internal").ap()
    with Stage(nc, "moe") as st:
        key = st.sb("key", [P, MOE_E, TT])
        info = st.sb("info", [P, MOE_E, TT, MOE_INFO], BF16)
        moe_route(nc, k, a, xtok, key, info)
        moe_experts(nc, k, a, xtok, key, info)


def moe_route(nc, k, a, xtok, key, info):
    with Stage(nc, "mr") as st:
        wcls = st.sb("wcls", [P, DC, MOE_N])
        bias = st.sb("bias", [P, MOE_N])
        tri = st.sb("tri", [P, P])
        ones = st.sb("ones", [P, P])
        ids = st.sb("ids", [P, TT, 3])
        again = st.sb("again", [P, MOE_E * TT])
        rowsN = st.sb("rowsN", [P, TT + 1, D])
        rowsX = st.sb("rowsX", [P, TT + 1, D])
        e1 = st.sb("e1", [P, TT, MOE_N])
        s1 = st.sb("s1", [P, TT, MOE_N])
        biased = st.sb("biased", [P, TT, MOE_N])
        left = st.sb("left", [P, TT, MOE_N])
        chosen = st.sb("chosen", [P, TT, MOE_N])
        w1 = st.sb("w1", [P, TT, MOE_N])
        top8 = st.sb("top8", [P, TT, 8])
        small = st.sb("small", [P, 8, TT])
        maskE = st.sb("maskE", [P, MOE_E, TT])
        before = st.sb("before", [P, MOE_E, TT])
        wE, wa, wb = st.sb("wE", [P, MOE_E, TT]), st.sb("wa", [P, MOE_E, TT]), st.sb("wb", [P, MOE_E, TT])
        lg = st.ps("lg", 2 * BANK)
        place = st.ps("place")
        tr = [st.ps(f"tr{i}") for i in range(4)]
        loaded, logits_made, lowered, exped = st.sem("loaded"), st.sem("logits_made"), st.sem("lowered"), st.sem("exped")
        done, counted, placed = st.sem("done"), st.sem("counted"), st.sem("placed")
        turned, tr_act, tr_pool, zero_rows, stored = st.sem("turned"), st.sem("tr_act"), st.sem("tr_pool"), st.sem("zero_rows"), st.sem("stored")
        jobs = [(src, dst, j) for src, dst in ((k.XN, rowsN), (k.XT, rowsX)) for j in range(TT // 2)]

        with nc.Block() as block:

            @block.sync
            def _(sp):
                sp.dma_start(wcls[:, :, :], rows(a["L3_ffn_w_clsT"])).then_inc(loaded, 16)
                sp.dma_start(bias[:, :], a["L3_ffn_bias_row"].to_broadcast([P, MOE_N])).then_inc(loaded, 16)
                sp.dma_start(tri[:, :], a["c_before"]).then_inc(loaded, 16)
                sp.dma_start(ids[:, :, :], a["c_moe_ids"]).then_inc(loaded, 16)
                sp.dma_start(again[:, :], a["c_moe_again"].to_broadcast([P, MOE_E * TT])).then_inc(loaded, 16)
                sp.wait_ge(zero_rows, 2)
                half = len(jobs) // 2
                sp.wait_ge(tr_act, half)
                sp.dma_start(rows(xtok), rowsN[:, :, :]).then_inc(stored, 16)
                sp.wait_ge(tr_act, 2 * half)
                sp.dma_start(rows(a["out"]), rowsX[:, :, :]).then_inc(stored, 16)
                sp.wait_ge(stored, 32)

            @block.gpsimd
            def _(pool):
                pool.memset(rowsN[:, TT, :], 0.0).then_inc(zero_rows, 1)
                pool.memset(rowsX[:, TT, :], 0.0).then_inc(zero_rows, 1)

            @block.tensor
            def _(pe):
                pe.wait_ge(loaded, 80)
                for t in range(TT):
                    for c in range(DC):
                        mm = pe.matmul(lg[:, t * MOE_N:(t + 1) * MOE_N], k.XN[:, c, t * P:(t + 1) * P], wcls[:, c, :], start=(c == 0), stop=(c == DC - 1))
                mm.then_inc(logits_made, 1)
                for n, (src, _dst, j) in enumerate(jobs):
                    if n >= 4:
                        pe.wait_ge(tr_act, n - 3)
                    for i in range(2):
                        for c in range(DC):
                            t = 2 * j + i
                            mm = pe.transpose(tr[n % 4][:, i * D + c * P:i * D + (c + 1) * P], src[:, c, t * P:(t + 1) * P], k.ident[:, :])
                    mm.then_inc(turned, 1)
                pe.wait_ge(counted, 1)
                pe.matmul(place[:, :], tri[:, :], maskE[:, :, :].rearrange("p e t -> p (e t)"), start=True, stop=False)
                pe.matmul(place[:, :], ones[:, :], before[:, :, :].rearrange("p e t -> p (e t)"), start=False, stop=True).then_inc(placed, 1)

            @block.scalar
            def _(act):
                act.wait_ge(lowered, 1)
                act.activation(e1[:, :, :], e1[:, :, :], ACT.Exp).then_inc(exped, 1)
                for n, (_src, dst, j) in enumerate(jobs):
                    act.wait_ge(turned, n + 1)
                    act.activation(dst[:, 2 * j:2 * j + 2, :], tr[n % 4][:, :].rearrange("p (i n) -> p i n", i=2), ACT.Copy).then_inc(tr_act, 1)

            @block.vector
            def _(dve):
                def per_tile(i):
                    return small[:, i, :].unsqueeze(2).to_broadcast([P, TT, MOE_N])

                logits = lg[:, :].rearrange("p (t n) -> p t n", t=TT)
                dve.memset(ones[:, :], 1.0)
                dve.wait_ge(loaded, 80)
                dve.tensor_copy(info[:, :, :, 0:3], ids[:, :, :].unsqueeze(1).to_broadcast([P, MOE_E, TT, 3]))
                dve.memset(info[:, :, :, 6:7], 1.0)
                dve.wait_ge(logits_made, 1)
                dve.tensor_reduce(small[:, 0, :], logits, AX_X, ALU.max).then_inc(done, 1)
                dve.wait_ge(done, 1)
                dve.tensor_tensor(e1[:, :, :], logits, per_tile(0), ALU.subtract).then_inc(lowered, 1)
                dve.wait_ge(exped, 1)
                dve.tensor_reduce(small[:, 1, :], e1[:, :, :], AX_X, ALU.add).then_inc(done, 1)
                dve.wait_ge(done, 2)
                dve.reciprocal(small[:, 2, :], small[:, 1, :]).then_inc(done, 1)
                dve.wait_ge(done, 3)
                dve.tensor_tensor(s1[:, :, :], e1[:, :, :], per_tile(2), ALU.mult).then_inc(done, 1)
                dve.wait_ge(done, 4)
                dve.tensor_tensor(biased[:, :, :], s1[:, :, :], bias[:, :].unsqueeze(1).to_broadcast([P, TT, MOE_N]), ALU.add).then_inc(done, 1)
                dve.wait_ge(done, 5)
                for t in range(TT):
                    op = dve.max(top8[:, t, :], biased[:, t, :])
                op.then_inc(done, 1)
                dve.wait_ge(done, 6)
                for t in range(TT):
                    op = dve.match_replace(left[:, t, :], top8[:, t, :], biased[:, t, :], -1e30)
                op.then_inc(done, 1)
                dve.wait_ge(done, 7)
                dve.tensor_tensor(chosen[:, :, :], left[:, :, :], biased[:, :, :], ALU.not_equal).then_inc(done, 1)
                dve.wait_ge(done, 8)
                dve.tensor_copy(maskE[:, :, :], chosen[:, :, 0:MOE_E].rearrange("p t e -> p e t")).then_inc(done, 1)
                dve.wait_ge(done, 9)
                dve.tensor_tensor_scan(before[:, :, :].rearrange("p e t -> p (e t)"), again[:, :], maskE[:, :, :].rearrange("p e t -> p (e t)"), 0.0,
                                            ALU.mult, ALU.add).then_inc(done, 1)
                dve.wait_ge(done, 10)
                dve.tensor_tensor(before[:, :, :], before[:, :, :], maskE[:, :, :], ALU.subtract).then_inc(counted, 1)
                dve.tensor_tensor(w1[:, :, :], s1[:, :, :], chosen[:, :, :], ALU.mult).then_inc(done, 1)
                dve.wait_ge(done, 11)
                dve.tensor_reduce(small[:, 3, :], w1[:, :, :], AX_X, ALU.add).then_inc(done, 1)
                dve.wait_ge(done, 12)
                dve.tensor_scalar(small[:, 4, :], small[:, 3, :], MOE_TINY, None, ALU.add).then_inc(done, 1)
                dve.wait_ge(done, 13)
                dve.reciprocal(small[:, 5, :], small[:, 4, :]).then_inc(done, 1)
                dve.wait_ge(done, 14)
                dve.scalar_tensor_tensor(out=w1[:, :, :], in0=w1[:, :, :], scalar=MOE_SCALE, in1=per_tile(5), op0=ALU.mult, op1=ALU.mult).then_inc(done, 1)
                dve.wait_ge(done, 15)
                dve.tensor_reduce(small[:, 6, :], w1[:, :, MOE_E:], AX_X, ALU.add).then_inc(done, 1)
                dve.wait_ge(done, 16)
                dve.tensor_scalar(small[:, 7, :], small[:, 6, :], 1.0, None, ALU.add).then_inc(done, 1)
                dve.wait_ge(done, 17)
                dve.tensor_tensor(wE[:, :, :], w1[:, :, 0:MOE_E].rearrange("p t e -> p e t"), small[:, 7, :].unsqueeze(1).to_broadcast([P, MOE_E, TT]),
                                       ALU.mult).then_inc(done, 1)
                dve.wait_ge(done, 18)
                dve.tensor_copy(info[:, :, :, 3], wE[:, :, :]).then_inc(done, 1)
                dve.wait_ge(done, 19)
                dve.tensor_tensor(wa[:, :, :], wE[:, :, :], info[:, :, :, 3], ALU.subtract).then_inc(done, 1)
                dve.wait_ge(done, 20)
                dve.tensor_copy(info[:, :, :, 4], wa[:, :, :]).then_inc(done, 1)
                dve.wait_ge(done, 21)
                dve.tensor_tensor(wb[:, :, :], wa[:, :, :], info[:, :, :, 4], ALU.subtract).then_inc(done, 1)
                dve.wait_ge(done, 22)
                dve.tensor_copy(info[:, :, :, 5], wb[:, :, :]).then_inc(done, 1)
                dve.wait_ge(done, 23)
                dve.wait_ge(placed, 1)
                dve.scalar_tensor_tensor(out=key[:, :, :].rearrange("p e t -> p (e t)"), in0=maskE[:, :, :].rearrange("p e t -> p (e t)"), scalar=-MOE_OFF,
                                         in1=place[:, :], op0=ALU.mult, op1=ALU.add)


def moe_experts(nc, k, a, xtok, key, info):
    with Stage(nc, "mx") as st:
        slots = st.sb("slots", [P, P])
        spare = st.sb("spare", [P, 2])
        onehot = st.sb("onehot", [P, 2, TT, P], BF16)
        idw = st.sb("idw", [P, MOE_TURN, 2])
        spill = st.sb("spill", [P, 1])
        index = [st.sb(f"index{i}", [P, 1], U32) for i in range(MOE_TURN)]
        xg = [st.sb(f"xg{i}", [P, D]) for i in range(2)]
        xgT = st.sb("xgT", [P, DC * P])
        wgu = st.sb("wgu", [P, 2, DC, 2 * MOE_I])
        wdn = st.sb("wdn", [P, 2, D])
        sg, gated = st.sb("sg", [P, P]), st.sb("gated", [P, P])
        y = [st.sb(f"y{i}", [P, D]) for i in range(2)]
        ptab = [st.ps(f"ptab{i}") for i in range(2)]
        pxt, pgu, py = st.ps("pxt"), st.ps("pgu"), st.ps("py")
        consts, loaded = st.sem("consts"), [st.sem(f"loaded{i}") for i in range(2)]
        marked, tabled, spilled, summed, indexed = (st.sem(n) for n in ("marked", "tabled", "spilled", "summed", "indexed"))
        gathers, scatters = st.sem("gathers"), st.sem("scatters")
        gathered = [st.sem(f"gathered{i}") for i in range(2)]
        turned, x_kept, gu_made, sg_kept, gated_ready, down_made, scaled, scattered = (
            st.sem(n) for n in ("turned", "x_kept", "gu_made", "sg_kept", "gated_ready", "down_made", "scaled", "scattered"))
        TURNS = MOE_E // MOE_TURN

        def steps(engine, step):
            def turn(h, last=False):
                for i in range(MOE_TURN):
                    step(MOE_TURN * h + i, i, lambda n, i=i: not last or i + n < MOE_TURN)
            turn(0)
            with engine.Fori(1, TURNS - 1) as h:
                turn(h)
            turn(TURNS - 1, last=True)

        def uses(e, o):
            return 8 * (e - o) + 16

        with nc.Block() as block:

            @block.sync
            def _(sp):
                sp.dma_start(slots[:, :], a["c_moe_slots"].to_broadcast([P, P])).then_inc(consts, 16)
                sp.dma_start(spare[:, :], a["c_moe_spare"]).then_inc(consts, 16)

                def step(e, i, ahead):
                    o = i % 2
                    wait(sp, down_made, e - 1)
                    sp.dma_start(wgu[:, o, :, :], a["L3_ffn_w_gate_up"][ds(e, 1)].rearrange("a (c p) n -> p (a c) n", p=P)).then_inc(loaded[o], 16)
                    sp.dma_start(wdn[:, o, :], a["L3_ffn_w_down"][ds(e, 1)].rearrange("a p n -> (a p) n")).then_inc(loaded[o], 16)

                steps(sp, step)

            @block.gpsimd
            def _(pool):
                def gather(e, i):
                    pool.wait_ge(indexed, e + 1)
                    wait(pool, turned, e - 1)
                    pool.sem_inc(gathers, 1)
                    pool.indirect_dma_start(xg[i % 2][:, :], None, xtok, bass.IndirectOffsetOnAxis(ap=index[i][:, 0:1], axis=0)).then_inc(gathered[i % 2], 16)

                gather(0, 0)

                def step(e, i, ahead):
                    if ahead(1):
                        gather(e + 1, (i + 1) % MOE_TURN)
                    wait(pool, scattered, 16 * e)
                    pool.wait_ge(scaled, e + 1)
                    pool.sem_inc(scatters, 1)
                    pool.indirect_dma_start(a["out"], bass.IndirectOffsetOnAxis(ap=index[i][:, 0:1], axis=0), y[i % 2][:, :], None,
                                            compute_op=ALU.add).then_inc(scattered, 16)

                steps(pool, step)
                pool.wait_ge(scattered, 16 * MOE_E)

            @block.tensor
            def _(pe):
                def table(e, i):
                    pe.wait_ge(marked, e + 1)
                    wait(pe, indexed, e - 1)
                    for t in range(TT):
                        mm = pe.matmul(ptab[i % 2][:, 0:MOE_INFO], onehot[:, i % 2, t, :], info[:, ds(e, 1), t, :].rearrange("p a n -> p (a n)"),
                                       start=(t == 0), stop=(t == TT - 1))
                    mm.then_inc(tabled, 1)

                table(0, 0)

                def step(e, i, ahead):
                    o = i % 2
                    if ahead(1):
                        table(e + 1, (i + 1) % MOE_TURN)
                    pe.wait_ge(gathered[o], uses(e, o))
                    wait(pe, x_kept, e)
                    for c in range(DC):
                        mm = pe.transpose(pxt[:, c * P:(c + 1) * P], xg[o][:, c * P:(c + 1) * P], k.ident[:, :])
                    mm.then_inc(turned, 1)
                    pe.wait_ge(loaded[o], 2 * uses(e, o))
                    pe.wait_ge(x_kept, e + 1)
                    wait(pe, gated_ready, e)
                    for f in range(2):
                        for c in range(DC):
                            mm = pe.matmul(pgu[:, f * P:(f + 1) * P], wgu[:, o, c, f * P:(f + 1) * P], xgT[:, c * P:(c + 1) * P],
                                           start=(c == 0), stop=(c == DC - 1))
                    mm.then_inc(gu_made, 1)
                    pe.wait_ge(gated_ready, e + 1)
                    wait(pe, scaled, e)
                    pe.matmul(py[:, 0:D], gated[:, :], wdn[:, o, :], start=True, stop=True).then_inc(down_made, 1)

                steps(pe, step)

            @block.scalar
            def _(act):
                def step(e, i, ahead):
                    act.wait_ge(turned, e + 1)
                    wait(act, gu_made, e)
                    act.activation(xgT[:, :], pxt[:, 0:D], ACT.Copy).then_inc(x_kept, 1)
                    act.wait_ge(gu_made, e + 1)
                    wait(act, gated_ready, e)
                    act.activation(sg[:, :], pgu[:, 0:P], ACT.Silu).then_inc(sg_kept, 1)

                steps(act, step)

            @block.vector
            def _(dve):
                def mark(e, i):
                    wait(dve, tabled, e - 1)
                    dve.tensor_tensor(onehot[:, i % 2, :, :], slots[:, :].unsqueeze(1).to_broadcast([P, TT, P]),
                                      key[:, ds(e, 1), :].rearrange("p a t -> p (a t)").unsqueeze(2).to_broadcast([P, TT, P]),
                                      ALU.is_equal).then_inc(marked, 1)

                def make_index(e, i):
                    dve.wait_ge(tabled, e + 1)
                    wait(dve, scattered, 16 * (e - 3))
                    tab = ptab[i % 2]
                    dve.tensor_reduce(idw[:, i, :], tab[:, 0:6].rearrange("p (a b) -> p a b", a=2), AX_X, ALU.add).then_inc(summed, 1)
                    wait(dve, indexed, e)
                    dve.tensor_scalar(spill[:, :], tab[:, 6:7], spare[:, 0:1], spare[:, 1:2], ALU.mult, ALU.add).then_inc(spilled, 1)
                    dve.wait_ge(summed, e + 1)
                    dve.wait_ge(spilled, e + 1)
                    dve.tensor_tensor(index[i][:, :], spill[:, :], idw[:, i, 0:1], ALU.add).then_inc(indexed, 1)

                dve.wait_ge(consts, 32)
                mark(0, 0)
                mark(1, 1)
                make_index(0, 0)

                def step(e, i, ahead):
                    o = i % 2
                    if ahead(1):
                        make_index(e + 1, (i + 1) % MOE_TURN)
                    dve.wait_ge(sg_kept, e + 1)
                    wait(dve, down_made, e)
                    dve.tensor_tensor(gated[:, :], sg[:, :], pgu[:, P:2 * P], ALU.mult).then_inc(gated_ready, 1)
                    if ahead(2):
                        mark(e + 2, (i + 2) % MOE_TURN)
                    dve.wait_ge(down_made, e + 1)
                    wait(dve, scattered, 16 * (e - 1))
                    dve.tensor_scalar(y[o][:, :], py[:, 0:D], idw[:, i, 1:2], None, ALU.mult).then_inc(scaled, 1)

                steps(dve, step)


def moe_constants():
    f = np.float32
    p = np.arange(P)
    ids = np.stack([np.broadcast_to(np.arange(TT) * P, (P, TT)), np.broadcast_to(p[:, None], (P, TT)), np.zeros((P, TT))], axis=2)
    return {"c_before": (p[:, None] < p[None, :]).astype(f), "c_moe_ids": ids.astype(f),
            "c_moe_again": (np.arange(MOE_E * TT) % TT > 0).astype(f).reshape(1, -1), "c_moe_slots": (p - MOE_OFF).astype(f).reshape(1, -1),
            "c_moe_spare": np.stack([-(T + p), T + p], axis=1).astype(f)}


def moe_layout(x):
    return {"L3_ffn_w_clsT": x["L3_ffn_w_cls"].T, "L3_ffn_bias_row": x["L3_ffn_bias"].reshape(1, -1), "L3_ffn_w_gate_up": x["L3_ffn_w_gate_up"],
            "L3_ffn_w_down": x["L3_ffn_w_down"]}


def start(nc, k, a):
    with Stage(nc, "start") as st:
        loaded = st.sem("loaded")
        with nc.Block() as block:

            @block.sync
            def _(sp):
                sp.dma_start(k.XT[:, :, :], rows(a["xT"])).then_inc(loaded, 16)
                sp.dma_start(k.ident[:, :], a["c_ident"]).then_inc(loaded, 16)
                sp.dma_start(k.causal[:, :], a["c_causal"]).then_inc(loaded, 16)
                sp.wait_ge(loaded, 48)

            @block.vector
            def _(dve):
                dve.memset(k.avg[:, :], 1.0 / D)
                dve.memset(k.eps[:, :], EPS)


class Kept:
    pass


LAYERS = [(l0_attn, l0_ffn), (l1_attn, l1_ffn), (l2_attn, l2_ffn), (l3_attn, l3_ffn)]


def program(nc, a):
    with ExitStack() as ctx:
        def keep(name, shape):
            return ctx.enter_context(nc.sbuf_tensor(name, shape, F32))

        k = Kept()
        k.XT = keep("XT", [P, DC, T])
        k.XN = keep("XN", [P, DC, T])
        k.ident = keep("ident", [P, P])
        k.avg = keep("avg", [P, P])
        k.causal = keep("causal", [P, P])
        k.eps = keep("eps", [P, 1])
        Stage.counts.clear()
        start(nc, k, a)
        for i, (attn, ffn) in enumerate(LAYERS):
            norm_stage(nc, k, f"n{i}", k.XT, k.XN)
            attn(nc, k, a)
            clear_semaphores(nc)
            ffn(nc, k, a)
            clear_semaphores(nc)


def constants():
    i = np.arange(P)
    had = np.array([[1.0]])
    while len(had) < P:
        had = np.block([[had, had], [had, -had]])
    return {
        "c_ident": np.eye(P),
        "c_causal": np.where(i[:, None] >= i[None, :], 0.0, -1e30),
        "c_had": had,
        **l1_constants(), **l2_constants(), **l3_constants(), **moe_constants(),
    }


def columns(v):
    return v.reshape(-1, P).T


def layout(x):
    out = {"xT": x["L0_attn_x"].reshape(T, D).T}
    for n in ("L0_attn_w_q", "L0_attn_w_kv", "L0_attn_w_dense"):
        out[n] = x[n]
    for n in ("L0_ffn_W_up", "L0_ffn_W_gate", "L0_ffn_W_down", "L1_ffn_weight", "L2_ffn_weight"):
        out[n + "T"] = x[n].T
    for n in ("L0_ffn_SU_ug", "L0_ffn_SU_dp", "L0_ffn_Wscale_ug", "L0_ffn_Wscale_dp", "L2_ffn_bias"):
        out[n + "_cols"] = columns(x[n])
    out["L1_ffn_cols"] = np.stack([columns(x[n]) for n in ("L1_ffn_gamma", "L1_ffn_beta", "L1_ffn_ln_weight", "L1_ffn_ln_bias", "L1_attn_bo")], axis=1)
    return {**out, **l1_layout(x), **l2_layout(x), **l3_layout(x), **moe_layout(x)}


def kernel(**inputs):
    import concourse.bacc as _bacc
    from concourse.bass_utils import run_bass_kernel_spmd as _run

    x = {n: np.asarray(v) for n, v in inputs.items()}
    arrays = {n: np.ascontiguousarray(v) for n, v in layout(x).items()}
    arrays.update({n: np.ascontiguousarray(v, dtype=np.float32) for n, v in constants().items()})

    nc = _bacc.Bacc("TRN2", target_bir_lowering=False, num_devices=1)
    a = {n: nc.dram_tensor(n, v.shape, mybir.dt.from_np(v.dtype), kind="ExternalInput").ap() for n, v in arrays.items()}
    out = nc.dram_tensor("out", (T + P, D), F32, kind="ExternalOutput").ap()
    program(nc, {**a, "out": out})
    r = _run(nc, [arrays], core_ids=[0])
    return r.results[0]["out"][:T].reshape(B, S, D)
```

```python
from contextlib import ExitStack

import numpy as np

import concourse.bass as bass
from concourse import mybir

F32 = mybir.dt.float32
F32R = mybir.dt.float32r
U32 = mybir.dt.uint32
BF16 = mybir.dt.bfloat16
ALU = mybir.AluOpType
ACT = mybir.ActivationFunctionType
AX_X = mybir.AxisListType.X
ds = bass.ds

P = 128
BANK = 512
B, S, D = 2, 1024, 256
T = B * S
DC = D // P
NQ = S // P
TT = T // P
NJ = T // BANK
EPS = 1e-5


class Stage:

    counts = []

    def __init__(self, nc, name):
        self.nc, self.name, self.ctx = nc, name, ExitStack()

    def __enter__(self):
        return self

    def __exit__(self, *e):
        return self.ctx.__exit__(*e)

    def sb(self, name, shape, dt=F32):
        return self.ctx.enter_context(self.nc.sbuf_tensor(f"{self.name}_{name}", shape, dt))

    def ps(self, name, cols=BANK):
        return self.ctx.enter_context(self.nc.psum_tensor(f"{self.name}_{name}", [P, cols], F32))

    def sem(self, name):
        s = self.ctx.enter_context(self.nc.semaphore(f"{self.name}_{name}"))
        Stage.counts.append(s.num)
        return s


def clear_semaphores(nc):
    numbers = sorted(set(Stage.counts))
    Stage.counts.clear()
    with nc.Block() as block:

        @block.gpsimd
        def _(pool):
            while numbers:
                first = last = numbers.pop(0)
                while numbers and numbers[0] == last + 1:
                    last = numbers.pop(0)
                pool.sem_clear(range(first, last + 1))


def rows(w):
    return w.rearrange("(c p) n -> p c n", p=P)


def wait(engine, sem, value):
    if not isinstance(value, int) or value > 0:
        engine.wait_ge(sem, value)


def norm_stage(nc, k, name, src, dst):
    with Stage(nc, name) as st:
        mean = [st.ps(f"mean{i}") for i in range(2)]
        var = [st.ps(f"var{i}") for i in range(2)]
        sq = st.sb("sq", [P, 2, DC, BANK])
        std = st.sb("std", [P, 2, BANK])
        rstd = st.sb("rstd", [P, 2, BANK])
        mean_ready, centred, squared = st.sem("mean_ready"), st.sem("centred"), st.sem("squared")
        var_ready, std_ready, rstd_ready = st.sem("var_ready"), st.sem("std_ready"), st.sem("rstd_ready")
        scaled = st.sem("scaled")

        def tok(j):
            return slice(j * BANK, (j + 1) * BANK)

        with nc.Block() as block:

            @block.tensor
            def _(pe):
                def mean_of(j):
                    if j >= 2:
                        pe.wait_ge(centred, j - 1)
                    for c in range(DC):
                        mm = pe.matmul(mean[j % 2][:, :], k.avg[:, :], src[:, c, tok(j)], start=(c == 0), stop=(c == DC - 1))
                    mm.then_inc(mean_ready, 1)

                def var_of(j):
                    pe.wait_ge(squared, j + 1)
                    if j >= 2:
                        pe.wait_ge(std_ready, j - 1)
                    for c in range(DC):
                        mm = pe.matmul(var[j % 2][:, :], k.avg[:, :], sq[:, j % 2, c, :], start=(c == 0), stop=(c == DC - 1))
                    mm.then_inc(var_ready, 1)

                mean_of(0)
                for j in range(NJ):
                    if j + 1 < NJ:
                        mean_of(j + 1)
                    var_of(j)

            @block.vector
            def _(dve):
                def centre(j):
                    dve.wait_ge(mean_ready, j + 1)
                    for c in range(DC):
                        op = dve.tensor_tensor(dst[:, c, tok(j)], src[:, c, tok(j)], mean[j % 2][:, :], ALU.subtract)
                    op.then_inc(centred, 1)

                centre(0)
                for j in range(NJ):
                    if j + 1 < NJ:
                        centre(j + 1)
                    dve.wait_ge(std_ready, j + 1)
                    if j >= 2:
                        dve.wait_ge(scaled, j - 1)
                    dve.reciprocal(rstd[:, j % 2, :], std[:, j % 2, :]).then_inc(rstd_ready, 1)

            @block.scalar
            def _(act):
                for j in range(NJ):
                    act.wait_ge(centred, j + 1)
                    if j >= 2:
                        act.wait_ge(var_ready, j - 1)
                    act.activation(sq[:, j % 2, :, :], dst[:, :, tok(j)], ACT.Square).then_inc(squared, 1)
                    act.wait_ge(var_ready, j + 1)
                    if j >= 2:
                        act.wait_ge(rstd_ready, j - 1)
                    act.activation(std[:, j % 2, :], var[j % 2][:, :], ACT.Sqrt, bias=k.eps[:, 0:1]).then_inc(std_ready, 1)

            @block.gpsimd
            def _(pool):
                for j in range(NJ):
                    pool.wait_ge(rstd_ready, j + 1)
                    for c in range(DC):
                        op = pool.tensor_tensor(dst[:, c, tok(j)], dst[:, c, tok(j)], rstd[:, j % 2, :], ALU.mult)
                    op.then_inc(scaled, 1)


def split_stage(nc, name, src, hi, lo):
    with Stage(nc, name) as st:
        rounded = st.sem("rounded")
        n = src.shape[-1]
        parts = [(c, slice(j, j + BANK)) for j in range(0, n, BANK) for c in range(DC)]
        with nc.Block() as block:

            @block.scalar
            def _(act):
                for c, tok in parts:
                    act.activation(hi[:, c, tok], src[:, c, tok], ACT.Copy).then_inc(rounded, 1)

            @block.vector
            def _(dve):
                for i, (c, tok) in enumerate(parts):
                    if i % 3 != 2:
                        dve.wait_ge(rounded, i + 1)
                        dve.tensor_tensor(lo[:, c, tok], src[:, c, tok], hi[:, c, tok].bitcast(F32), ALU.subtract)

            @block.gpsimd
            def _(pool):
                for i, (c, tok) in enumerate(parts):
                    if i % 3 == 2:
                        pool.wait_ge(rounded, i + 1)
                        pool.tensor_tensor(lo[:, c, tok], src[:, c, tok], hi[:, c, tok].bitcast(F32), ALU.subtract)


def split_product(pe, out, w_hi, w_lo, x_hi, x_lo):
    terms = [(w, x, c) for c in range(DC) for w, x in ((w_hi, x_hi), (w_hi, x_lo), (w_lo, x_hi))]
    for i, (w, x, c) in enumerate(terms):
        mm = pe.matmul(out, w(c), x(c), start=(i == 0), stop=(i == len(terms) - 1))
    return mm


L0_HEADS, L0_GROUPS, L0_HD = 16, 4, 128
L0_HPG = L0_HEADS // L0_GROUPS
L0_SCALE = L0_HD ** -0.5


def l0_attn(nc, k, a):
    with Stage(nc, "l0a") as st:
        KT = st.sb("KT", [P, L0_GROUPS, T])
        V = st.sb("V", [P, TT, L0_GROUPS * L0_HD])
        l0_kv(nc, k, a, KT, V)
        l0_heads(nc, k, a, KT, V)


def l0_kv(nc, k, a, KT, V):
    with Stage(nc, "l0kv") as st:
        acc = [st.ps(f"acc{i}") for i in range(8)]
        w_loaded, made, kept_act, kept_dve = st.sem("w_loaded"), st.sem("made"), st.sem("kept_act"), st.sem("kept_dve")
        GD = L0_GROUPS * L0_HD
        wkv = st.sb("wkv", [P, DC, 2 * GD])
        w_hi, w_lo = st.sb("w_hi", [P, DC, 2 * GD], F32R), st.sb("w_lo", [P, DC, 2 * GD], F32R)
        whi_ready, wlo_ready = st.sem("whi_ready"), st.sem("wlo_ready")
        jobs = [("k", g, j) for g in range(L0_GROUPS) for j in range(NJ)] + [("v", t, 0) for t in range(TT)]

        def target(n):
            kind, i, j = jobs[n]
            return KT[:, i, j * BANK:(j + 1) * BANK] if kind == "k" else V[:, i, :]

        with nc.Block() as block:

            @block.sync
            def _(sp):
                sp.dma_start(wkv[:, :, :], rows(a["L0_attn_w_kv"])).then_inc(w_loaded, 16)

            @block.tensor
            def _(pe):
                pe.wait_ge(wlo_ready, DC)
                for n, (kind, i, j) in enumerate(jobs):
                    if n >= 8:
                        pe.wait_ge(kept_act if n % 2 == 0 else kept_dve, (n - 8) // 2 + 1)
                    if kind == "k":
                        tok, col = slice(j * BANK, (j + 1) * BANK), slice(i * P, (i + 1) * P)
                        mm = split_product(pe, acc[n % 8][:, :], lambda c: w_hi[:, c, col], lambda c: w_lo[:, c, col],
                                           lambda c: k.XH[:, c, tok], lambda c: k.XL[:, c, tok])
                    else:
                        tok, col = slice(i * P, (i + 1) * P), slice(GD, 2 * GD)
                        mm = split_product(pe, acc[n % 8][:, :], lambda c: k.XH[:, c, tok], lambda c: k.XL[:, c, tok],
                                           lambda c: w_hi[:, c, col], lambda c: w_lo[:, c, col])
                    mm.then_inc(made, 1)

            @block.scalar
            def _(act):
                act.wait_ge(w_loaded, 16)
                for c in range(DC):
                    act.activation(w_hi[:, c, :], wkv[:, c, :], ACT.Copy).then_inc(whi_ready, 1)
                for n in range(0, len(jobs), 2):
                    act.wait_ge(made, n + 1)
                    act.activation(target(n), acc[n % 8][:, :], ACT.Copy).then_inc(kept_act, 1)

            @block.vector
            def _(dve):
                for c in range(DC):
                    dve.wait_ge(whi_ready, c + 1)
                    dve.tensor_tensor(w_lo[:, c, :], wkv[:, c, :], w_hi[:, c, :].bitcast(F32), ALU.subtract).then_inc(wlo_ready, 1)
                for n in range(1, len(jobs), 2):
                    dve.wait_ge(made, n + 1)
                    dve.tensor_copy(target(n), acc[n % 8][:, :]).then_inc(kept_dve, 1)


def l0_heads(nc, k, a, KT, V):
    U = B * NQ
    GPB = sum(-(-(t + 1) // 4) for t in range(NQ))
    G = B * GPB
    group_of = [(u, g) for u in range(U) for g in range(-(-(u % NQ + 1) // 4))]
    first_group = [group_of.index((u, 0)) for u in range(U)]

    with Stage(nc, "l0h") as st:
        wq = st.sb("wq", [P, DC, P])
        wq_hi, wq_lo = st.sb("wq_hi", [P, DC, P], F32R), st.sb("wq_lo", [P, DC, P], F32R)
        whi_ready, wlo_ready = st.sem("whi_ready"), st.sem("wlo_ready")
        wd = st.sb("wd", [P, D])
        QT = st.sb("QT", [P, T])
        probs = st.sb("probs", [P, 4, S])
        VG = st.sb("VG", [P, TT, P])
        PT = st.sb("PT", [P, 2, NQ, P])
        ctxT = st.sb("ctxT", [P, 2, P])
        top = st.sb("top", [P, 2])
        negtop = st.sb("negtop", [P, 2])
        total = st.sb("total", [P, 4])
        inv = st.sb("inv", [P, 4])
        sc = [st.ps(f"sc{i}", 2 * BANK) for i in range(2)]
        tp = [st.ps(f"tp{i}") for i in range(2)]
        cx = st.ps("cx")
        outp = st.ps("outp")
        wq_loaded, wd_loaded = st.sem("wq_loaded"), st.sem("wd_loaded")
        q_made, q_kept = st.sem("q_made"), st.sem("q_kept")
        scores_ready, masked, top_ready, negtop_ready = st.sem("scores_ready"), st.sem("masked"), st.sem("top_ready"), st.sem("negtop_ready")
        probs_ready, inv_ready = st.sem("probs_ready"), st.sem("inv_ready")
        turned, pt_act, pt_dve, pv_done = st.sem("turned"), st.sem("pt_act"), st.sem("pt_dve"), st.sem("pv_done")
        ctxT_ready, probs_scaled, vg_ready, copies = st.sem("ctxT_ready"), st.sem("probs_scaled"), st.sem("vg_ready"), st.sem("copies")
        dense_done, added = st.sem("dense_done"), st.sem("added")

        SPLIT_AT = 4

        def keys(u):
            return (u % NQ + 1) * P

        with nc.Block() as block:

            @block.sync
            def _(sp):
                sp.dma_start(wq[:, :, :], rows(a["L0_attn_w_q"])[:, :, 0:P]).then_inc(wq_loaded, 16)
                sp.dma_start(wd[:, :], a["L0_attn_w_dense"][0:P, :]).then_inc(wd_loaded, 16)
                with sp.Fori(1, L0_HEADS) as h:
                    sp.wait_ge(wlo_ready, h)
                    sp.dma_start(wq[:, :, :], rows(a["L0_attn_w_q"])[:, :, ds(h * P, P)]).then_inc(wq_loaded, 16)
                    sp.wait_ge(dense_done, h * U)
                    sp.dma_start(wd[:, :], a["L0_attn_w_dense"][ds(h * P, P), :]).then_inc(wd_loaded, 16)
                sp.wait_ge(wlo_ready, L0_HEADS)
                sp.dma_start(wq[:, :, :], rows(a["L0_attn_w_q"])[:, :, 0:P]).then_inc(wq_loaded, 16)

            @block.tensor
            def _(pe):
                def project(h, pieces):
                    pe.wait_ge(wlo_ready, h + 1)
                    for j in pieces:
                        tok = slice(j * BANK, (j + 1) * BANK)
                        split_product(pe, sc[j // 2][:, (j % 2) * BANK:(j % 2 + 1) * BANK], lambda c: wq_hi[:, c, :], lambda c: wq_lo[:, c, :],
                                      lambda c: k.XH[:, c, tok], lambda c: k.XL[:, c, tok]).then_inc(q_made, 1)

                project(0, range(NJ))
                with pe.Fori(0, L0_GROUPS) as g:
                    with pe.Fori(0, L0_HPG) as hg:
                        h = g * L0_HPG + hg

                        def scores(u):
                            b, t = divmod(u, NQ)
                            if u >= 2:
                                pe.wait_ge(probs_ready, h * U + u - 1)
                            elif u == 0:
                                pe.wait_ge(q_kept, h * NJ + 2)
                            else:
                                pe.wait_ge(q_kept, h * NJ + 4)
                            for lo in range(0, keys(u), BANK):
                                n = min(BANK, keys(u) - lo)
                                mm = pe.matmul(sc[u % 2][:, lo:lo + n], QT[:, u * P:(u + 1) * P],
                                               KT[:, ds(g, 1), b * S + lo:b * S + lo + n], start=True, stop=True)
                            mm.then_inc(scores_ready, 1)

                        def turn_probs(u):
                            t = u % NQ
                            pe.wait_ge(probs_scaled, h * U + u + 1)
                            for n in range(first_group[u], first_group[u] + -(-(t + 1) // 4)):
                                if n % 2 == 0:
                                    pe.wait_ge(pt_act, h * (G // 2) + n // 2 + 1)
                                else:
                                    pe.wait_ge(pt_dve, h * (G // 2) + n // 2 + 1)
                                q = 4 * (n - first_group[u])
                                for kb in range(q, min(q + 4, t + 1)):
                                    mm = pe.transpose(tp[n % 2][:, (kb - q) * P:(kb - q + 1) * P],
                                                      probs[:, u % 4, kb * P:(kb + 1) * P], k.ident[:, :])
                                mm.then_inc(turned, 1)

                        def weigh_values(u):
                            b, t = divmod(u, NQ)
                            last = first_group[u] + -(-(t + 1) // 4) - 1
                            pe.wait_ge(pt_act, h * (G // 2) + last // 2 + 2)
                            pe.wait_ge(pt_dve, h * (G // 2) + (last + 1) // 2 + 1)
                            if t == 0:
                                pe.wait_ge(vg_ready, B * g + b + 1)
                            for kb in range(t + 1):
                                mm = pe.matmul(cx[:, 0:P], VG[:, b * NQ + kb, :], PT[:, u % 2, kb, :], start=(kb == 0), stop=(kb == t))
                            mm.then_inc(pv_done, 1)

                        def dense(u):
                            if u == 0:
                                pe.wait_ge(wd_loaded, h * 16 + 16)
                            pe.wait_ge(ctxT_ready, h * U + u + 1)
                            pe.wait_ge(added, h * U + u + 1)
                            for c in range(DC):
                                mm = pe.matmul(outp[:, c * P:(c + 1) * P], wd[:, c * P:(c + 1) * P], ctxT[:, u % 2, :],
                                               start=True, stop=True)
                            mm.then_inc(dense_done, 1)

                        for s in range(U + 4):
                            if s < U:
                                scores(s)
                            else:
                                if s < U + 2:
                                    pe.wait_ge(probs_ready, h * U + s - 1)
                                    project(h + 1, (2 * (s - U), 2 * (s - U) + 1))
                            if 2 <= s <= U + 1:
                                turn_probs(s - 2)
                            if s >= 4:
                                dense(s - 4)
                            if 3 <= s <= U + 2:
                                weigh_values(s - 3)

            @block.gpsimd
            def _(pool):
                def split_weights(h):
                    pool.wait_ge(whi_ready, h + 1)
                    pool.tensor_tensor(wq_lo[:, :, :], wq[:, :, :], wq_hi[:, :, :].bitcast(F32), ALU.subtract).then_inc(wlo_ready, 1)

                def copy_values(g, b):
                    pool.tensor_copy(VG[:, b * NQ:(b + 1) * NQ, :], V[:, b * NQ:(b + 1) * NQ, ds(g * P, P)]).then_inc(vg_ready, 1)

                def scale_probs(g):
                    with pool.Fori(0, L0_HPG) as hg:
                        h = g * L0_HPG + hg
                        for u in range(U):
                            pool.wait_ge(inv_ready, h * U + u + 1)
                            p = probs[:, u % 4, 0:keys(u)]
                            pool.tensor_tensor(p, p, inv[:, u % 4:u % 4 + 1].to_broadcast([P, keys(u)]), ALU.mult).then_inc(probs_scaled, 1)
                            if u == SPLIT_AT:
                                split_weights(h + 1)

                split_weights(0)
                for b in range(B):
                    copy_values(0, b)
                with pool.Fori(0, L0_GROUPS - 1) as g:
                    scale_probs(g)
                    for b in range(B):
                        pool.wait_ge(pv_done, ((g + 1) * L0_HPG - 1) * U + (b + 1) * NQ)
                        pool.sem_inc(copies, 1)
                        copy_values(g + 1, b)
                scale_probs(L0_GROUPS - 1)

            @block.vector
            def _(dve):
                dve.sem_inc(pt_dve, 1)
                dve.sem_inc(added, 1)
                with dve.Fori(0, L0_HEADS) as h:

                    def row_max(u):
                        t = u % NQ
                        diag = sc[u % 2][:, t * P:(t + 1) * P]
                        dve.wait_ge(scores_ready, h * U + u + 1)
                        dve.tensor_tensor(diag, diag, k.causal[:, :], ALU.add).then_inc(masked, 1)
                        dve.wait_ge(masked, h * U + u + 1)
                        dve.reduce_max(top[:, u % 2:u % 2 + 1], sc[u % 2][:, 0:keys(u)], AX_X).then_inc(top_ready, 1)
                        dve.wait_ge(top_ready, h * U + u + 1)
                        dve.tensor_scalar(negtop[:, u % 2:u % 2 + 1], top[:, u % 2:u % 2 + 1], -L0_SCALE, None,
                                          ALU.mult).then_inc(negtop_ready, 1)

                    def invert(u):
                        dve.wait_ge(probs_ready, h * U + u + 1)
                        dve.reciprocal(inv[:, u % 4:u % 4 + 1], total[:, u % 4:u % 4 + 1]).then_inc(inv_ready, 1)

                    def keep_turned(u):
                        t = u % NQ
                        for n in range(first_group[u], first_group[u] + -(-(t + 1) // 4)):
                            if n % 2 == 1:
                                q = 4 * (n - first_group[u])
                                m = min(4, t + 1 - q)
                                dve.wait_ge(turned, h * G + n + 1)
                                if u >= 2:
                                    dve.wait_ge(pv_done, h * U + u - 1)
                                dve.tensor_copy(PT[:, u % 2, q:q + m, :], tp[1][:, 0:m * P]).then_inc(pt_dve, 1)

                    def add_dense(u):
                        dve.wait_ge(dense_done, h * U + u + 1)
                        x = k.XT[:, :, u * P:(u + 1) * P]
                        dve.tensor_tensor(x, x, outp[:, 0:DC * P].rearrange("p (c n) -> p c n", c=DC), ALU.add).then_inc(added, 1)

                    for s in range(U + 4):
                        if 1 <= s <= U:
                            invert(s - 1)
                        if s < U:
                            row_max(s)
                        if 2 <= s <= U + 1:
                            keep_turned(s - 2)
                        if s >= 4:
                            add_dense(s - 4)

            @block.scalar
            def _(act):
                def split_weights(h):
                    act.wait_ge(wq_loaded, h * 16 + 16)
                    wait(act, q_made, h * NJ)
                    act.activation(wq_hi[:, :, :], wq[:, :, :], ACT.Copy).then_inc(whi_ready, 1)

                def keep_q(h, pieces):
                    for j in pieces:
                        act.wait_ge(q_made, h * NJ + j + 1)
                        act.activation(QT[:, j * BANK:(j + 1) * BANK], sc[j // 2][:, (j % 2) * BANK:(j % 2 + 1) * BANK],
                                       ACT.Copy).then_inc(q_kept, 1)

                act.sem_inc(pt_act, 1)
                split_weights(0)
                keep_q(0, range(NJ))
                with act.Fori(0, L0_HEADS) as h:

                    def keep_turned(u):
                        t = u % NQ
                        for n in range(first_group[u], first_group[u] + -(-(t + 1) // 4)):
                            if n % 2 == 0:
                                q = 4 * (n - first_group[u])
                                m = min(4, t + 1 - q)
                                act.wait_ge(turned, h * G + n + 1)
                                if u >= 2:
                                    act.wait_ge(pv_done, h * U + u - 1)
                                act.activation(PT[:, u % 2, q:q + m, :], tp[0][:, 0:m * P].rearrange("p (m n) -> p m n", m=m),
                                               ACT.Copy).then_inc(pt_act, 1)

                    def keep_ctxT(u):
                        act.wait_ge(pv_done, h * U + u + 1)
                        if u >= 2:
                            act.wait_ge(dense_done, h * U + u - 1)
                        act.activation(ctxT[:, u % 2, :], cx[:, 0:P], ACT.Copy).then_inc(ctxT_ready, 1)

                    def exp(u):
                        act.wait_ge(negtop_ready, h * U + u + 1)
                        if u >= 4:
                            act.wait_ge(turned, h * G + first_group[u - 3])
                        act.activation(probs[:, u % 4, 0:keys(u)], sc[u % 2][:, 0:keys(u)], ACT.Exp,
                                       bias=negtop[:, u % 2:u % 2 + 1], scale=L0_SCALE,
                                       accum_out=total[:, u % 4:u % 4 + 1]).then_inc(probs_ready, 1)

                    for s in range(U + 4):
                        if s >= 4:
                            keep_ctxT(s - 4)
                        if 2 <= s <= U + 1:
                            keep_turned(s - 2)
                        if s == SPLIT_AT:
                            split_weights(h + 1)
                        if s < U:
                            exp(s)
                        elif s < U + 2:
                            keep_q(h + 1, (2 * (s - U), 2 * (s - U) + 1))


L0_INTER = 1024
L0_FC = L0_INTER // P


def l0_ffn(nc, k, a):
    with Stage(nc, "l0f") as st:
        wu_hi, wu_lo = st.sb("wu_hi", [P, DC, L0_INTER], F32R), st.sb("wu_lo", [P, DC, L0_INTER], F32R)
        wg_hi, wg_lo = st.sb("wg_hi", [P, DC, L0_INTER], F32R), st.sb("wg_lo", [P, DC, L0_INTER], F32R)
        wd_hi, wd_lo = st.sb("wd_hi", [P, L0_FC, D], F32R), st.sb("wd_lo", [P, L0_FC, D], F32R)
        su = st.sb("su", [P, DC])
        sd = st.sb("sd", [P, L0_FC])
        su_n = st.sb("su_n", [P, DC])
        sd_n = st.sb("sd_n", [P, L0_FC])
        s_up = st.sb("s_up", [P, L0_FC])
        s_gate = st.sb("s_gate", [P, L0_FC])
        s_down = st.sb("s_down", [P, DC])
        with Stage(nc, "l0w") as s2:
            had = s2.sb("had", [P, 2, P])
            raw = s2.sb("raw", [P, 2, DC, L0_INTER])
            rawd = s2.sb("rawd", [P, L0_FC, D])
            bf0 = s2.sb("bf0", [P, L0_FC, D])
            bf1 = s2.sb("bf1", [P, L0_FC, D])
            wdn = s2.sb("wdn", [P, L0_FC, D])
            low, wd_ready = s2.sem("low"), s2.sem("wd_ready")
            acc = [s2.ps(f"acc{i}") for i in range(8)]
            loaded, made, kept, had_ready, flown = s2.sem("loaded"), s2.sem("made"), s2.sem("kept"), s2.sem("had_ready"), s2.sem("flown")
            NL = 9

            with nc.Block() as block:

                @block.sync
                def _(sp):
                    sp.dma_start(had[:, 0, :], a["c_had"]).then_inc(loaded, 16)
                    sp.dma_start(su[:, :], a["L0_ffn_SU_ug_cols"]).then_inc(loaded, 16)
                    sp.dma_start(raw[:, 0, :, :], rows(a["L0_ffn_W_upT"])).then_inc(loaded, 16)
                    sp.dma_start(raw[:, 1, :, :], rows(a["L0_ffn_W_gateT"])).then_inc(loaded, 16)
                    sp.dma_start(rawd[:, :, :], rows(a["L0_ffn_W_downT"])).then_inc(loaded, 16)
                    sp.dma_start(sd[:, :], a["L0_ffn_SU_dp_cols"]).then_inc(loaded, 16)
                    sp.dma_start(s_up[:, :], a["L0_ffn_Wscale_ug_cols"][:, 0:L0_FC]).then_inc(loaded, 16)
                    sp.dma_start(s_gate[:, :], a["L0_ffn_Wscale_ug_cols"][:, L0_FC:2 * L0_FC]).then_inc(loaded, 16)
                    sp.dma_start(s_down[:, :], a["L0_ffn_Wscale_dp_cols"]).then_inc(loaded, 16)

                @block.tensor
                def _(pe):
                    pe.wait_ge(had_ready, 1)
                    n = 0
                    for m in range(2):
                        for half in range(2):
                            for lo in range(0, L0_INTER, BANK):
                                for c in range(DC):
                                    neg = 1 if half == 1 and c == 1 else 0
                                    mm = pe.matmul(acc[n % 8][:, :], had[:, neg, :], raw[:, m, c, lo:lo + BANK],
                                                   start=(c == 0), stop=(c == DC - 1))
                                mm.then_inc(made, 1)
                                n += 1
                    for i in range(L0_FC // 2):
                        pe.wait_ge(low, i + 1)
                        pe.matmul(acc[i][:, :], had[:, 0, :], rawd[:, 2 * i:2 * i + 2, :], start=True, stop=True).then_inc(made, 1)

                @block.scalar
                def _(act):
                    act.wait_ge(had_ready, 3)
                    for n in range(8):
                        m, half, q = n // 4, n // 2 % 2, n % 2
                        act.wait_ge(made, n + 1)
                        act.activation((wu_hi, wg_hi)[m][:, half, q * BANK:(q + 1) * BANK], acc[n][:, :], ACT.Copy,
                                       scale=su_n[:, half:half + 1]).then_inc(kept, 1)
                    for i in range(L0_FC // 2):
                        act.wait_ge(made, 9 + i)
                        act.activation(bf0[:, 2 * i:2 * i + 2, :], acc[i][:, :].rearrange("p (i n) -> p i n", i=2),
                                       ACT.Copy).then_inc(kept, 1)
                    for i in range(0, L0_FC, 2):
                        act.wait_ge(wd_ready, i + 2)
                        act.activation(wd_hi[:, i:i + 2, :], wdn[:, i:i + 2, :], ACT.Copy).then_inc(kept, 1)

                @block.vector
                def _(dve):
                    dve.wait_ge(loaded, 16 * NL)
                    dve.tensor_scalar(had[:, 1, :], had[:, 0, :], -1.0, None, ALU.mult).then_inc(had_ready, 1)
                    dve.tensor_scalar(su_n[:, :], su[:, :], D ** -0.5, None, ALU.mult).then_inc(had_ready, 1)
                    dve.tensor_scalar(sd_n[:, :], sd[:, :], L0_INTER ** -0.5, None, ALU.mult).then_inc(had_ready, 1)
                    for n in range(8):
                        m, half, q = n // 4, n // 2 % 2, n % 2
                        part = slice(q * BANK, (q + 1) * BANK)
                        dve.wait_ge(kept, n + 1)
                        if n == 0:
                            dve.wait_ge(had_ready, 3)
                        dve.scalar_tensor_tensor(out=(wu_lo, wg_lo)[m][:, half, part], in0=acc[n][:, :], scalar=su_n[:, half:half + 1],
                                                 in1=(wu_hi, wg_hi)[m][:, half, part].bitcast(F32), op0=ALU.mult, op1=ALU.subtract).then_inc(low, 1)
                    dve.wait_ge(kept, 12)
                    src, dst = bf0, bf1
                    for i, h in enumerate((1, 2, 4)):
                        if i:
                            dve.wait_ge(flown, 2 * i)
                        sv = src[:, :, :].rearrange("p (g t h) n -> p g t (h n)", t=2, h=h)
                        dv = dst[:, :, :].rearrange("p (g t h) n -> p g t (h n)", t=2, h=h)
                        dve.tensor_tensor(dv[:, :, 0, :], sv[:, :, 0, :], sv[:, :, 1, :], ALU.add).then_inc(flown, 1)
                        dve.tensor_tensor(dv[:, :, 1, :], sv[:, :, 0, :], sv[:, :, 1, :], ALU.subtract).then_inc(flown, 1)
                        src, dst = dst, src
                    dve.wait_ge(flown, 6)
                    dve.wait_ge(had_ready, 3)
                    for i in range(L0_FC):
                        dve.tensor_scalar(wdn[:, i, :], src[:, i, :], sd_n[:, i:i + 1], None, ALU.mult).then_inc(wd_ready, 1)
                    for i in range(0, L0_FC, 2):
                        dve.wait_ge(kept, 12 + i // 2 + 1)
                        dve.tensor_tensor(wd_lo[:, i:i + 2, :], wdn[:, i:i + 2, :], wd_hi[:, i:i + 2, :].bitcast(F32), ALU.subtract)

        hid = st.sb("hid", [P, 2, BANK])
        hid_hi, hid_lo = st.sb("hid_hi", [P, L0_FC, BANK], F32R), st.sb("hid_lo", [P, L0_FC, BANK], F32R)
        sg = st.sb("sg", [P, 2, BANK])
        up = [st.ps(f"up{i}") for i in range(2)]
        gate = [st.ps(f"gate{i}") for i in range(2)]
        down = [st.ps(f"down{i}") for i in range(2)]
        gate_ready, up_ready, silu_ready, hid_ready = st.sem("gate_ready"), st.sem("up_ready"), st.sem("silu_ready"), st.sem("hid_ready")
        down_ready, added, hhi_ready, hlo_ready = st.sem("down_ready"), st.sem("added"), st.sem("hhi_ready"), st.sem("hlo_ready")

        with nc.Block() as block:

            @block.tensor
            def _(pe):
                with pe.Fori(0, NJ) as j:
                    for f in range(L0_FC):
                        for hi, lo, psum, ready, used in ((wg_hi, wg_lo, gate, gate_ready, silu_ready), (wu_hi, wu_lo, up, up_ready, hid_ready)):
                            pe.wait_ge(used, j * L0_FC + f + 1)
                            split_product(pe, psum[f % 2][:, :], lambda c, hi=hi: hi[:, c, f * P:(f + 1) * P], lambda c, lo=lo: lo[:, c, f * P:(f + 1) * P],
                                          lambda c: k.XH[:, c, ds(j * BANK, BANK)], lambda c: k.XL[:, c, ds(j * BANK, BANK)]).then_inc(ready, 1)
                    for c in range(DC):
                        pe.wait_ge(added, j * DC + c + 1)
                        for f in range(L0_FC):
                            if c == 0:
                                pe.wait_ge(hlo_ready, j * L0_FC + f + 1 + 2)
                            for i, (w, x) in enumerate(((wd_hi, hid_hi), (wd_hi, hid_lo), (wd_lo, hid_hi))):
                                mm = pe.matmul(down[c][:, :], w[:, f, c * P:(c + 1) * P], x[:, f, :],
                                               start=(f == 0 and i == 0), stop=(f == L0_FC - 1 and i == 2))
                        mm.then_inc(down_ready, 1)

            @block.scalar
            def _(act):
                def keep_high(j, f):
                    act.wait_ge(hid_ready, j * L0_FC + f + 1 + 2)
                    act.activation(hid_hi[:, f, :], hid[:, f % 2, :], ACT.Copy).then_inc(hhi_ready, 1)

                act.sem_inc(silu_ready, 2)
                with act.Fori(0, NJ) as j:
                    for f in range(L0_FC):
                        act.wait_ge(gate_ready, j * L0_FC + f + 1)
                        act.wait_ge(hid_ready, j * L0_FC + f + 1)
                        act.activation(sg[:, f % 2, :], gate[f % 2][:, :], ACT.Silu, scale=s_gate[:, f:f + 1]).then_inc(silu_ready, 1)
                        if f > 0:
                            keep_high(j, f - 1)
                    keep_high(j, L0_FC - 1)

            @block.gpsimd
            def _(pool):
                pool.sem_inc(hlo_ready, 2)
                with pool.Fori(0, NJ) as j:
                    for f in range(L0_FC):
                        pool.wait_ge(hhi_ready, j * L0_FC + f + 1)
                        pool.tensor_tensor(hid_lo[:, f, :], hid[:, f % 2, :], hid_hi[:, f, :].bitcast(F32), ALU.subtract).then_inc(hlo_ready, 1)

            @block.vector
            def _(dve):
                dve.sem_inc(hid_ready, 2)
                dve.sem_inc(added, 1)
                with dve.Fori(0, NJ) as j:
                    for f in range(L0_FC):
                        dve.wait_ge(up_ready, j * L0_FC + f + 1)
                        dve.wait_ge(silu_ready, j * L0_FC + f + 1 + 2)
                        dve.wait_ge(hlo_ready, j * L0_FC + f + 1)
                        dve.scalar_tensor_tensor(out=hid[:, f % 2, :], in0=up[f % 2][:, :], scalar=s_up[:, f:f + 1],
                                                 in1=sg[:, f % 2, :], op0=ALU.mult, op1=ALU.mult).then_inc(hid_ready, 1)
                    for c in range(DC):
                        dve.wait_ge(down_ready, j * DC + c + 1)
                        x = k.XT[:, c, ds(j * BANK, BANK)]
                        dve.scalar_tensor_tensor(out=x, in0=down[c][:, :], scalar=s_down[:, c:c + 1], in1=x,
                                                 op0=ALU.mult, op1=ALU.add).then_inc(added, 1)



L1_HEADS, L1_HD = 16, 128
QUAD = 4
NZ = S // BANK
NQD = B * NZ


def l1_attn(nc, k, a):
    with Stage(nc, "l1a") as st:
        w3 = st.sb("w3", [P, 3, DC, P])
        w_hi, w_lo = st.sb("w_hi", [P, 3, DC, P], F32R), st.sb("w_lo", [P, 3, DC, P], F32R)
        wv = st.sb("wv", [P, DC, P])
        wo = st.sb("wo", [P, D])
        bias = st.sb("bias", [P, 3])
        bv = st.sb("bv", [P, P])
        mask = st.sb("mask", [P, P])
        grow = st.sb("grow", [P, P])
        gcol = st.sb("gcol", [P, 2])
        cosq, sinq = st.sb("cosq", [P, S]), st.sb("sinq", [P, S])
        cosk, sink = st.sb("cosk", [P, S]), st.sb("sink", [P, S])
        neghalf = st.sb("neghalf", [P, QUAD])
        qraw, kraw = st.sb("qraw", [P, 2, BANK]), st.sb("kraw", [P, 2, BANK])
        qc, kc = st.sb("qc", [P, 2, BANK]), st.sb("kc", [P, 2, BANK])
        qs, ks = st.sb("qs", [P, 2, BANK]), st.sb("ks", [P, 2, BANK])
        qT, kT, qdT = st.sb("qT", [P, 2, BANK]), st.sb("kT", [P, 2, BANK]), st.sb("qdT", [P, 2, BANK])
        v = st.sb("v", [P, 2, QUAD, P])
        ktok = st.sb("ktok", [P, 2, QUAD, P])
        smT = st.sb("smT", [P, 2, QUAD, P])
        state = st.sb("state", [P, 2, QUAD, P])
        sg = st.sb("sg", [P, 2, BANK])
        stats = st.sb("stats", [P, QUAD, 6])
        mv = st.sb("mv", [P, QUAD, 2])
        veps = st.sb("veps", [P, QUAD])
        rstd = st.sb("rstd", [P, QUAD])
        gn = st.sb("gn", [P, QUAD, P])
        gated = st.sb("gated", [P, 2, BANK])
        pq, pk, pg, pv = st.ps("pq"), st.ps("pk"), st.ps("pg"), st.ps("pv")
        psc, pkt, pds, pret = st.ps("psc"), st.ps("pkt"), st.ps("pds"), st.ps("pret")
        pgt, pout = pq, (pk, pg)

        loaded_w3, loaded_wo, loaded_hc, loaded_t = st.sem("loaded_w3"), st.sem("loaded_wo"), st.sem("loaded_hc"), st.sem("loaded_t")
        q_made, k_made, g_made, v_made = st.sem("q_made"), st.sem("k_made"), st.sem("g_made"), st.sem("v_made")
        sc_made, kt_made, ds_made, ret_made = st.sem("sc_made"), st.sem("kt_made"), st.sem("ds_made"), st.sem("ret_made")
        gt_made, out_made = st.sem("gt_made"), st.sem("out_made")
        q_kept, k_kept, silu_kept, kt_kept = st.sem("q_kept"), st.sem("k_kept"), st.sem("silu_kept"), st.sem("kt_kept")
        v_kept, q_rot, k_rot, sc_masked = st.sem("v_kept"), st.sem("q_rot"), st.sem("k_rot"), st.sem("sc_masked")
        states, linked, stat1, stat2, veps_ready = st.sem("states"), st.sem("linked"), st.sem("stat1"), st.sem("stat2"), st.sem("veps_ready")
        normed, gated_ready, added = st.sem("normed"), st.sem("gated_ready"), st.sem("added")
        q_cos, k_cos, q_roped, k_roped = st.sem("q_cos"), st.sem("k_cos"), st.sem("q_roped"), st.sem("k_roped")
        q_decayed, rstd_ready, half_set = st.sem("q_decayed"), st.sem("rstd_ready"), st.sem("half_set")
        measured = st.sem("measured")
        loaded_wv, whi_ready, wlo_ready = st.sem("loaded_wv"), st.sem("whi_ready"), st.sem("wlo_ready")
        NHC = 5

        def place(n):
            b, z = divmod(n, NZ)
            return b, z, b * S + z * BANK

        def steps(engine, step):
            for q in range(NQD):
                step(0, q)
            with engine.Fori(1, L1_HEADS) as h:
                for q in range(NQD):
                    step(h, q)

        with nc.Block() as block:

            @block.sync
            def _(sp):
                def load_head(h, q):
                    hh = ds(h, 1)
                    if q == 0:
                        wait(sp, wlo_ready, h)
                        sp.dma_start(w3[:, :, :, :], a["L1_w3"][hh].rearrange("a p t c n -> (a p) t c n")).then_inc(loaded_w3, 16)
                        wait(sp, v_made, NQD * h)
                        sp.dma_start(wv[:, :, :], a["L1_wv"][hh].rearrange("a p c n -> (a p) c n")).then_inc(loaded_wv, 16)
                    if q == 1:
                        wait(sp, silu_kept, NQD * h)
                        wait(sp, kt_kept, NQD * h)
                        wait(sp, q_decayed, NQD * h)
                        wait(sp, states, NQD * h)
                        sp.dma_start(bias[:, :], a["L1_bias"][hh].rearrange("a p n -> (a p) n")).then_inc(loaded_hc, 16)
                        sp.dma_start(bv[:, :], a["L1_attn_bv"][hh, :].to_broadcast([P, P])).then_inc(loaded_hc, 16)
                        sp.dma_start(mask[:, :], a["c_l1_mask"][hh].rearrange("a p n -> (a p) n")).then_inc(loaded_hc, 16)
                        sp.dma_start(grow[:, :], a["c_l1_grow"][hh, :].to_broadcast([P, P])).then_inc(loaded_hc, 16)
                        sp.dma_start(gcol[:, :], a["c_l1_gcol"][hh].rearrange("a p n -> (a p) n")).then_inc(loaded_hc, 16)
                    if q == 2:
                        wait(sp, out_made, 2 * NQD * h)
                        sp.dma_start(wo[:, :], a["L1_attn_Wo"][ds(h * P, P), :]).then_inc(loaded_wo, 16)

                load_head(0, 0)
                load_head(0, 1)
                sp.dma_start(cosq[:, :], a["c_l1_rope"][0]).then_inc(loaded_t, 16)
                sp.dma_start(sinq[:, :], a["c_l1_rope"][1]).then_inc(loaded_t, 16)
                sp.dma_start(cosk[:, :], a["c_l1_rope"][2]).then_inc(loaded_t, 16)
                sp.dma_start(sink[:, :], a["c_l1_rope"][3]).then_inc(loaded_t, 16)
                load_head(0, 2)
                with sp.Fori(1, L1_HEADS) as h:
                    for q in range(3):
                        load_head(h, q)
                sp.wait_ge(wlo_ready, L1_HEADS)
                sp.dma_start(w3[:, :, :, :], a["L1_w3"][0]).then_inc(loaded_w3, 16)

            @block.tensor
            def _(pe):
                def project(h, q, which):
                    n, o = h * NQD + q, q % 2
                    b, z, c0 = place(q)
                    if q == 0:
                        pe.wait_ge(wlo_ready, h + 1)
                    for i, bank, made, used, count in ((1, pk, k_made, added, 2 * (n - 2) + 1), (0, pq, q_made, gated_ready, n - 1),
                                                       (2, pg, g_made, added, 2 * (n - 2) + 2)):
                        if i not in which:
                            continue
                        wait(pe, used, count)
                        split_product(pe, bank[:, :], lambda c, i=i: w_hi[:, i, c, :], lambda c, i=i: w_lo[:, i, c, :],
                                      lambda c: k.XH[:, c, c0:c0 + BANK], lambda c: k.XL[:, c, c0:c0 + BANK]).then_inc(made, 1)
                    if 3 not in which:
                        return
                    wait(pe, v_kept, n)
                    if q == 0:
                        pe.wait_ge(loaded_wv, 16 * h + 16)
                    for t in range(QUAD):
                        for c in range(DC):
                            mm = pe.matmul(pv[:, t * P:(t + 1) * P], k.XN[:, c, c0 + t * P:c0 + (t + 1) * P], wv[:, c, :],
                                           start=(c == 0), stop=(c == DC - 1))
                    mm.then_inc(v_made, 1)

                def retain(h, q):
                    n, o = h * NQD + q, q % 2
                    b, z, c0 = place(q)
                    wait(pe, normed, n)
                    pe.wait_ge(sc_masked, n + 1)
                    pe.wait_ge(q_decayed, n + 1)
                    pe.wait_ge(states, n + 1)
                    for t in range(QUAD):
                        inter = t > 0 or z > 0
                        mm = pe.matmul(pret[:, t * P:(t + 1) * P], smT[:, o, t, :], v[:, o, t, :], start=True, stop=not inter)
                        if inter:
                            mm = pe.matmul(pret[:, t * P:(t + 1) * P], qdT[:, o, t * P:(t + 1) * P], state[:, o, t, :],
                                           start=False, stop=True)
                    mm.then_inc(ret_made, 1)

                def turn_keys(h, q):
                    n, o = h * NQD + q, q % 2
                    pe.wait_ge(k_roped, n + 1)
                    wait(pe, kt_kept, n)
                    for t in range(QUAD):
                        mm = pe.transpose(pkt[:, t * P:(t + 1) * P], kT[:, o, t * P:(t + 1) * P], k.ident[:, :])
                    mm.then_inc(kt_made, 1)

                def scores(h, q):
                    n, o = h * NQD + q, q % 2
                    pe.wait_ge(q_roped, n + 1)
                    wait(pe, sc_masked, n)
                    for t in range(QUAD):
                        mm = pe.matmul(psc[:, t * P:(t + 1) * P], kT[:, o, t * P:(t + 1) * P], qT[:, o, t * P:(t + 1) * P],
                                       start=True, stop=True)
                    mm.then_inc(sc_made, 1)

                def state_sums(h, q):
                    n, o = h * NQD + q, q % 2
                    pe.wait_ge(kt_kept, n + 1)
                    pe.wait_ge(v_kept, n + 1)
                    wait(pe, states, n)
                    for t in range(QUAD):
                        mm = pe.matmul(pds[:, t * P:(t + 1) * P], ktok[:, o, t, :], v[:, o, t, :], start=True, stop=True)
                    mm.then_inc(ds_made, 1)

                def turn_normed(h, q):
                    n = h * NQD + q
                    pe.wait_ge(q_kept, n + 2)
                    pe.wait_ge(normed, n + 1)
                    for t in range(QUAD):
                        mm = pe.transpose(pgt[:, t * P:(t + 1) * P], gn[:, t, :], k.ident[:, :])
                    mm.then_inc(gt_made, 1)

                def output(h, q):
                    n, o = h * NQD + q, q % 2
                    if q == 0:
                        pe.wait_ge(loaded_wo, 16 * h + 16)
                    pe.wait_ge(gated_ready, n + 1)
                    for c in range(DC):
                        pe.matmul(pout[c][:, :], wo[:, c * P:(c + 1) * P], gated[:, o, :], start=True, stop=True).then_inc(out_made, 1)

                def before(h, q):
                    return (h, q - 1) if q else (h - 1, NQD - 1)

                def step(h, q):
                    n = h * NQD + q
                    project(h, q, (0, 1))
                    first = isinstance(h, int) and n == 0
                    if not first:
                        retain(*before(h, q))
                    project(h, q, (2, 3))
                    turn_keys(h, q)
                    scores(h, q)
                    state_sums(h, q)
                    if not first:
                        turn_normed(*before(h, q))
                        pe.wait_ge(k_kept, n + 1)
                        pe.wait_ge(silu_kept, n + 1)
                        output(*before(h, q))

                steps(pe, step)
                retain(L1_HEADS - 1, NQD - 1)
                n = L1_HEADS * NQD - 1
                pe.wait_ge(normed, n + 1)
                for t in range(QUAD):
                    mm = pe.transpose(pgt[:, t * P:(t + 1) * P], gn[:, t, :], k.ident[:, :])
                mm.then_inc(gt_made, 1)
                output(L1_HEADS - 1, NQD - 1)

            @block.scalar
            def _(act):
                def split_weights(h):
                    act.wait_ge(loaded_w3, 16 * h + 16)
                    wait(act, g_made, NQD * h)
                    act.activation(w_hi[:, :, :, :], w3[:, :, :, :], ACT.Copy).then_inc(whi_ready, 1)

                split_weights(0)

                def step(h, q):
                    n, o = h * NQD + q, q % 2
                    if q == 0:
                        act.wait_ge(loaded_hc, 16 * NHC * (h + 1))
                    act.wait_ge(k_made, n + 1)
                    wait(act, k_rot, n - 1)
                    wait(act, k_cos, n - 1)
                    act.activation(kraw[:, o, :], pk[:, :], ACT.Identity, bias=bias[:, 1:2]).then_inc(k_kept, 1)
                    act.wait_ge(q_made, n + 1)
                    wait(act, q_rot, n - 1)
                    wait(act, q_cos, n - 1)
                    act.activation(qraw[:, o, :], pq[:, :], ACT.Identity, bias=bias[:, 0:1]).then_inc(q_kept, 1)
                    act.wait_ge(g_made, n + 1)
                    wait(act, gated_ready, n - 1)
                    act.activation(sg[:, o, :], pg[:, :], ACT.Silu, bias=bias[:, 2:3]).then_inc(silu_kept, 1)
                    if q == NQD - 1:
                        split_weights(h + 1)
                    act.wait_ge(kt_made, n + 1)
                    wait(act, ds_made, n - 1)
                    act.activation(ktok[:, o, :, :], pkt[:, :].rearrange("p (t n) -> p t n", t=QUAD), ACT.Copy,
                                   scale=gcol[:, 0:1]).then_inc(kt_kept, 1)

                steps(act, step)

            @block.gpsimd
            def _(pool):
                pool.memset(neghalf[:, :], -0.5).then_inc(half_set, 1)
                def split_weights(h):
                    pool.wait_ge(whi_ready, h + 1)
                    pool.tensor_tensor(w_lo[:, :, :, :], w3[:, :, :, :], w_hi[:, :, :, :].bitcast(F32), ALU.subtract).then_inc(wlo_ready, 1)

                split_weights(0)
                pool.wait_ge(loaded_t, 64)
                pool.wait_ge(half_set, 1)

                def invert_std(n):
                    pool.wait_ge(veps_ready, n + 1)
                    wait(pool, normed, n)
                    pool.tensor_tensor(rstd[:, :], veps[:, :], neghalf[:, :], ALU.pow).then_inc(rstd_ready, 1)

                def step(h, q):
                    n, o = h * NQD + q, q % 2
                    b, z, c0 = place(q)
                    tok = slice(z * BANK, (z + 1) * BANK)
                    pool.wait_ge(k_kept, n + 1)
                    wait(pool, k_roped, n - 1)
                    pool.tensor_tensor(kc[:, o, :], kraw[:, o, :], cosk[:, tok], ALU.mult).then_inc(k_cos, 1)
                    pool.wait_ge(q_kept, n + 1)
                    pool.tensor_tensor(qc[:, o, :], qraw[:, o, :], cosq[:, tok], ALU.mult).then_inc(q_cos, 1)
                    pool.wait_ge(q_rot, n + 1)
                    pool.wait_ge(q_cos, n + 1)
                    wait(pool, sc_made, n - 1)
                    pool.tensor_tensor(qT[:, o, :], qc[:, o, :], qs[:, o, :], ALU.add).then_inc(q_roped, 1)
                    if not (isinstance(h, int) and n == 0):
                        invert_std(n - 1)
                    pool.wait_ge(q_roped, n + 1)
                    wait(pool, ret_made, n - 1)
                    if q == 0:
                        pool.wait_ge(loaded_hc, 16 * NHC * (h + 1))
                    pool.tensor_tensor(qdT[:, o, :].rearrange("p (t n) -> p t n", t=QUAD), qT[:, o, :].rearrange("p (t n) -> p t n", t=QUAD),
                                       grow[:, :].unsqueeze(1).to_broadcast([P, QUAD, P]), ALU.mult).then_inc(q_decayed, 1)
                    if q == NQD - 1:
                        split_weights(h + 1)

                steps(pool, step)
                invert_std(L1_HEADS * NQD - 1)

            @block.vector
            def _(dve):
                HALF = P // 2

                def rotate(n, o, z, raw, sin, out, kept, roped, done):
                    tok = slice(z * BANK, (z + 1) * BANK)
                    dve.wait_ge(kept, n + 1)
                    wait(dve, roped, n - 1)
                    dve.tensor_tensor(out[0:HALF, o, :], raw[HALF:P, o, :], sin[HALF:P, tok], ALU.mult)
                    dve.tensor_tensor(out[HALF:P, o, :], raw[0:HALF, o, :], sin[0:HALF, tok], ALU.mult).then_inc(done, 1)

                def measure(n):
                    dve.wait_ge(ret_made, n + 1)
                    for t in range(QUAD):
                        dve.bn_stats(stats[:, t, :], pret[:, t * P:(t + 1) * P]).then_inc(stat1, 1)

                def aggregate(n):
                    dve.wait_ge(stat1, QUAD * n + QUAD)
                    dve.sem_inc(measured, 1)
                    for t in range(QUAD):
                        dve.bn_aggr(mv[:, t, :], stats[:, t, :]).then_inc(stat2, 1)
                    dve.wait_ge(stat2, QUAD * n + QUAD)
                    dve.tensor_scalar(veps[:, :], mv[:, :, 1], EPS, None, ALU.add).then_inc(veps_ready, 1)

                def normalise(n):
                    dve.wait_ge(rstd_ready, n + 1)
                    wait(dve, gt_made, n)
                    for t in range(QUAD):
                        op = dve.tensor_scalar(gn[:, t, :], pret[:, t * P:(t + 1) * P], mv[:, t, 0:1], rstd[:, t:t + 1],
                                               ALU.subtract, ALU.mult)
                    op.then_inc(normed, 1)

                def gate(n, o):
                    dve.wait_ge(gt_made, n + 1)
                    dve.wait_ge(silu_kept, n + 1)
                    wait(dve, out_made, 2 * (n - 1))
                    dve.tensor_tensor(gated[:, o, :], pgt[:, :], sg[:, o, :], ALU.mult).then_inc(gated_ready, 1)

                def add(n, c0):
                    for c in range(DC):
                        dve.wait_ge(out_made, 2 * n + c + 1)
                        x = k.XT[:, c, c0:c0 + BANK]
                        dve.tensor_tensor(x, x, pout[c][:, :], ALU.add).then_inc(added, 1)

                def chain(h, q):
                    n, o = h * NQD + q, q % 2
                    b, z, _ = place(q)
                    base = (h * B + b) * (2 * QUAD - 3) + z * (QUAD - 1)
                    dve.wait_ge(ds_made, n + 1)
                    for t in range(QUAD if z + 1 < NZ else QUAD - 1):
                        out = state[:, o, t + 1, :] if t + 1 < QUAD else state[:, 1 - o, 0, :]
                        if t == 0 and z == 0:
                            op = dve.tensor_copy(out, pds[:, 0:P])
                        else:
                            if t:
                                dve.wait_ge(linked, base + t)
                            else:
                                dve.wait_ge(states, n)
                            op = dve.scalar_tensor_tensor(out=out, in0=state[:, o, t, :], scalar=gcol[:, 1:2], in1=pds[:, t * P:(t + 1) * P],
                                                          op0=ALU.mult, op1=ALU.add)
                        last = t == (QUAD - 1 if z + 1 < NZ else QUAD - 2)
                        op.then_inc(states if last else linked, 1)

                def step(h, q):
                    n, o = h * NQD + q, q % 2
                    b, z, c0 = place(q)
                    first = isinstance(h, int) and n == 0
                    rotate(n, o, z, kraw, sink, ks, k_kept, k_roped, k_rot)
                    dve.wait_ge(k_cos, n + 1)
                    dve.wait_ge(k_rot, n + 1)
                    wait(dve, sc_made, n - 1)
                    dve.tensor_tensor(kT[:, o, :], kc[:, o, :], ks[:, o, :], ALU.add).then_inc(k_roped, 1)
                    rotate(n, o, z, qraw, sinq, qs, q_kept, q_roped, q_rot)
                    if not first:
                        measure(n - 1)
                        aggregate(n - 1)
                    dve.wait_ge(v_made, n + 1)
                    wait(dve, ret_made, n - 1)
                    if q == 0:
                        dve.wait_ge(loaded_hc, 16 * NHC * (h + 1))
                    dve.tensor_tensor(v[:, o, :, :], pv[:, :].rearrange("p (t n) -> p t n", t=QUAD),
                                      bv[:, :].unsqueeze(1).to_broadcast([P, QUAD, P]), ALU.add).then_inc(v_kept, 1)
                    if not first:
                        normalise(n - 1)
                    dve.wait_ge(sc_made, n + 1)
                    dve.tensor_tensor(smT[:, o, :, :], psc[:, :].rearrange("p (t n) -> p t n", t=QUAD),
                                      mask[:, :].unsqueeze(1).to_broadcast([P, QUAD, P]), ALU.mult).then_inc(sc_masked, 1)
                    if not first:
                        gate(n - 1, 1 - o)
                    chain(h, q)
                    if not first:
                        add(n - 1, place((q - 1) % NQD)[2])

                dve.wait_ge(loaded_t, 64)
                steps(dve, step)
                n = L1_HEADS * NQD - 1
                measure(n)
                aggregate(n)
                normalise(n)
                gate(n, n % 2)
                add(n, place(NQD - 1)[2])


def l1_constants():
    f = np.float32
    pos = np.arange(S, dtype=f)
    inv_freq = (1.0 / f(10000.0) ** (np.arange(0, L1_HD, 2, dtype=f) / f(L1_HD))).astype(f)
    ang = (inv_freq[:, None] * pos[None, :]).astype(f)
    sbase = ((np.arange(0, L1_HD, 2, dtype=f) + f(0.4 * L1_HD)) / f(1.4 * L1_HD)).astype(f)
    power = ((pos - S // 2) / f(512.0)).astype(f)
    scale = (sbase[:, None] ** power[None, :]).astype(f)
    both = lambda m: np.concatenate([m, m]).astype(f)
    cross = lambda m: np.concatenate([m, -m]).astype(f)
    cos, sin = np.cos(ang), np.sin(ang)
    rope = np.stack([both(cos * scale), cross(sin * scale), both(cos / scale), cross(sin / scale)])
    gamma = 1.0 - 2.0 ** (-5.0 - np.arange(L1_HEADS, dtype=np.float64))
    i = np.arange(P)
    d = i[None, :] - i[:, None]
    mask = np.where(d >= 0, gamma[:, None, None] ** np.maximum(d, 0), 0.0)
    grow = gamma[:, None] ** (i + 1)[None, :]
    gcol = np.stack([gamma[:, None] ** (P - 1 - i)[None, :], np.repeat(gamma[:, None] ** P, P, 1)], axis=2)
    return {"c_l1_rope": rope, "c_l1_mask": mask.astype(f), "c_l1_grow": grow.astype(f), "c_l1_gcol": gcol.astype(f)}


def l1_layout(x):
    order = np.concatenate([np.arange(0, L1_HD, 2), np.arange(1, L1_HD, 2)])
    w = lambda m: m.reshape(DC, P, L1_HEADS, L1_HD).transpose(2, 1, 0, 3)
    w3 = np.stack([w(x["L1_attn_Wq"])[..., order], w(x["L1_attn_Wk"])[..., order], w(x["L1_attn_Wg"])], axis=2)
    b = lambda v: v.reshape(L1_HEADS, L1_HD)
    bias = np.stack([b(x["L1_attn_bq"])[:, order], b(x["L1_attn_bk"])[:, order], b(x["L1_attn_bg"])], axis=2)
    return {"L1_w3": w3, "L1_wv": w(x["L1_attn_Wv"]), "L1_bias": bias, "L1_attn_bv": b(x["L1_attn_bv"]), "L1_attn_Wo": x["L1_attn_Wo"]}


def linear(nc, k, name, x, w, scale, bias):
    with Stage(nc, name) as st:
        acc = [st.ps(f"acc{i}") for i in range(4)]
        out = st.sb("out", [P, 2, BANK])
        made, scaled, added = st.sem("made"), st.sem("scaled"), st.sem("added")
        jobs = [(j, c) for j in range(NJ) for c in range(DC)]
        with nc.Block() as block:

            @block.tensor
            def _(pe):
                for n, (j, c) in enumerate(jobs):
                    wait(pe, scaled, n - 3)
                    for i in range(DC):
                        mm = pe.matmul(acc[n % 4][:, :], w[:, i, c * P:(c + 1) * P], x[:, i, j * BANK:(j + 1) * BANK],
                                       start=(i == 0), stop=(i == DC - 1))
                    mm.then_inc(made, 1)

            @block.scalar
            def _(act):
                for n, (j, c) in enumerate(jobs):
                    act.wait_ge(made, n + 1)
                    wait(act, added, n - 1)
                    act.activation(out[:, n % 2, :], acc[n % 4][:, :], ACT.Identity, bias=bias[:, c:c + 1],
                                   scale=scale[:, c:c + 1]).then_inc(scaled, 1)

            @block.vector
            def _(dve):
                for n, (j, c) in enumerate(jobs):
                    dve.wait_ge(scaled, n + 1)
                    t = k.XT[:, c, j * BANK:(j + 1) * BANK]
                    dve.tensor_tensor(t, t, out[:, n % 2, :], ALU.add).then_inc(added, 1)


def l1_ffn(nc, k, a):
    with Stage(nc, "l1f") as st:
        X2 = st.sb("X2", [P, DC, T])
        w = st.sb("w", [P, DC, D])
        sgn = st.sb("sgn", [P, 2, DC, D])
        v = st.sb("v", [P, 6, DC])
        top = st.sb("top", [P, 4])
        norm_stage(nc, k, "l1n", k.XN, X2)
        with Stage(nc, "l1p") as s2:
            loaded, tops, alltop, signs, done = s2.sem("loaded"), s2.sem("tops"), s2.sem("alltop"), s2.sem("signs"), s2.sem("done")
            with nc.Block() as block:

                @block.sync
                def _(sp):
                    sp.dma_start(w[:, :, :], rows(a["L1_ffn_weightT"])).then_inc(loaded, 16)
                    sp.dma_start(v[:, 0:5, :], a["L1_ffn_cols"]).then_inc(loaded, 16)

                @block.vector
                def _(dve):
                    dve.wait_ge(loaded, 32)
                    dve.tensor_reduce(top[:, 0:1], w[:, :, :], mybir.AxisListType.XY, ALU.max).then_inc(tops, 1)
                    dve.tensor_reduce(top[:, 1:2], w[:, :, :], mybir.AxisListType.XY, ALU.min).then_inc(tops, 1)
                    dve.tensor_scalar(sgn[:, 0, :, :], w[:, :, :], 0.0, None, ALU.is_gt).then_inc(signs, 1)
                    dve.tensor_scalar(sgn[:, 1, :, :], w[:, :, :], 0.0, None, ALU.is_lt).then_inc(signs, 1)
                    dve.tensor_tensor(v[:, 1, :], v[:, 1, :], v[:, 4, :], ALU.add)
                    dve.wait_ge(tops, 2)
                    dve.scalar_tensor_tensor(out=top[:, 2:3], in0=top[:, 1:2], scalar=-1.0, in1=top[:, 0:1],
                                             op0=ALU.mult, op1=ALU.max).then_inc(tops, 1)
                    dve.wait_ge(signs, 2)
                    dve.tensor_tensor(sgn[:, 0, :, :], sgn[:, 0, :, :], sgn[:, 1, :, :], ALU.subtract)
                    for c in range(DC):
                        dve.tensor_scalar(X2[:, c, :], X2[:, c, :], v[:, 2, c:c + 1], v[:, 3, c:c + 1], ALU.mult, ALU.add)
                    dve.wait_ge(alltop, 1)
                    dve.tensor_scalar(v[:, 0, :], v[:, 0, :], top[:, 3:4], None, ALU.mult)

                @block.gpsimd
                def _(pool):
                    pool.wait_ge(tops, 3)
                    pool.partition_all_reduce(top[:, 3:4], top[:, 2:3], P, bass.bass_isa.ReduceOp.max).then_inc(alltop, 1)

        linear(nc, k, "l1l", X2, sgn[:, 0, :, :], v[:, 0, :], v[:, 1, :])


def l2_ffn(nc, k, a):
    with Stage(nc, "l2f") as st:
        w = st.sb("w", [P, DC, D])
        t = st.sb("t", [P, 2, DC, D])
        sc = st.sb("sc", [P, DC])
        bias = st.sb("bias", [P, DC])
        with Stage(nc, "l2p") as s2:
            pa = s2.ps("pa")
            loaded, absd, mean_made, steps = s2.sem("loaded"), s2.sem("absd"), s2.sem("mean_made"), s2.sem("steps")
            with nc.Block() as block:

                @block.sync
                def _(sp):
                    sp.dma_start(w[:, :, :], rows(a["L2_ffn_weightT"])).then_inc(loaded, 16)
                    sp.dma_start(bias[:, :], a["L2_ffn_bias_cols"]).then_inc(loaded, 16)

                @block.tensor
                def _(pe):
                    pe.wait_ge(absd, 1)
                    for c in range(DC):
                        mm = pe.matmul(pa[:, 0:D], k.avg[:, :], t[:, 0, c, :], start=(c == 0), stop=(c == DC - 1))
                    mm.then_inc(mean_made, 1)

                @block.vector
                def _(dve):
                    dve.memset(sc[:, :], 1.0)
                    dve.wait_ge(loaded, 32)
                    dve.scalar_tensor_tensor(out=t[:, 0, :, :], in0=w[:, :, :], scalar=-1.0, in1=w[:, :, :],
                                             op0=ALU.mult, op1=ALU.max).then_inc(absd, 1)
                    dve.tensor_scalar(t[:, 1, :, :], w[:, :, :], 0.0, None, ALU.is_ge).then_inc(steps, 1)
                    dve.wait_ge(steps, 1)
                    dve.tensor_scalar(t[:, 1, :, :], t[:, 1, :, :], 2.0, -1.0, ALU.mult, ALU.add).then_inc(steps, 1)
                    dve.wait_ge(steps, 2)
                    dve.wait_ge(mean_made, 1)
                    for c in range(DC):
                        dve.tensor_tensor(t[:, 1, c, :], t[:, 1, c, :], pa[:, 0:D], ALU.mult).then_inc(steps, 1)
                    dve.wait_ge(steps, 4)
                    dve.tensor_tensor(t[:, 1, :, :], t[:, 1, :, :], w[:, :, :], ALU.subtract).then_inc(steps, 1)
                    dve.wait_ge(steps, 5)
                    dve.tensor_tensor(t[:, 1, :, :], t[:, 1, :, :], w[:, :, :], ALU.add)

        linear(nc, k, "l2l", k.XN, t[:, 1, :, :], sc, bias)


L2_HEADS, L2_HD = 16, 16
L2_W = 32
L2_HPC = P // L2_HD
L2_SCALE = L2_HD ** -0.5
SPLIT = 4 * L2_HD
L2_N = L2_HEADS * B


def l2_attn(nc, k, a):
    split = nc.dram_tensor("l2_split", [2, 4, D, T], F32, kind="Internal").ap()
    with Stage(nc, "l2a") as st:
        VA = st.sb("VA", [P, TT, L2_HEADS, L2_W])
        mem = st.sb("mem", [P, DC, T])
        gate = st.sb("gate", [P, 2, DC])
        with Stage(nc, "l2q") as s2:
            QF = s2.sb("QF", [P, DC, T])
            KF = s2.sb("KF", [P, DC, T])
            hi, lo = s2.sb("hi", [P, 2, DC, BANK], F32R), s2.sb("lo", [P, 2, DC, BANK], F32R)
            hi_stored, lo_stored = [s2.sem(f"hi_stored{i}") for i in range(2)], [s2.sem(f"lo_stored{i}") for i in range(2)]
            l2_project(nc, k, a, split, VA, QF, KF, hi, lo, hi_stored, lo_stored)
            l2_memory(nc, k, a, VA, QF, KF, mem, gate, hi_stored + lo_stored)
        CT = st.sb("CT", [P, TT, D])
        l2_heads(nc, k, split, VA, CT)
        l2_output(nc, k, a, CT, mem, gate)


def l2_project(nc, k, a, split, VA, QF, KF, hi, lo, hi_stored, lo_stored):
    with Stage(nc, "l2p") as st:
        w = st.sb("w", [P, 3, DC, D])
        cos, sin = st.sb("cos", [P, S]), st.sb("sin", [P, S])
        xc, xs = st.sb("xc", [P, 2, DC, BANK]), st.sb("xs", [P, 2, DC, BANK])
        rot = st.sb("rot", [P, 2, DC, BANK])
        low, ex = st.sb("low", [P, DC, BANK]), st.sb("ex", [P, DC, BANK])
        acc = [st.ps(f"acc{i}") for i in range(4)]
        vacc = [st.ps(f"vacc{i}") for i in range(2)]
        loaded, rope_loaded, made, turned, roped = st.sem("loaded"), st.sem("rope_loaded"), st.sem("made"), st.sem("turned"), st.sem("roped")
        hi_ready, lo_ready = st.sem("hi_ready"), st.sem("lo_ready")
        low_ready, ex_ready, feat = st.sem("low_ready"), st.sem("ex_ready"), st.sem("feat")
        v_made, v_kept = st.sem("v_made"), st.sem("v_kept")
        jobs = [(m, j) for j in range(NJ) for m in range(2)]

        with nc.Block() as block:

            @block.sync
            def _(sp):
                sp.dma_start(w[:, :, :, :], a["L2_w3"]).then_inc(loaded, 16)
                sp.dma_start(cos[:, :], a["c_l2_rope"][0]).then_inc(rope_loaded, 16)
                sp.dma_start(sin[:, :], a["c_l2_rope"][1]).then_inc(rope_loaded, 16)
                for n, (m, j) in enumerate(jobs):
                    tok = slice(j * BANK, (j + 1) * BANK)
                    sp.wait_ge(hi_ready, n + 1)
                    for part in ((0, 1), (0, 2))[m]:
                        sp.dma_start(rows(split[m, part])[:, :, tok], hi[:, n % 2, :, :].bitcast(F32)).then_inc(hi_stored[n % 2], 16)
                    sp.wait_ge(lo_ready, n + 1)
                    for part in ((2, 3), (1, 3))[m]:
                        sp.dma_start(rows(split[m, part])[:, :, tok], lo[:, n % 2, :, :].bitcast(F32)).then_inc(lo_stored[n % 2], 16)

            @block.tensor
            def _(pe):
                pe.wait_ge(loaded, 16)
                for n, (m, j) in enumerate(jobs):
                    wait(pe, turned, n - 1)
                    for o in range(DC):
                        for c in range(DC):
                            mm = pe.matmul(acc[n % 2 * 2 + o][:, :], w[:, m, c, o * P:(o + 1) * P], k.XN[:, c, j * BANK:(j + 1) * BANK],
                                           start=(c == 0), stop=(c == DC - 1))
                    mm.then_inc(made, 1)
                    for t in (2 * n, 2 * n + 1):
                        wait(pe, v_kept, t - 1)
                        for c in range(DC):
                            mm = pe.matmul(vacc[t % 2][:, 0:D], k.XN[:, c, t * P:(t + 1) * P], w[:, 2, c, :],
                                           start=(c == 0), stop=(c == DC - 1))
                        mm.then_inc(v_made, 1)

            @block.vector
            def _(dve):
                dve.wait_ge(rope_loaded, 32)

                def turn(n):
                    j = jobs[n][1]
                    A, Bk = acc[n % 2 * 2], acc[n % 2 * 2 + 1]
                    pos = slice(j * BANK % S, j * BANK % S + BANK)
                    dve.wait_ge(made, n + 1)
                    wait(dve, roped, n - 1)
                    dve.tensor_tensor(xc[:, n % 2, 0, :], A[:, :], cos[:, pos], ALU.mult)
                    dve.tensor_tensor(xc[:, n % 2, 1, :], Bk[:, :], cos[:, pos], ALU.mult)
                    dve.tensor_tensor(xs[:, n % 2, 0, :], Bk[:, :], sin[:, pos], ALU.mult)
                    dve.tensor_tensor(xs[:, n % 2, 1, :], A[:, :], sin[:, pos], ALU.mult).then_inc(turned, 1)

                turn(0)
                for n, (m, j) in enumerate(jobs):
                    f = (QF, KF)[m]
                    tok = slice(j * BANK, (j + 1) * BANK)
                    if n + 1 < len(jobs):
                        turn(n + 1)
                    dve.wait_ge(roped, n + 1)
                    wait(dve, ex_ready, n)
                    dve.tensor_scalar(low[:, :, :], rot[:, n % 2, :, :], 0.0, None, ALU.min).then_inc(low_ready, 1)
                    dve.wait_ge(hi_ready, n + 1)
                    wait(dve, lo_stored[n % 2], 32 * (n // 2))
                    dve.tensor_tensor(lo[:, n % 2, :, :], rot[:, n % 2, :, :], hi[:, n % 2, :, :].bitcast(F32), ALU.subtract).then_inc(lo_ready, 1)
                    dve.wait_ge(ex_ready, n + 1)
                    dve.scalar_tensor_tensor(out=f[:, :, tok], in0=rot[:, n % 2, :, :], scalar=0.0, in1=ex[:, :, :],
                                             op0=ALU.max, op1=ALU.add).then_inc(feat, 1)

            @block.gpsimd
            def _(pool):
                pool.memset(VA[:, :, :, L2_HD:L2_HD + 1], 1.0)
                pool.memset(VA[:, :, :, L2_HD + 1:L2_W], 0.0)
                for n, (m, j) in enumerate(jobs):
                    pool.wait_ge(turned, n + 1)
                    wait(pool, feat, n - 1)
                    wait(pool, hi_ready, n - 1)
                    pool.tensor_tensor(rot[:, n % 2, 0, :], xc[:, n % 2, 0, :], xs[:, n % 2, 0, :], ALU.subtract)
                    pool.tensor_tensor(rot[:, n % 2, 1, :], xc[:, n % 2, 1, :], xs[:, n % 2, 1, :], ALU.add).then_inc(roped, 1)

            @block.scalar
            def _(act):
                for n, (m, j) in enumerate(jobs):
                    for t in (2 * n, 2 * n + 1):
                        act.wait_ge(v_made, t + 1)
                        act.activation(VA[:, t, :, 0:L2_HD], vacc[t % 2][:, 0:D].rearrange("p (h e) -> p h e", h=L2_HEADS),
                                       ACT.Copy).then_inc(v_kept, 1)
                    act.wait_ge(roped, n + 1)
                    wait(act, hi_stored[n % 2], 32 * (n // 2))
                    act.activation(hi[:, n % 2, :, :], rot[:, n % 2, :, :], ACT.Copy).then_inc(hi_ready, 1)
                    act.wait_ge(low_ready, n + 1)
                    wait(act, feat, n)
                    act.activation(ex[:, :, :], low[:, :, :], ACT.Exp).then_inc(ex_ready, 1)


def l2_memory(nc, k, a, VA, QF, KF, mem, gate, split_stored):
    with Stage(nc, "l2m") as st:
        blk = st.sb("blk", [P, P])
        ones = st.sb("ones", [P, P])
        ktok = st.sb("ktok", [P, 2, BANK])
        M, N = st.sb("M", [P, 2, P]), st.sb("N", [P, 2, P])
        raw = st.sb("raw", [P, DC])
        inv = st.sb("inv", [P, 2, BANK])
        ptr = [st.ps(f"ptr{i}") for i in range(2)]
        pm, pn = st.ps("pm"), st.ps("pn")
        num, den = [st.ps(f"num{i}") for i in range(2)], [st.ps(f"den{i}") for i in range(2)]
        loaded, set_up, turned, kept = st.sem("loaded"), st.sem("set_up"), st.sem("turned"), st.sem("kept")
        summed, masked, out_made, inv_ready, used, gates = st.sem("summed"), st.sem("masked"), st.sem("out_made"), st.sem("inv_ready"), st.sem("used"), st.sem("gates")
        jobs = [(b, c) for b in range(B) for c in range(DC)]
        QT_ = NQ // 4

        with nc.Block() as block:

            @block.sync
            def _(sp):
                sp.dma_start(blk[:, :], a["c_l2_block"]).then_inc(loaded, 16)
                sp.dma_start(raw[:, :], a["L2_gate_cols"]).then_inc(loaded, 16)
                for sem in split_stored:
                    sp.wait_ge(sem, 16 * 2 * NJ)

            @block.scalar
            def _(act):
                for n in range(len(jobs) * QT_):
                    act.wait_ge(turned, n + 1)
                    wait(act, summed, n - 1)
                    act.activation(ktok[:, n % 2, :], ptr[n % 2][:, :], ACT.Copy).then_inc(kept, 1)
                    if n == QT_ - 1:
                        act.wait_ge(loaded, 32)
                        act.activation(gate[:, 0, :], raw[:, :], ACT.Sigmoid).then_inc(gates, 1)

            @block.tensor
            def _(pe):
                def outputs(n):
                    b, c = jobs[n]
                    pe.wait_ge(masked, n + 1)
                    for z in range(NZ):
                        i = n * NZ + z
                        wait(pe, used, i - 1)
                        f = QF[:, c, b * S + z * BANK:b * S + (z + 1) * BANK]
                        pe.matmul(num[i % 2][:, :], M[:, n % 2, :], f, start=True, stop=True)
                        pe.matmul(den[i % 2][:, :], N[:, n % 2, :], f, start=True, stop=True).then_inc(out_made, 1)

                pe.wait_ge(set_up, 1)
                for n, (b, c) in enumerate(jobs):
                    for g in range(QT_):
                        i = n * QT_ + g
                        wait(pe, kept, i - 1)
                        for t in range(4):
                            lo = b * S + (g * 4 + t) * P
                            mm = pe.transpose(ptr[i % 2][:, t * P:(t + 1) * P], KF[:, c, lo:lo + P], k.ident[:, :])
                        mm.then_inc(turned, 1)
                    if n:
                        outputs(n - 1)
                    wait(pe, masked, n)
                    for g in range(QT_):
                        i = n * QT_ + g
                        pe.wait_ge(kept, i + 1)
                        for t in range(4):
                            kt = ktok[:, i % 2, t * P:(t + 1) * P]
                            first, last = g == 0 and t == 0, g == QT_ - 1 and t == 3
                            pe.matmul(pm[:, 0:P], kt, VA[:, b * NQ + g * 4 + t, c * L2_HPC:(c + 1) * L2_HPC, 0:L2_HD], start=first, stop=last)
                            mm = pe.matmul(pn[:, 0:P], kt, ones[:, :], start=first, stop=last)
                        mm.then_inc(summed, 1)
                outputs(len(jobs) - 1)

            @block.vector
            def _(dve):
                dve.memset(ones[:, :], 1.0).then_inc(set_up, 1)
                dve.wait_ge(gates, 1)
                dve.tensor_scalar(gate[:, 1, :], gate[:, 0, :], -1.0, 1.0, ALU.mult, ALU.add)

                def divide(n):
                    b, c = jobs[n]
                    for z in range(NZ):
                        i = n * NZ + z
                        dve.wait_ge(out_made, i + 1)
                        dve.reciprocal(inv[:, i % 2, :], den[i % 2][:, :]).then_inc(inv_ready, 1)
                        dve.wait_ge(inv_ready, i + 1)
                        dve.scalar_tensor_tensor(out=mem[:, c, b * S + z * BANK:b * S + (z + 1) * BANK], in0=num[i % 2][:, :],
                                                 scalar=gate[:, 0, c:c + 1], in1=inv[:, i % 2, :], op0=ALU.mult, op1=ALU.mult).then_inc(used, 1)

                for n in range(len(jobs)):
                    if n:
                        divide(n - 1)
                    dve.wait_ge(summed, (n + 1) * QT_)
                    wait(dve, out_made, (n - 1) * NZ)
                    dve.tensor_tensor(M[:, n % 2, :], pm[:, 0:P], blk[:, :], ALU.mult)
                    dve.tensor_tensor(N[:, n % 2, :], pn[:, 0:P], blk[:, :], ALU.mult).then_inc(masked, 1)
                divide(len(jobs) - 1)


def l2_heads(nc, k, split, VA, CT):
    with Stage(nc, "l2h") as st:
        Q1, K1 = st.sb("Q1", [P, 2, S], F32R), st.sb("K1", [P, 2, S], F32R)
        Q2, K2 = st.sb("Q2", [P, 2, S], F32R), st.sb("K2", [P, 2, S], F32R)
        PT = st.sb("PT", [P, 2, NQ, S])
        half = st.sb("half", [P, 2, NQ, 2])
        top = st.sb("top", [P, 2, NQ])
        mhi, mlo = st.sb("mhi", [NQ, 2, P], F32R), st.sb("mlo", [NQ, 2, P], F32R)
        inv = st.sb("inv", [P, 4, 2])
        VH = st.sb("VH", [P, 2, NQ, L2_W])
        s1 = [st.ps(f"s1_{i}") for i in range(2)]
        s2 = [st.ps(f"s2_{i}", 2 * BANK) for i in range(2)]
        turns, pv = st.ps("turns"), st.ps("pv")
        ctxT = st.sb("ctxT", [P, 2 * P])
        pmt = turns[0:NQ, NQ * L2_W:NQ * L2_W + P]
        filled, q1_loaded = st.sem("filled"), [st.sem(f"q1_loaded{i}") for i in range(B)]
        q2_loaded, m_loaded = [st.sem(f"q2_loaded{i}") for i in range(B)], [st.sem(f"m_loaded{i}") for i in range(B)]
        s1_made, maxed, top_ready = st.sem("s1_made"), st.sem("maxed"), st.sem("top_ready")
        mhi_ready, m_ready, s2_made, exped = st.sem("mhi_ready"), st.sem("m_ready"), st.sem("s2_made"), st.sem("exped")
        pv_made, pv_kept, turned, inv_ready, ctx_kept = (st.sem(n) for n in ("pv_made", "pv_kept", "turned", "inv_ready", "ctx_kept"))
        vh_ready, second_loads = st.sem("vh_ready"), st.sem("second_loads")
        NP = 2 * NQ
        TURN_AT = 1
        MROW = SPLIT

        def steps(engine, step):
            for b in range(B):
                step(0, b)
            with engine.Fori(1, L2_HEADS - 1) as h:
                for b in range(B):
                    step(h, b)
            for b in range(B):
                step(L2_HEADS - 1, b)

        def after(h, b, n):
            return (h + (b + n) // B, (b + n) % B)

        def before(h, b):
            return (h, b - 1) if b else (h - 1, B - 1)

        def is_first(h, b):
            return isinstance(h, int) and h == 0 and b == 0

        def exists(h, b, n):
            return not isinstance(h, int) or B * h + b + n < L2_N

        with nc.Block() as block:

            @block.sync
            def _(sp):
                def load(Q, K, h, b, sem):
                    for i, m in enumerate((Q, K)):
                        sp.dma_start(m[0:SPLIT, :].bitcast(F32), split[i][:, ds(h * L2_HD, L2_HD), b * S:(b + 1) * S]).then_inc(sem, 16)

                def load_first(h, b):
                    n = B * h + b
                    wait(sp, s1_made, NP * (n - 1))
                    load(Q1[:, b, :], K1[:, b, :], h, b, q1_loaded[b])

                def load_second(h, b):
                    n = B * h + b
                    wait(sp, s2_made, NQ * (n - 1))
                    sp.sem_inc(second_loads, 1)
                    load(Q2[:, b, :], K2[:, b, :], h, b, q2_loaded[b])

                def load_max(h, b):
                    n = B * h + b
                    sp.wait_ge(m_ready, n + 1)
                    for i, m in enumerate((mhi, mlo)):
                        sp.dma_start(Q2[MROW + i:MROW + i + 1, b, :].bitcast(F32).rearrange("a (t n) -> a t n", t=NQ), m[:, b, :].bitcast(F32)).then_inc(m_loaded[b], 16)

                sp.wait_ge(filled, 2)
                load_first(0, 0)
                load_first(0, 1)
                sp.wait_ge(filled, 5)
                load_second(0, 0)
                load_max(0, 0)
                load_first(1, 0)

                def step(h, b):
                    if exists(h, b, 1):
                        load_second(*after(h, b, 1))
                    if exists(h, b, 3):
                        load_first(*after(h, b, 3))
                    if exists(h, b, 1):
                        load_max(*after(h, b, 1))

                for b in range(B):
                    step(0, b)
                with sp.Fori(1, L2_HEADS - 2) as h:
                    for b in range(B):
                        step(h, b)
                for h in (L2_HEADS - 2, L2_HEADS - 1):
                    for b in range(B):
                        step(h, b)

            @block.gpsimd
            def _(pool):
                for m in (Q1[SPLIT:P, :], K1[SPLIT:P, :], Q2[SPLIT:P, :, :], K2[SPLIT:P, :, :]):
                    pool.memset(m.bitcast(F32), 0.0).then_inc(filled, 1)
                pool.wait_ge(filled, 4)
                pool.memset(K2[MROW:MROW + 2, :, :].bitcast(F32), -1.0).then_inc(filled, 1)

            @block.tensor
            def _(pe):
                def first_pass(h, b, pieces):
                    n = B * h + b
                    for i in pieces:
                        t, z = divmod(i, 2)
                        if i == 0:
                            pe.wait_ge(q1_loaded[b], 32 * h + 32)
                        wait(pe, maxed, NP * n + i - 1)
                        pe.matmul(s1[i % 2][:, :], Q1[:, b, t * P:(t + 1) * P], K1[:, b, z * BANK:(z + 1) * BANK],
                                  start=True, stop=True).then_inc(s1_made, 1)

                def second_pass(h, b, kb):
                    n = B * h + b
                    if kb == 0:
                        pe.wait_ge(q2_loaded[b], 32 * h + 32)
                        pe.wait_ge(m_loaded[b], 32 * h + 32)
                    wait(pe, exped, NQ * n + kb - 1)
                    for z in range(NZ):
                        mm = pe.matmul(s2[kb % 2][:, z * BANK:(z + 1) * BANK], K2[:, b, kb * P:(kb + 1) * P],
                                       Q2[:, b, z * BANK:(z + 1) * BANK], start=True, stop=True)
                    mm.then_inc(s2_made, 1)

                def values(h, b, kb):
                    n = B * h + b
                    if kb == 0:
                        pe.wait_ge(vh_ready, n + 1)
                        pe.wait_ge(exped, NQ * (n + 1))
                        wait(pe, pv_kept, n)
                    for g in range(4):
                        mm = pe.matmul(pv[g * L2_W:(g + 1) * L2_W, 0:2 * P], VH[:, b, kb, :],
                                       PT[:, b, kb, g * 2 * P:(g + 1) * 2 * P], start=(kb == 0), stop=(kb == NQ - 1), skip_group_check=True)
                    if kb == NQ - 1:
                        mm.then_inc(pv_made, 1)

                def turn(m, ctx, top_of):
                    wait(pe, m_ready, min(m, L2_N) if isinstance(m, int) else m)
                    if ctx:
                        pe.wait_ge(pv_kept, m - 2)
                        wait(pe, ctx_kept, m - 3)
                        for i in range(2):
                            mm = pe.transpose(turns[:, i * P:(i + 1) * P], ctxT[:, i * P:(i + 1) * P], k.ident[:, :])
                    if top_of is not None:
                        pe.wait_ge(top_ready, m + 1)
                        mm = pe.transpose(pmt, top[:, top_of, :], k.ident[:, :])
                    mm.then_inc(turned, 1)

                first_pass(0, 0, range(NP))
                turn(0, False, 0)
                first_pass(0, 1, range(NP))

                def step(h, b):
                    for kb in range(NQ):
                        second_pass(h, b, kb)
                        if exists(h, b, 2):
                            first_pass(*after(h, b, 2), range(2 * kb, 2 * kb + 2))
                        if kb == TURN_AT:
                            turn(B * h + b + 1, not isinstance(h, int) or h > 0, (b + 1) % B if exists(h, b, 1) else None)
                        if not is_first(h, b):
                            values(*before(h, b), kb)

                steps(pe, step)
                turn(L2_N + 1, True, None)
                for kb in range(NQ):
                    values(L2_HEADS - 1, B - 1, kb)
                turn(L2_N + 2, True, None)

            @block.scalar
            def _(act):
                def keep_ctx(h, b):
                    n = B * h + b
                    act.wait_ge(pv_made, n + 1)
                    if not is_first(h, b):
                        act.wait_ge(turned, n + 3)
                    act.activation(ctxT[:, :], pv[:, 0:2 * P], ACT.Copy).then_inc(pv_kept, 1)

                def step(h, b):
                    n = B * h + b
                    if not isinstance(h, int) or h > 0:
                        keep_ctx(h - 1, b)
                    act.activation(VH[:, b, :, :], VA[:, b * NQ:(b + 1) * NQ, ds(h, 1), :].rearrange("p t a e -> p t (a e)"), ACT.Copy).then_inc(vh_ready, 1)
                    for kb in range(NQ):
                        act.wait_ge(s2_made, NQ * n + kb + 1)
                        act.activation(PT[:, b, kb, :], s2[kb % 2][:, :], ACT.Exp, scale=L2_SCALE).then_inc(exped, 1)

                steps(act, step)
                for b in range(B):
                    keep_ctx(L2_HEADS - 1, b)

            @block.vector
            def _(dve):
                def maxima(h, b, pieces):
                    n = B * h + b
                    for i in pieces:
                        t, z = divmod(i, 2)
                        dve.wait_ge(s1_made, NP * n + i + 1)
                        dve.reduce_max(half[:, b, t, z:z + 1], s1[i % 2][:, :], AX_X).then_inc(maxed, 1)

                def take_top(h, b):
                    n = B * h + b
                    dve.wait_ge(maxed, NP * (n + 1))
                    dve.reduce_max(top[:, b, :], half[:, b, :, :], AX_X).then_inc(top_ready, 1)

                def split_max(h, b):
                    n = B * h + b
                    dve.wait_ge(turned, n + 1)
                    wait(dve, m_loaded[b], 32 * h)
                    dve.tensor_copy(mhi[:, b, :], pmt).then_inc(mhi_ready, 1)
                    dve.wait_ge(mhi_ready, n + 1)
                    dve.tensor_tensor(mlo[:, b, :], pmt, mhi[:, b, :].bitcast(F32), ALU.subtract).then_inc(m_ready, 1)

                def normalise(h, b):
                    n = B * h + b
                    out = turns[:, 0:NQ * L2_W].rearrange("p (i g e) -> p g i e", i=2, e=L2_W)
                    dve.wait_ge(turned, n + 4)
                    dve.reciprocal(inv[:, :, :], out[:, :, :, L2_HD]).then_inc(inv_ready, 1)
                    dve.wait_ge(inv_ready, n + 1)
                    dve.tensor_tensor(CT[:, b * NQ:(b + 1) * NQ, ds(h * L2_HD, L2_HD)].rearrange("p (g i) e -> p g i e", i=2), out[:, :, :, 0:L2_HD],
                                      inv[:, :, :].unsqueeze(3).to_broadcast([P, 4, 2, L2_HD]), ALU.mult).then_inc(ctx_kept, 1)

                maxima(0, 0, range(NP))
                take_top(0, 0)
                split_max(0, 0)
                maxima(0, 1, range(NP))
                take_top(0, 1)

                def step(h, b):
                    n = B * h + b
                    more = exists(h, b, 2)
                    early = 2 * (TURN_AT + 1)
                    if more:
                        maxima(*after(h, b, 2), range(early))
                    if exists(h, b, 1):
                        split_max(*after(h, b, 1))
                    if not isinstance(h, int) or h > 0:
                        normalise(h - 1, b)
                    if more:
                        maxima(*after(h, b, 2), range(early, NP))
                        take_top(*after(h, b, 2))

                steps(dve, step)
                for b in range(B):
                    normalise(L2_HEADS - 1, b)


def l2_output(nc, k, a, CT, mem, gate):
    with Stage(nc, "l2o") as st:
        wo = st.sb("wo", [P, DC, D])
        comb = st.sb("comb", [P, 2, DC, BANK])
        ptr = [st.ps(f"ptr{i}") for i in range(4)]
        out = [st.ps(f"out{i}") for i in range(4)]
        loaded, turned, combined, made, added = st.sem("loaded"), st.sem("turned"), st.sem("combined"), st.sem("made"), st.sem("added")

        with nc.Block() as block:

            @block.sync
            def _(sp):
                sp.dma_start(wo[:, :, :], rows(a["L2_attn_WoT"])).then_inc(loaded, 16)

            @block.tensor
            def _(pe):
                def turn(j):
                    wait(pe, combined, DC * (j - 1))
                    for c in range(DC):
                        for t in range(4):
                            mm = pe.transpose(ptr[j % 2 * 2 + c][:, t * P:(t + 1) * P], CT[:, 4 * j + t, c * P:(c + 1) * P], k.ident[:, :])
                        mm.then_inc(turned, 1)

                turn(0)
                pe.wait_ge(loaded, 16)
                for j in range(NJ):
                    if j + 1 < NJ:
                        turn(j + 1)
                    pe.wait_ge(combined, DC * (j + 1))
                    wait(pe, added, DC * (j - 1))
                    for o in range(DC):
                        for c in range(DC):
                            mm = pe.matmul(out[j % 2 * 2 + o][:, :], wo[:, c, o * P:(o + 1) * P], comb[:, j % 2, c, :], start=(c == 0), stop=(c == DC - 1))
                        mm.then_inc(made, 1)

            @block.vector
            def _(dve):
                def combine(j):
                    wait(dve, made, DC * (j - 1))
                    for c in range(DC):
                        dve.wait_ge(turned, DC * j + c + 1)
                        dve.scalar_tensor_tensor(out=comb[:, j % 2, c, :], in0=ptr[j % 2 * 2 + c][:, :], scalar=gate[:, 1, c:c + 1],
                                                 in1=mem[:, c, j * BANK:(j + 1) * BANK], op0=ALU.mult, op1=ALU.add).then_inc(combined, 1)

                combine(0)
                for j in range(NJ):
                    if j + 1 < NJ:
                        combine(j + 1)
                    for o in range(DC):
                        dve.wait_ge(made, DC * j + o + 1)
                        x = k.XT[:, o, j * BANK:(j + 1) * BANK]
                        dve.tensor_tensor(x, x, out[j % 2 * 2 + o][:, :], ALU.add).then_inc(added, 1)


def l2_constants():
    f = np.float32
    inv_freq = (1.0 / f(10000.0) ** (np.arange(0, D, 2, dtype=f) / f(D))).astype(f)
    ang = (inv_freq[:, None] * np.arange(S, dtype=f)[None, :]).astype(f)
    i = np.arange(P) // L2_HD
    return {"c_l2_rope": np.stack([np.cos(ang), np.sin(ang)]).astype(f), "c_l2_block": (i[:, None] == i[None, :]).astype(f)}


def l2_layout(x):
    w = lambda m: m.T.reshape(DC, P, D).transpose(1, 0, 2)
    return {"L2_w3": np.stack([w(x["L2_attn_Wq"]), w(x["L2_attn_Wk"]), w(x["L2_attn_Wv"])], axis=1), "L2_attn_WoT": x["L2_attn_Wo"].T,
            "L2_gate_cols": np.repeat(x["L2_attn_gate"].reshape(-1), L2_HD).reshape(DC, P).T}


L3_HEADS, L3_HD = 32, 64
L3_INNER = L3_HEADS * L3_HD
L3_PAIRS = L3_HEADS // 2
NCH = T // P


def l3_attn(nc, k, a):
    decays = nc.dram_tensor("l3_decays", [2, L3_HEADS, T], F32, kind="Internal").ap()
    with Stage(nc, "l3w") as sw:
        wout = sw.sb("wout", [P, L3_PAIRS, D])
        bcol = sw.sb("bcol", [P, DC])
        l3_decays(nc, k, a, decays, wout, bcol)
        for b in range(B):
            l3_batch(nc, k, a, decays, b, wout, bcol)


def l3_batch(nc, k, a, decays, b, wout, bcol):
    with Stage(nc, f"l3a{b}") as st:
        Y = st.sb("Y", [P, L3_PAIRS, S])
        ysum = st.sb("ysum", [P, S])
        with Stage(nc, f"l3x{b}") as sx:
            XH, XL = sx.sb("XH", [P, DC, S], F32R), sx.sb("XL", [P, DC, S], F32R)
            split_stage(nc, f"l3s{b}", k.XN[:, :, b * S:(b + 1) * S], XH, XL)
            l3_pairs(nc, k, a, decays, b, Y, ysum, XH, XL)
        l3_output(nc, k, a, b, Y, ysum, wout, bcol)
    if b + 1 < B:
        clear_semaphores(nc)


def l3_decays(nc, k, a, decays, wout, bcol):
    with Stage(nc, "l3d") as st:
        H = L3_HEADS
        w = st.sb("w", [P, DC, H])
        ex = st.sb("ex", [H, 2, BANK])
        dec = st.sb("dec", [H, T])
        run = st.sb("run", [H, T])
        zero = st.sb("zero", [H, P])
        acc = [st.ps(f"acc{i}") for i in range(2)]
        loaded, made, exped, decayed, prods, stored = st.sem("loaded"), st.sem("made"), st.sem("exped"), st.sem("decayed"), st.sem("prods"), st.sem("stored")
        zeroed = st.sem("zeroed")
        gb = st.sb("gb", [P, 2, L3_PAIRS])
        pbeta = st.ps("pbeta")
        w_loaded, beta_made = st.sem("w_loaded"), st.sem("beta_made")
        with nc.Block() as block:

            @block.sync
            def _(sp):
                sp.dma_start(w[:, :, :], rows(a["L3_wa"])).then_inc(loaded, 16)
                sp.dma_start(gb[:, :, :], a["L3_gb"]).then_inc(w_loaded, 16)
                sp.dma_start(wout[:, :, :], rows(a["L3_W_outT"])).then_inc(w_loaded, 16)
                sp.wait_ge(prods, NCH)
                sp.dma_start(decays[1], run[:, :]).then_inc(stored, 16)
                sp.wait_ge(zeroed, 2)
                sp.dma_start(decays[0], dec[:, :]).then_inc(stored, 16)
                sp.wait_ge(stored, 32)

            @block.tensor
            def _(pe):
                pe.wait_ge(loaded, 16)
                for j in range(NJ):
                    wait(pe, exped, j - 1)
                    for c in range(DC):
                        mm = pe.matmul(acc[j % 2][0:H, :], w[:, c, :], k.XN[:, c, j * BANK:(j + 1) * BANK], start=(c == 0), stop=(c == DC - 1))
                    mm.then_inc(made, 1)
                pe.wait_ge(w_loaded, 32)
                for c in range(DC):
                    for i in range(L3_PAIRS):
                        mm = pe.matmul(pbeta[:, c:c + 1], wout[:, i, c * P:(c + 1) * P], gb[:, 1, i:i + 1], start=(i == 0), stop=(i == L3_PAIRS - 1))
                mm.then_inc(beta_made, 1)

            @block.scalar
            def _(act):
                for j in range(NJ):
                    act.wait_ge(made, j + 1)
                    act.activation(ex[:, j % 2, :], acc[j % 2][0:H, :], ACT.Exp).then_inc(exped, 1)
                    act.wait_ge(exped, j + 1)
                    act.activation(dec[:, j * BANK:(j + 1) * BANK], ex[:, j % 2, :], ACT.Exp, scale=-1.0).then_inc(decayed, 1)

            @block.vector
            def _(dve):
                dve.memset(zero[:, :], 0.0).then_inc(zeroed, 1)
                dve.wait_ge(zeroed, 1)
                for i in range(NCH):
                    if i % 4 == 0:
                        dve.wait_ge(decayed, i // 4 + 1)
                    t = slice(i * P, (i + 1) * P)
                    dve.tensor_tensor_scan(run[:, t], dec[:, t], zero[:, :], 1.0, ALU.mult, ALU.add).then_inc(prods, 1)
                dve.wait_ge(prods, NCH)
                dve.memset(dec[:, :].rearrange("h (i n) -> h i n", n=P)[:, :, 0:1], 0.0).then_inc(zeroed, 1)
                dve.wait_ge(beta_made, 1)
                dve.tensor_copy(bcol[:, :], pbeta[:, 0:DC])
                for i in range(L3_PAIRS):
                    dve.tensor_scalar(wout[:, i, :], wout[:, i, :], gb[:, 0, i:i + 1], None, ALU.mult)


def l3_pairs(nc, k, a, decays, b, Y, ysum, XH, XL):
    with Stage(nc, f"l3p{b}") as st:
        w4 = st.sb("w4", [P, 4, DC, P])
        w_hi, w_lo = st.sb("w_hi", [P, 4, DC, P], F32R), st.sb("w_lo", [P, 4, DC, P], F32R)
        dcol = st.sb("dcol", [P, 1])
        eye4 = st.sb("eye4", [P, BANK])
        blk = st.sb("blk", [P, P])
        decb = st.sb("decb", [P, 2, 2, BANK])
        prow = st.sb("prow", [P, 2, BANK])
        xT, bT = st.sb("xT", [P, 2, BANK]), st.sb("bT", [P, BANK])
        cT2 = st.sb("cT2", [P, 2, BANK])
        cdT = st.sb("cdT", [P, 2, BANK])
        sz = st.sb("sz", [P, 2, BANK])
        xtok = st.sb("xtok", [P, 2, QUAD, P])
        btok = st.sb("btok", [P, QUAD, P])
        table = st.sb("table", [P, 2, BANK])
        mixT = st.sb("mixT", [P, 2, 2, BANK])
        dsm = st.sb("dsm", [P, QUAD, P])
        state = st.sb("state", [P, 2, QUAD, P])
        skip = st.sb("skip", [P, BANK])
        px, pb, pc, pz, pds, py = (st.ps(n) for n in ("px", "pb", "pc", "pz", "pds", "py"))
        psc = st.ps("psc", 2 * BANK)
        loaded_w4, loaded_c, loaded_d, consts, zeroed = st.sem("loaded_w4"), st.sem("loaded_c"), [st.sem(f"loaded_d{i}") for i in range(2)], st.sem("consts"), st.sem("zeroed")
        x_made, b_made, c_made, z_made = st.sem("x_made"), st.sem("b_made"), st.sem("c_made"), st.sem("z_made")
        x_kept, b_kept, c_kept, z_kept = st.sem("x_kept"), st.sem("b_kept"), st.sem("c_kept"), st.sem("z_kept")
        xt_made, bt_made, xt_kept, bt_kept = st.sem("xt_made"), st.sem("bt_made"), st.sem("xt_kept"), st.sem("bt_kept")
        tables, sc_made, mixed, ds_made, ds_masked, states, linked = (st.sem(n) for n in ("tables", "sc_made", "mixed", "ds_made", "ds_masked", "states", "linked"))
        whi_ready, wlo_ready = st.sem("whi_ready"), st.sem("wlo_ready")
        summed, summing = st.sem("summed"), st.sem("summing")
        c_decayed, y_made, skipped, y_ready = st.sem("c_decayed"), st.sem("y_made"), st.sem("skipped"), st.sem("y_ready")

        def steps(engine, step):
            for z in range(NZ):
                step(0, z)
            with engine.Fori(1, L3_PAIRS) as h:
                for z in range(NZ):
                    step(h, z)

        def before(h, z):
            return (h, z - 1) if z else (h - 1, NZ - 1)

        def is_first(h, z):
            return isinstance(h, int) and h == 0 and z == 0

        with nc.Block() as block:

            @block.sync
            def _(sp):
                def load(h, z):
                    n, o = NZ * h + z, z
                    if z == 0:
                        wait(sp, wlo_ready, h)
                        sp.dma_start(w4[:, :, :, :], a["L3_w4"][ds(h, 1)].rearrange("a p t c n -> (a p) t c n")).then_inc(loaded_w4, 16)
                    wait(sp, tables, 2 * n - 2)
                    tok = slice(b * S + z * BANK, b * S + (z + 1) * BANK)
                    for i in range(2):
                        sp.dma_start(decb[:, o, i, :], decays[0][ds(2 * h + i, 1), tok].to_broadcast([P, BANK])).then_inc(loaded_d[o], 16)
                    wait(sp, states, n - 1)
                    for i in range(2):
                        sp.dma_start(prow[i * L3_HD:(i + 1) * L3_HD, o, :],
                                     decays[1][ds(2 * h + i, 1), tok].to_broadcast([L3_HD, BANK])).then_inc(loaded_d[o], 16)

                load(0, 0)
                sp.dma_start(eye4[:, :], a["c_eye4"]).then_inc(consts, 16)
                sp.dma_start(blk[:, :], a["c_l3_block"]).then_inc(consts, 16)
                sp.dma_start(dcol[:, :], a["L3_dcol"][0]).then_inc(loaded_c, 16)
                load(0, 1)
                with sp.Fori(1, L3_PAIRS) as h:
                    load(h, 0)
                    sp.wait_ge(skipped, NZ * h)
                    sp.dma_start(dcol[:, :], a["L3_dcol"][ds(h, 1)].rearrange("a p n -> (a p) n")).then_inc(loaded_c, 16)
                    load(h, 1)
                sp.wait_ge(wlo_ready, L3_PAIRS)
                sp.dma_start(w4[:, :, :, :], a["L3_w4"][0]).then_inc(loaded_w4, 16)

            @block.tensor
            def _(pe):
                def project(h, z):
                    n = NZ * h + z
                    if z == 0:
                        pe.wait_ge(wlo_ready, h + 1)
                    tok = slice(z * BANK, (z + 1) * BANK)
                    for i, (bank, made, used) in enumerate(((px, x_made, xt_kept), (pb, b_made, bt_kept), (pc, c_made, c_decayed), (pz, z_made, z_kept))):
                        wait(pe, used, n)
                        split_product(pe, bank[:, :], lambda c, i=i: w_hi[:, i, c, :], lambda c, i=i: w_lo[:, i, c, :],
                                      lambda c: XH[:, c, tok], lambda c: XL[:, c, tok]).then_inc(made, 1)

                def outputs(h, z):
                    n, o = NZ * h + z, z
                    pe.wait_ge(states, n + 1)
                    pe.wait_ge(c_decayed, n + 1)
                    pe.wait_ge(mixed, n + 1)
                    wait(pe, skipped, n)
                    for t in range(QUAD):
                        col = slice(t * P, (t + 1) * P)
                        inter = t > 0 or z > 0
                        if inter:
                            pe.matmul(py[:, col], state[:, o, t, :], cdT[:, o, col], start=True, stop=False, skip_group_check=True)
                        for i in range(2):
                            half = slice(i * L3_HD, (i + 1) * L3_HD)
                            mm = pe.matmul(py[half, col], xtok[:, o, t, half], mixT[:, o, i, col], start=not inter, stop=True,
                                           skip_group_check=True)
                    mm.then_inc(y_made, 1)

                def tables_and_states(h, z):
                    n, o = NZ * h + z, z
                    pe.wait_ge(x_kept, n + 1)
                    for t in range(QUAD):
                        mm = pe.transpose(px[:, t * P:(t + 1) * P], xT[:, o, t * P:(t + 1) * P], k.ident[:, :])
                    mm.then_inc(xt_made, 1)
                    pe.wait_ge(b_kept, n + 1)
                    for t in range(QUAD):
                        mm = pe.transpose(pb[:, t * P:(t + 1) * P], bT[:, t * P:(t + 1) * P], k.ident[:, :])
                    mm.then_inc(bt_made, 1)
                    pe.wait_ge(c_kept, n + 1)
                    wait(pe, mixed, n)
                    for t in range(QUAD):
                        mm = pe.matmul(psc[:, 2 * t * P:2 * (t + 1) * P], bT[:, t * P:(t + 1) * P], cT2[:, :, t * P:(t + 1) * P], start=True, stop=True)
                    mm.then_inc(sc_made, 1)
                    pe.wait_ge(bt_kept, n + 1)
                    pe.wait_ge(xt_kept, n + 1)
                    wait(pe, ds_masked, n)
                    for t in range(QUAD):
                        mm = pe.matmul(pds[:, t * P:(t + 1) * P], btok[:, t, :], xtok[:, o, t, :], start=True, stop=True)
                    mm.then_inc(ds_made, 1)

                pe.wait_ge(zeroed, 1)
                def step(h, z):
                    project(h, z)
                    if not is_first(h, z):
                        outputs(*before(h, z))
                    tables_and_states(h, z)

                steps(pe, step)
                outputs(L3_PAIRS - 1, NZ - 1)

            @block.scalar
            def _(act):
                def split_weights(h):
                    act.wait_ge(loaded_w4, 16 * h + 16)
                    wait(act, z_made, NZ * h)
                    act.activation(w_hi[:, :, :, :], w4[:, :, :, :], ACT.Copy).then_inc(whi_ready, 1)

                split_weights(0)

                def step(h, z):
                    n, o = NZ * h + z, z
                    act.wait_ge(x_made, n + 1)
                    wait(act, skipped, n - 1)
                    act.activation(xT[:, o, :], px[:, :], ACT.Copy).then_inc(x_kept, 1)
                    act.wait_ge(b_made, n + 1)
                    wait(act, sc_made, n)
                    act.activation(bT[:, :], pb[:, :], ACT.Copy).then_inc(b_kept, 1)
                    act.wait_ge(c_made, n + 1)
                    wait(act, sc_made, n)
                    act.activation(cT2[0:L3_HD, 0, :], pc[0:L3_HD, :], ACT.Copy)
                    act.activation(cT2[L3_HD:P, 1, :], pc[L3_HD:P, :], ACT.Copy).then_inc(c_kept, 1)
                    act.wait_ge(z_made, n + 1)
                    wait(act, y_ready, n - 1)
                    act.activation(sz[:, o, :], pz[:, :], ACT.Silu).then_inc(z_kept, 1)
                    if z == NZ - 1:
                        split_weights(h + 1)
                    act.wait_ge(xt_made, n + 1)
                    wait(act, y_made, n - 1)
                    act.activation(xtok[:, o, :, :], px[:, :].rearrange("p (t n) -> p t n", t=QUAD), ACT.Copy).then_inc(xt_kept, 1)

                steps(act, step)

            @block.gpsimd
            def _(pool):
                pool.memset(cT2[:, :, :], 0.0).then_inc(zeroed, 1)
                pool.memset(ysum[:, :], 0.0).then_inc(summed, 1)

                def gate(h, z):
                    n, o = NZ * h + z, z
                    pool.wait_ge(skipped, n + 1)
                    pool.wait_ge(z_kept, n + 1)
                    pool.tensor_tensor(Y[:, ds(h, 1), z * BANK:(z + 1) * BANK].rearrange("p a n -> p (a n)"), skip[:, :], sz[:, o, :],
                                       ALU.mult).then_inc(y_ready, 1)
                    pool.wait_ge(y_ready, n + 1)
                    pool.wait_ge(summed, n + 1)
                    pool.sem_inc(summing, 1)
                    part = ysum[:, z * BANK:(z + 1) * BANK]
                    pool.tensor_tensor(part, part, Y[:, ds(h, 1), z * BANK:(z + 1) * BANK].rearrange("p a n -> p (a n)"), ALU.add).then_inc(summed, 1)

                def split_weights(h):
                    pool.wait_ge(whi_ready, h + 1)
                    pool.tensor_tensor(w_lo[:, :, :, :], w4[:, :, :, :], w_hi[:, :, :, :].bitcast(F32), ALU.subtract).then_inc(wlo_ready, 1)

                split_weights(0)

                def step(h, z):
                    if z == NZ - 1:
                        split_weights(h + 1)
                    if not is_first(h, z):
                        gate(*before(h, z))

                steps(pool, step)
                gate(L3_PAIRS - 1, NZ - 1)

            @block.vector
            def _(dve):
                dve.wait_ge(consts, 32)

                def add_skip(h, z):
                    n, o = NZ * h + z, z
                    dve.wait_ge(y_made, n + 1)
                    wait(dve, y_ready, n)
                    if z == 0:
                        dve.wait_ge(loaded_c, 16 * h + 16)
                    dve.scalar_tensor_tensor(out=skip[:, :], in0=xT[:, o, :], scalar=dcol[:, 0:1], in1=py[:, :],
                                             op0=ALU.mult, op1=ALU.add).then_inc(skipped, 1)

                def step(h, z):
                    n, o = NZ * h + z, z
                    dve.wait_ge(loaded_d[o], 64 * h + 64)
                    wait(dve, mixed, n)
                    wait(dve, bt_kept, n)
                    for i in range(2):
                        dve.tensor_tensor_scan(table[:, i, :], decb[:, o, i, :], eye4[:, :], 0.0, ALU.mult, ALU.add).then_inc(tables, 1)
                    if not is_first(h, z):
                        add_skip(*before(h, z))
                    dve.wait_ge(c_kept, n + 1)
                    wait(dve, y_made, n - 1)
                    dve.tensor_tensor(cdT[:, o, :], pc[:, :], prow[:, o, :], ALU.mult).then_inc(c_decayed, 1)
                    dve.wait_ge(tables, 2 * n + 2)
                    dve.wait_ge(bt_made, n + 1)
                    wait(dve, ds_made, n)
                    last = table[:, :, :].rearrange("p i (t n) -> p t i n", t=QUAD)[:, :, :, P - 1:P]
                    dve.tensor_tensor(btok[:, :, :].rearrange("p t (i n) -> p t i n", i=2), pb[:, :].rearrange("p (t i n) -> p t i n", t=QUAD, i=2),
                                      last.to_broadcast([P, QUAD, 2, L3_HD]), ALU.mult).then_inc(bt_kept, 1)
                    dve.wait_ge(sc_made, n + 1)
                    dve.tensor_tensor(mixT[:, o, :, :].rearrange("p i (t n) -> p t i n", t=QUAD), psc[:, :].rearrange("p (t i n) -> p t i n", t=QUAD, i=2),
                                      table[:, :, :].rearrange("p i (t n) -> p t i n", t=QUAD), ALU.mult).then_inc(mixed, 1)
                    dve.wait_ge(ds_made, n + 1)
                    wait(dve, states, n)
                    dve.tensor_tensor(dsm[:, :, :], pds[:, :].rearrange("p (t n) -> p t n", t=QUAD), blk[:, :].unsqueeze(1).to_broadcast([P, QUAD, P]),
                                      ALU.mult).then_inc(ds_masked, 1)
                    base = (2 * QUAD - 3) * h + z * (QUAD - 1)
                    dve.wait_ge(ds_masked, n + 1)
                    for t in range(QUAD if z + 1 < NZ else QUAD - 1):
                        out = state[:, o, t + 1, :] if t + 1 < QUAD else state[:, 1 - o, 0, :]
                        if t == 0 and z == 0:
                            op = dve.tensor_copy(out, dsm[:, 0, :])
                        else:
                            if t:
                                dve.wait_ge(linked, base + t)
                            op = dve.scalar_tensor_tensor(out=out, in0=state[:, o, t, :], scalar=prow[:, o, (t + 1) * P - 1:(t + 1) * P], in1=dsm[:, t, :],
                                                          op0=ALU.mult, op1=ALU.add)
                        op.then_inc(states if t == (QUAD - 1 if z + 1 < NZ else QUAD - 2) else linked, 1)

                steps(dve, step)
                add_skip(L3_PAIRS - 1, NZ - 1)


def l3_output(nc, k, a, b, Y, ysum, wout, bcol):
    with Stage(nc, f"l3o{b}") as st:
        NP_ = L3_PAIRS
        sq = st.sb("sq", [P, 4, BANK])
        sqsum = st.sb("sqsum", [P, NZ, BANK])
        avg = st.sb("avg", [P, P])
        std, rstd = st.sb("std", [P, NZ, BANK]), st.sb("rstd", [P, NZ, BANK])
        tmp = st.sb("tmp", [P, 2, BANK])
        stat = [st.ps(f"stat{z}") for z in range(NZ)]
        out = [st.ps(f"out{i}") for i in range(NZ * DC)]
        set_up = st.sem("set_up")
        mu_made, centred, squared, sq_added, var_made, std_ready, rstd_ready, out_made, scaled, added = (
            st.sem(n) for n in ("mu_made", "centred", "squared", "sq_added", "var_made", "std_ready", "rstd_ready", "out_made", "scaled", "added"))
        jobs = [(z, i) for z in range(NZ) for i in range(NP_)]

        def y(z, i):
            return Y[:, i, z * BANK:(z + 1) * BANK]

        with nc.Block() as block:

            @block.tensor
            def _(pe):
                pe.wait_ge(set_up, 1)
                for z in range(NZ):
                    pe.matmul(stat[z][:, :], avg[:, :], ysum[:, z * BANK:(z + 1) * BANK], start=True, stop=True).then_inc(mu_made, 1)
                for z in range(NZ):
                    for i in range(NP_):
                        pe.wait_ge(centred, z * NP_ + i + 1)
                        for c in range(DC):
                            mm = pe.matmul(out[z * DC + c][:, :], wout[:, i, c * P:(c + 1) * P], y(z, i), start=(i == 0), stop=(i == NP_ - 1))
                    mm.then_inc(out_made, 1)
                    pe.wait_ge(sq_added, (z + 1) * NP_ + 1)
                    pe.matmul(stat[z][:, :], avg[:, :], sqsum[:, z, :], start=True, stop=True).then_inc(var_made, 1)

            @block.scalar
            def _(act):
                for n, (z, i) in enumerate(jobs):
                    act.wait_ge(centred, n + 1)
                    wait(act, sq_added, n - 2 if n >= 4 else 0)
                    act.activation(sq[:, n % 4, :], y(z, i), ACT.Square).then_inc(squared, 1)
                for z in range(NZ):
                    act.wait_ge(var_made, z + 1)
                    act.activation(std[:, z, :], stat[z][:, :], ACT.Sqrt, bias=k.eps[:, 0:1]).then_inc(std_ready, 1)

            @block.gpsimd
            def _(pool):
                pool.memset(sqsum[:, :, :], 0.0).then_inc(sq_added, 1)
                for n, (z, i) in enumerate(jobs):
                    pool.wait_ge(squared, n + 1)
                    pool.wait_ge(sq_added, n + 1)
                    pool.tensor_tensor(sqsum[:, z, :], sqsum[:, z, :], sq[:, n % 4, :], ALU.add).then_inc(sq_added, 1)

            @block.vector
            def _(dve):
                dve.memset(avg[:, :], 1.0 / L3_INNER).then_inc(set_up, 1)
                for z in range(NZ):
                    dve.wait_ge(mu_made, z + 1)
                    for i in range(NP_):
                        dve.tensor_tensor(y(z, i), y(z, i), stat[z][:, :], ALU.subtract).then_inc(centred, 1)
                for z in range(NZ):
                    dve.wait_ge(std_ready, z + 1)
                    dve.reciprocal(rstd[:, z, :], std[:, z, :]).then_inc(rstd_ready, 1)
                    dve.wait_ge(rstd_ready, z + 1)
                    dve.wait_ge(out_made, z + 1)
                    for c in range(DC):
                        n = z * DC + c
                        wait(dve, added, n - 1)
                        dve.tensor_tensor(tmp[:, n % 2, :], out[n][:, :], rstd[:, z, :], ALU.mult).then_inc(scaled, 1)
                        dve.wait_ge(scaled, n + 1)
                        x = k.XT[:, c, b * S + z * BANK:b * S + (z + 1) * BANK]
                        dve.scalar_tensor_tensor(out=x, in0=tmp[:, n % 2, :], scalar=bcol[:, c:c + 1], in1=x, op0=ALU.add, op1=ALU.add).then_inc(added, 1)


def l3_constants():
    f = np.float32
    i = np.arange(P) // L3_HD
    return {"c_eye4": np.tile(np.eye(P, dtype=f), (1, QUAD)), "c_l3_block": (i[:, None] == i[None, :]).astype(f)}


def l3_layout(x):
    wT = x["L3_attn_W_in"].T
    part = lambda i: wT[:, i * L3_INNER:(i + 1) * L3_INNER].reshape(DC, P, L3_PAIRS, P).transpose(2, 1, 0, 3)
    gb = np.stack([x["L3_attn_gamma"].reshape(L3_PAIRS, P).T, x["L3_attn_beta"].reshape(L3_PAIRS, P).T], axis=1)
    return {"L3_w4": np.stack([part(0), part(2), part(3), part(1)], axis=2), "L3_wa": wT[:, 4 * L3_INNER:],
            "L3_dcol": x["L3_attn_D"].reshape(L3_PAIRS, P, 1), "L3_W_outT": x["L3_attn_W_out"].T, "L3_gb": gb}


MOE_E, MOE_Z, MOE_K = 32, 32, 8
MOE_I, MOE_CAP = 128, 128
MOE_N = MOE_E + MOE_Z
MOE_SCALE, MOE_TINY = 1.5, 1e-20
MOE_TURN = 4
MOE_OFF = 1e4
MOE_INFO = 7


def l3_ffn(nc, k, a):
    xtok = nc.dram_tensor("moe_xtok", [T + P, D], F32, kind="Internal").ap()
    with Stage(nc, "moe") as st:
        key = st.sb("key", [P, MOE_E, TT])
        info = st.sb("info", [P, MOE_E, TT, MOE_INFO], BF16)
        moe_route(nc, k, a, xtok, key, info)
        moe_experts(nc, k, a, xtok, key, info)


def moe_route(nc, k, a, xtok, key, info):
    with Stage(nc, "mr") as st:
        wcls = st.sb("wcls", [P, DC, MOE_N])
        bias = st.sb("bias", [P, MOE_N])
        tri = st.sb("tri", [P, P])
        ones = st.sb("ones", [P, P])
        ids = st.sb("ids", [P, TT, 3])
        again = st.sb("again", [P, MOE_E * TT])
        rowsN = st.sb("rowsN", [P, TT + 1, D])
        rowsX = st.sb("rowsX", [P, TT + 1, D])
        e1 = st.sb("e1", [P, TT, MOE_N])
        s1 = st.sb("s1", [P, TT, MOE_N])
        biased = st.sb("biased", [P, TT, MOE_N])
        left = st.sb("left", [P, TT, MOE_N])
        chosen = st.sb("chosen", [P, TT, MOE_N])
        w1 = st.sb("w1", [P, TT, MOE_N])
        top8 = st.sb("top8", [P, TT, 8])
        small = st.sb("small", [P, 8, TT])
        maskE = st.sb("maskE", [P, MOE_E, TT])
        before = st.sb("before", [P, MOE_E, TT])
        wE, wa, wb = st.sb("wE", [P, MOE_E, TT]), st.sb("wa", [P, MOE_E, TT]), st.sb("wb", [P, MOE_E, TT])
        lg = st.ps("lg", 2 * BANK)
        place = st.ps("place")
        tr = [st.ps(f"tr{i}") for i in range(4)]
        loaded, logits_made, lowered, exped = st.sem("loaded"), st.sem("logits_made"), st.sem("lowered"), st.sem("exped")
        done, counted, placed = st.sem("done"), st.sem("counted"), st.sem("placed")
        turned, tr_act, zero_rows, stored = st.sem("turned"), st.sem("tr_act"), st.sem("zero_rows"), st.sem("stored")
        jobs = [(src, dst, j) for src, dst in ((k.XN, rowsN), (k.XT, rowsX)) for j in range(TT // 2)]

        with nc.Block() as block:

            @block.sync
            def _(sp):
                sp.dma_start(wcls[:, :, :], rows(a["L3_ffn_w_clsT"])).then_inc(loaded, 16)
                sp.dma_start(bias[:, :], a["L3_ffn_bias_row"].to_broadcast([P, MOE_N])).then_inc(loaded, 16)
                sp.dma_start(tri[:, :], a["c_before"]).then_inc(loaded, 16)
                sp.dma_start(ids[:, :, :], a["c_moe_ids"]).then_inc(loaded, 16)
                sp.dma_start(again[:, :], a["c_moe_again"].to_broadcast([P, MOE_E * TT])).then_inc(loaded, 16)
                sp.wait_ge(zero_rows, 2)
                half = len(jobs) // 2
                sp.wait_ge(tr_act, half)
                sp.dma_start(rows(xtok), rowsN[:, :, :]).then_inc(stored, 16)
                sp.wait_ge(tr_act, 2 * half)
                sp.dma_start(rows(a["out"]), rowsX[:, :, :]).then_inc(stored, 16)
                sp.wait_ge(stored, 32)

            @block.gpsimd
            def _(pool):
                pool.memset(rowsN[:, TT, :], 0.0).then_inc(zero_rows, 1)
                pool.memset(rowsX[:, TT, :], 0.0).then_inc(zero_rows, 1)

            @block.tensor
            def _(pe):
                pe.wait_ge(loaded, 80)
                for t in range(TT):
                    for c in range(DC):
                        mm = pe.matmul(lg[:, t * MOE_N:(t + 1) * MOE_N], k.XN[:, c, t * P:(t + 1) * P], wcls[:, c, :], start=(c == 0), stop=(c == DC - 1))
                mm.then_inc(logits_made, 1)
                for n, (src, _dst, j) in enumerate(jobs):
                    if n >= 4:
                        pe.wait_ge(tr_act, n - 3)
                    for i in range(2):
                        for c in range(DC):
                            t = 2 * j + i
                            mm = pe.transpose(tr[n % 4][:, i * D + c * P:i * D + (c + 1) * P], src[:, c, t * P:(t + 1) * P], k.ident[:, :])
                    mm.then_inc(turned, 1)
                pe.wait_ge(counted, 1)
                pe.matmul(place[:, :], tri[:, :], maskE[:, :, :].rearrange("p e t -> p (e t)"), start=True, stop=False)
                pe.matmul(place[:, :], ones[:, :], before[:, :, :].rearrange("p e t -> p (e t)"), start=False, stop=True).then_inc(placed, 1)

            @block.scalar
            def _(act):
                act.wait_ge(lowered, 1)
                act.activation(e1[:, :, :], e1[:, :, :], ACT.Exp).then_inc(exped, 1)
                for n, (_src, dst, j) in enumerate(jobs):
                    act.wait_ge(turned, n + 1)
                    act.activation(dst[:, 2 * j:2 * j + 2, :], tr[n % 4][:, :].rearrange("p (i n) -> p i n", i=2), ACT.Copy).then_inc(tr_act, 1)

            @block.vector
            def _(dve):
                def per_tile(i):
                    return small[:, i, :].unsqueeze(2).to_broadcast([P, TT, MOE_N])

                logits = lg[:, :].rearrange("p (t n) -> p t n", t=TT)
                dve.memset(ones[:, :], 1.0)
                dve.wait_ge(loaded, 80)
                dve.tensor_copy(info[:, :, :, 0:3], ids[:, :, :].unsqueeze(1).to_broadcast([P, MOE_E, TT, 3]))
                dve.memset(info[:, :, :, 6:7], 1.0)
                dve.wait_ge(logits_made, 1)
                dve.tensor_reduce(small[:, 0, :], logits, AX_X, ALU.max).then_inc(done, 1)
                dve.wait_ge(done, 1)
                dve.tensor_tensor(e1[:, :, :], logits, per_tile(0), ALU.subtract).then_inc(lowered, 1)
                dve.wait_ge(exped, 1)
                dve.tensor_reduce(small[:, 1, :], e1[:, :, :], AX_X, ALU.add).then_inc(done, 1)
                dve.wait_ge(done, 2)
                dve.reciprocal(small[:, 2, :], small[:, 1, :]).then_inc(done, 1)
                dve.wait_ge(done, 3)
                dve.tensor_tensor(s1[:, :, :], e1[:, :, :], per_tile(2), ALU.mult).then_inc(done, 1)
                dve.wait_ge(done, 4)
                dve.tensor_tensor(biased[:, :, :], s1[:, :, :], bias[:, :].unsqueeze(1).to_broadcast([P, TT, MOE_N]), ALU.add).then_inc(done, 1)
                dve.wait_ge(done, 5)
                for t in range(TT):
                    op = dve.max(top8[:, t, :], biased[:, t, :])
                op.then_inc(done, 1)
                dve.wait_ge(done, 6)
                for t in range(TT):
                    op = dve.match_replace(left[:, t, :], top8[:, t, :], biased[:, t, :], -1e30)
                op.then_inc(done, 1)
                dve.wait_ge(done, 7)
                dve.tensor_tensor(chosen[:, :, :], left[:, :, :], biased[:, :, :], ALU.not_equal).then_inc(done, 1)
                dve.wait_ge(done, 8)
                dve.tensor_copy(maskE[:, :, :], chosen[:, :, 0:MOE_E].rearrange("p t e -> p e t")).then_inc(done, 1)
                dve.wait_ge(done, 9)
                dve.tensor_tensor_scan(before[:, :, :].rearrange("p e t -> p (e t)"), again[:, :], maskE[:, :, :].rearrange("p e t -> p (e t)"), 0.0,
                                            ALU.mult, ALU.add).then_inc(done, 1)
                dve.wait_ge(done, 10)
                dve.tensor_tensor(before[:, :, :], before[:, :, :], maskE[:, :, :], ALU.subtract).then_inc(counted, 1)
                dve.tensor_tensor(w1[:, :, :], s1[:, :, :], chosen[:, :, :], ALU.mult).then_inc(done, 1)
                dve.wait_ge(done, 11)
                dve.tensor_reduce(small[:, 3, :], w1[:, :, :], AX_X, ALU.add).then_inc(done, 1)
                dve.wait_ge(done, 12)
                dve.tensor_scalar(small[:, 4, :], small[:, 3, :], MOE_TINY, None, ALU.add).then_inc(done, 1)
                dve.wait_ge(done, 13)
                dve.reciprocal(small[:, 5, :], small[:, 4, :]).then_inc(done, 1)
                dve.wait_ge(done, 14)
                dve.scalar_tensor_tensor(out=w1[:, :, :], in0=w1[:, :, :], scalar=MOE_SCALE, in1=per_tile(5), op0=ALU.mult, op1=ALU.mult).then_inc(done, 1)
                dve.wait_ge(done, 15)
                dve.tensor_reduce(small[:, 6, :], w1[:, :, MOE_E:], AX_X, ALU.add).then_inc(done, 1)
                dve.wait_ge(done, 16)
                dve.tensor_scalar(small[:, 7, :], small[:, 6, :], 1.0, None, ALU.add).then_inc(done, 1)
                dve.wait_ge(done, 17)
                dve.tensor_tensor(wE[:, :, :], w1[:, :, 0:MOE_E].rearrange("p t e -> p e t"), small[:, 7, :].unsqueeze(1).to_broadcast([P, MOE_E, TT]),
                                       ALU.mult).then_inc(done, 1)
                dve.wait_ge(done, 18)
                dve.tensor_copy(info[:, :, :, 3], wE[:, :, :]).then_inc(done, 1)
                dve.wait_ge(done, 19)
                dve.tensor_tensor(wa[:, :, :], wE[:, :, :], info[:, :, :, 3], ALU.subtract).then_inc(done, 1)
                dve.wait_ge(done, 20)
                dve.tensor_copy(info[:, :, :, 4], wa[:, :, :]).then_inc(done, 1)
                dve.wait_ge(done, 21)
                dve.tensor_tensor(wb[:, :, :], wa[:, :, :], info[:, :, :, 4], ALU.subtract).then_inc(done, 1)
                dve.wait_ge(done, 22)
                dve.tensor_copy(info[:, :, :, 5], wb[:, :, :]).then_inc(done, 1)
                dve.wait_ge(done, 23)
                dve.wait_ge(placed, 1)
                dve.scalar_tensor_tensor(out=key[:, :, :].rearrange("p e t -> p (e t)"), in0=maskE[:, :, :].rearrange("p e t -> p (e t)"), scalar=-MOE_OFF,
                                         in1=place[:, :], op0=ALU.mult, op1=ALU.add)


def moe_experts(nc, k, a, xtok, key, info):
    with Stage(nc, "mx") as st:
        slots = st.sb("slots", [P, P])
        spare = st.sb("spare", [P, 2])
        onehot = st.sb("onehot", [P, 2, TT, P], BF16)
        idw = st.sb("idw", [P, MOE_TURN, 2])
        spill = st.sb("spill", [P, 1])
        index = [st.sb(f"index{i}", [P, 1], U32) for i in range(MOE_TURN)]
        xg = [st.sb(f"xg{i}", [P, D]) for i in range(2)]
        xgT = st.sb("xgT", [P, DC * P])
        wgu = st.sb("wgu", [P, 2, DC, 2 * MOE_I])
        wdn = st.sb("wdn", [P, 2, D])
        sg, gated = st.sb("sg", [P, P]), st.sb("gated", [P, P])
        y = [st.sb(f"y{i}", [P, D]) for i in range(2)]
        ptab = [st.ps(f"ptab{i}") for i in range(2)]
        pxt, pgu, py = st.ps("pxt"), st.ps("pgu"), st.ps("py")
        consts, loaded = st.sem("consts"), [st.sem(f"loaded{i}") for i in range(2)]
        marked, tabled, spilled, summed, indexed = (st.sem(n) for n in ("marked", "tabled", "spilled", "summed", "indexed"))
        gathers, scatters = st.sem("gathers"), st.sem("scatters")
        gathered = [st.sem(f"gathered{i}") for i in range(2)]
        turned, x_kept, gu_made, sg_kept, gated_ready, down_made, scaled, scattered = (
            st.sem(n) for n in ("turned", "x_kept", "gu_made", "sg_kept", "gated_ready", "down_made", "scaled", "scattered"))
        TURNS = MOE_E // MOE_TURN

        def steps(engine, step):
            def turn(h, last=False):
                for i in range(MOE_TURN):
                    step(MOE_TURN * h + i, i, lambda n, i=i: not last or i + n < MOE_TURN)
            turn(0)
            with engine.Fori(1, TURNS - 1) as h:
                turn(h)
            turn(TURNS - 1, last=True)

        def uses(e, o):
            return 8 * (e - o) + 16

        with nc.Block() as block:

            @block.sync
            def _(sp):
                sp.dma_start(slots[:, :], a["c_moe_slots"].to_broadcast([P, P])).then_inc(consts, 16)
                sp.dma_start(spare[:, :], a["c_moe_spare"]).then_inc(consts, 16)

                def step(e, i, ahead):
                    o = i % 2
                    wait(sp, down_made, e - 1)
                    sp.dma_start(wgu[:, o, :, :], a["L3_ffn_w_gate_up"][ds(e, 1)].rearrange("a (c p) n -> p (a c) n", p=P)).then_inc(loaded[o], 16)
                    sp.dma_start(wdn[:, o, :], a["L3_ffn_w_down"][ds(e, 1)].rearrange("a p n -> (a p) n")).then_inc(loaded[o], 16)

                steps(sp, step)

            @block.gpsimd
            def _(pool):
                def gather(e, i):
                    pool.wait_ge(indexed, e + 1)
                    wait(pool, turned, e - 1)
                    pool.sem_inc(gathers, 1)
                    pool.indirect_dma_start(xg[i % 2][:, :], None, xtok, bass.IndirectOffsetOnAxis(ap=index[i][:, 0:1], axis=0)).then_inc(gathered[i % 2], 16)

                gather(0, 0)

                def step(e, i, ahead):
                    if ahead(1):
                        gather(e + 1, (i + 1) % MOE_TURN)
                    wait(pool, scattered, 16 * e)
                    pool.wait_ge(scaled, e + 1)
                    pool.sem_inc(scatters, 1)
                    pool.indirect_dma_start(a["out"], bass.IndirectOffsetOnAxis(ap=index[i][:, 0:1], axis=0), y[i % 2][:, :], None,
                                            compute_op=ALU.add).then_inc(scattered, 16)

                steps(pool, step)
                pool.wait_ge(scattered, 16 * MOE_E)

            @block.tensor
            def _(pe):
                def table(e, i):
                    pe.wait_ge(marked, e + 1)
                    wait(pe, indexed, e - 1)
                    for t in range(TT):
                        mm = pe.matmul(ptab[i % 2][:, 0:MOE_INFO], onehot[:, i % 2, t, :], info[:, ds(e, 1), t, :].rearrange("p a n -> p (a n)"),
                                       start=(t == 0), stop=(t == TT - 1))
                    mm.then_inc(tabled, 1)

                table(0, 0)
                table(1, 1)

                def step(e, i, ahead):
                    o = i % 2
                    pe.wait_ge(gathered[o], uses(e, o))
                    wait(pe, x_kept, e)
                    for c in range(DC):
                        mm = pe.transpose(pxt[:, c * P:(c + 1) * P], xg[o][:, c * P:(c + 1) * P], k.ident[:, :])
                    mm.then_inc(turned, 1)
                    pe.wait_ge(loaded[o], 2 * uses(e, o))
                    pe.wait_ge(x_kept, e + 1)
                    wait(pe, gated_ready, e)
                    for f in range(2):
                        for c in range(DC):
                            mm = pe.matmul(pgu[:, f * P:(f + 1) * P], wgu[:, o, c, f * P:(f + 1) * P], xgT[:, c * P:(c + 1) * P],
                                           start=(c == 0), stop=(c == DC - 1))
                    mm.then_inc(gu_made, 1)
                    if ahead(2):
                        table(e + 2, (i + 2) % MOE_TURN)
                    pe.wait_ge(gated_ready, e + 1)
                    wait(pe, scaled, e)
                    pe.matmul(py[:, 0:D], gated[:, :], wdn[:, o, :], start=True, stop=True).then_inc(down_made, 1)

                steps(pe, step)

            @block.scalar
            def _(act):
                def step(e, i, ahead):
                    act.wait_ge(turned, e + 1)
                    wait(act, gu_made, e)
                    act.activation(xgT[:, :], pxt[:, 0:D], ACT.Copy).then_inc(x_kept, 1)
                    act.wait_ge(gu_made, e + 1)
                    wait(act, gated_ready, e)
                    act.activation(sg[:, :], pgu[:, 0:P], ACT.Silu).then_inc(sg_kept, 1)
                    act.wait_ge(down_made, e + 1)
                    wait(act, scattered, 16 * (e - 1))
                    act.activation(y[i % 2][:, :], py[:, 0:D], ACT.Copy, scale=idw[:, i, 1:2]).then_inc(scaled, 1)

                steps(act, step)

            @block.vector
            def _(dve):
                def mark(e, i):
                    wait(dve, tabled, e - 1)
                    dve.tensor_tensor(onehot[:, i % 2, :, :], slots[:, :].unsqueeze(1).to_broadcast([P, TT, P]),
                                      key[:, ds(e, 1), :].rearrange("p a t -> p (a t)").unsqueeze(2).to_broadcast([P, TT, P]),
                                      ALU.is_equal).then_inc(marked, 1)

                def make_index(e, i):
                    dve.wait_ge(tabled, e + 1)
                    wait(dve, scattered, 16 * (e - 3))
                    tab = ptab[i % 2]
                    dve.tensor_reduce(idw[:, i, :], tab[:, 0:6].rearrange("p (a b) -> p a b", a=2), AX_X, ALU.add).then_inc(summed, 1)
                    wait(dve, indexed, e)
                    dve.tensor_scalar(spill[:, :], tab[:, 6:7], spare[:, 0:1], spare[:, 1:2], ALU.mult, ALU.add).then_inc(spilled, 1)
                    dve.wait_ge(summed, e + 1)
                    dve.wait_ge(spilled, e + 1)
                    dve.tensor_tensor(index[i][:, :], spill[:, :], idw[:, i, 0:1], ALU.add).then_inc(indexed, 1)

                dve.wait_ge(consts, 32)
                mark(0, 0)
                mark(1, 1)
                make_index(0, 0)
                mark(2, 2)
                make_index(1, 1)

                def step(e, i, ahead):
                    dve.wait_ge(sg_kept, e + 1)
                    wait(dve, down_made, e)
                    dve.tensor_tensor(gated[:, :], sg[:, :], pgu[:, P:2 * P], ALU.mult).then_inc(gated_ready, 1)
                    if ahead(2):
                        make_index(e + 2, (i + 2) % MOE_TURN)
                    if ahead(3):
                        mark(e + 3, (i + 3) % MOE_TURN)

                steps(dve, step)


def moe_constants():
    f = np.float32
    p = np.arange(P)
    ids = np.stack([np.broadcast_to(np.arange(TT) * P, (P, TT)), np.broadcast_to(p[:, None], (P, TT)), np.zeros((P, TT))], axis=2)
    return {"c_before": (p[:, None] < p[None, :]).astype(f), "c_moe_ids": ids.astype(f),
            "c_moe_again": (np.arange(MOE_E * TT) % TT > 0).astype(f).reshape(1, -1), "c_moe_slots": (p - MOE_OFF).astype(f).reshape(1, -1),
            "c_moe_spare": np.stack([-(T + p), T + p], axis=1).astype(f)}


def moe_layout(x):
    return {"L3_ffn_w_clsT": x["L3_ffn_w_cls"].T, "L3_ffn_bias_row": x["L3_ffn_bias"].reshape(1, -1), "L3_ffn_w_gate_up": x["L3_ffn_w_gate_up"],
            "L3_ffn_w_down": x["L3_ffn_w_down"]}


def start(nc, k, a):
    with Stage(nc, "start") as st:
        loaded = st.sem("loaded")
        with nc.Block() as block:

            @block.sync
            def _(sp):
                sp.dma_start(k.XT[:, :, :], rows(a["xT"])).then_inc(loaded, 16)
                sp.dma_start(k.ident[:, :], a["c_ident"]).then_inc(loaded, 16)
                sp.dma_start(k.causal[:, :], a["c_causal"]).then_inc(loaded, 16)
                sp.wait_ge(loaded, 48)

            @block.vector
            def _(dve):
                dve.memset(k.avg[:, :], 1.0 / D)
                dve.memset(k.eps[:, :], EPS)


class Kept:
    pass


SPLIT_LAYERS = (0, 1)
LAYERS = [(l0_attn, l0_ffn), (l1_attn, l1_ffn), (l2_attn, l2_ffn), (l3_attn, l3_ffn)]


def program(nc, a):
    with ExitStack() as ctx:
        def keep(name, shape):
            return ctx.enter_context(nc.sbuf_tensor(name, shape, F32))

        k = Kept()
        k.XT = keep("XT", [P, DC, T])
        k.XN = keep("XN", [P, DC, T])
        k.ident = keep("ident", [P, P])
        k.avg = keep("avg", [P, P])
        k.causal = keep("causal", [P, P])
        k.eps = keep("eps", [P, 1])
        Stage.counts.clear()
        start(nc, k, a)
        for i, (attn, ffn) in enumerate(LAYERS):
            norm_stage(nc, k, f"n{i}", k.XT, k.XN)
            with Stage(nc, f"x{i}") as sx:
                if i in SPLIT_LAYERS:
                    k.XH, k.XL = sx.sb("XH", [P, DC, T], F32R), sx.sb("XL", [P, DC, T], F32R)
                    split_stage(nc, f"s{i}", k.XN, k.XH, k.XL)
                attn(nc, k, a)
                clear_semaphores(nc)
                ffn(nc, k, a)
                clear_semaphores(nc)


def constants():
    i = np.arange(P)
    had = np.array([[1.0]])
    while len(had) < P:
        had = np.block([[had, had], [had, -had]])
    return {
        "c_ident": np.eye(P),
        "c_causal": np.where(i[:, None] >= i[None, :], 0.0, -1e30),
        "c_had": had,
        **l1_constants(), **l2_constants(), **l3_constants(), **moe_constants(),
    }


def columns(v):
    return v.reshape(-1, P).T


def layout(x):
    out = {"xT": x["L0_attn_x"].reshape(T, D).T}
    for n in ("L0_attn_w_q", "L0_attn_w_kv", "L0_attn_w_dense"):
        out[n] = x[n]
    for n in ("L0_ffn_W_up", "L0_ffn_W_gate", "L0_ffn_W_down", "L1_ffn_weight", "L2_ffn_weight"):
        out[n + "T"] = x[n].T
    for n in ("L0_ffn_SU_ug", "L0_ffn_SU_dp", "L0_ffn_Wscale_ug", "L0_ffn_Wscale_dp", "L2_ffn_bias"):
        out[n + "_cols"] = columns(x[n])
    out["L1_ffn_cols"] = np.stack([columns(x[n]) for n in ("L1_ffn_gamma", "L1_ffn_beta", "L1_ffn_ln_weight", "L1_ffn_ln_bias", "L1_attn_bo")], axis=1)
    return {**out, **l1_layout(x), **l2_layout(x), **l3_layout(x), **moe_layout(x)}


def kernel(**inputs):
    import concourse.bacc as _bacc
    from concourse.bass_utils import run_bass_kernel_spmd as _run

    x = {n: np.asarray(v) for n, v in inputs.items()}
    arrays = {n: np.ascontiguousarray(v) for n, v in layout(x).items()}
    arrays.update({n: np.ascontiguousarray(v, dtype=np.float32) for n, v in constants().items()})

    nc = _bacc.Bacc("TRN2", target_bir_lowering=False, num_devices=1)
    a = {n: nc.dram_tensor(n, v.shape, mybir.dt.from_np(v.dtype), kind="ExternalInput").ap() for n, v in arrays.items()}
    out = nc.dram_tensor("out", (T + P, D), F32, kind="ExternalOutput").ap()
    program(nc, {**a, "out": out})
    r = _run(nc, [arrays], core_ids=[0])
    return r.results[0]["out"][:T].reshape(B, S, D)
```
